# Optimizing a Trainium2 kernel written in Bass

```python
import numpy as np
import jax
import jax.numpy as jnp

def _softmax(x, axis=-1):
    return jax.nn.softmax(x, axis=axis)

def _gelu(x):
    return jax.nn.gelu(x, approximate=True)

def _silu(x):
    return jax.nn.silu(x)

def _sigmoid(x):
    return jax.nn.sigmoid(x)

def _layernorm(x, axis=-1, eps=1e-05):
    m = jnp.mean(x, axis=axis, keepdims=True)
    v = jnp.var(x, axis=axis, keepdims=True)
    return (x - m) / jnp.sqrt(v + eps)

def _scatter_add(tgt, idx, src, axis=0):
    return tgt.at[idx].add(src)

def _segment_sum(src, seg, n):
    return jax.ops.segment_sum(src, seg, n)
kernel_name = 'mk_early_fusion_d2_tok_img768_r4_539076'

def setup_inputs(seed: int=0):
    np.random.seed(seed)
    _w = jnp.asarray

    def _rec_inputs():
        import jax
        import jax.numpy as jnp
        _rk = jax.random.key(seed)
        x = -0.000596345 + 1.00056 * jax.random.normal(jax.random.fold_in(_rk, 1), (8, 3, 64, 64), jnp.float32)
        txt = -0.000190561 + 0.886117 * jax.random.normal(jax.random.fold_in(_rk, 2), (8, 77, 192), jnp.float32)
        return (x, txt)
    x, txt = _rec_inputs()

    def _L0_tok_setup():
        import jax, jax.numpy as jnp
        import numpy as np
        B = 16
        IMG = 64
        CH = 3
        EMBED = 64
        GP = 16
        PRE = [1, 2, 4]
        N_LEVELS = 3
        FUSED = EMBED * N_LEVELS

        def hilbert_flat_indices(n):
            t = np.arange(n * n, dtype=np.int64)
            x = np.zeros(n * n, dtype=np.int64)
            y = np.zeros(n * n, dtype=np.int64)
            s = 1
            while s < n:
                rx = 1 & t // 2
                ry = 1 & (t ^ rx)
                swap = ry == 0
                flip = swap & (rx == 1)
                x = np.where(flip, s - 1 - x, x)
                y = np.where(flip, s - 1 - y, y)
                x2 = np.where(swap, y, x)
                y2 = np.where(swap, x, y)
                x, y = (x2, y2)
                x = x + s * rx
                y = y + s * ry
                t = t // 4
                s *= 2
            return y * n + x

        def _level(x, idx, W, b, p, gp):
            Bsz, C, H, _ = x.shape
            h = H // p
            t = x.reshape(Bsz, C, h, p, h, p).transpose(0, 2, 4, 3, 5, 1).reshape(Bsz, h * h, p * p * C)
            t = t[:, idx]
            t = t.reshape(Bsz, h * h // gp, gp * p * p * C)
            return t @ W.T + b

        def _interp_linear(x, n_out):
            L = x.shape[1]
            pos = (jnp.arange(n_out, dtype=jnp.float32) + 0.5) * (L / n_out) - 0.5
            pos = jnp.clip(pos, 0.0, L - 1)
            i0 = jnp.floor(pos).astype(jnp.int32)
            i1 = jnp.minimum(i0 + 1, L - 1)
            w = (pos - i0).astype(x.dtype)
            return x[:, i0] * (1.0 - w)[None, :, None] + x[:, i1] * w[None, :, None]
        key = jax.random.key(seed)
        ks = jax.random.split(key, 9)
        inp = {'x': jax.random.normal(ks[0], (B, CH, IMG, IMG), jnp.float32)}
        for i, p in enumerate(PRE):
            din = CH * p * p * GP
            inp[f'W{i}'] = jax.random.normal(ks[1 + 2 * i], (EMBED, din), jnp.float32) * din ** (-0.5)
            inp[f'b{i}'] = jax.random.normal(ks[2 + 2 * i], (EMBED,), jnp.float32) * 0.02
        inp['Wf'] = jax.random.normal(ks[7], (FUSED, FUSED), jnp.float32) * FUSED ** (-0.5)
        inp['bf'] = jax.random.normal(ks[8], (FUSED,), jnp.float32) * 0.02
        for i, p in enumerate(PRE):
            inp[f'idx{i}'] = jnp.asarray(hilbert_flat_indices(IMG // p), jnp.int32)
        return inp
    _L0_tok_all = _L0_tok_setup()
    _L0_tok_in = {k: v for k, v in _L0_tok_all.items() if k in ('W0', 'b0', 'W1', 'b1', 'W2', 'b2', 'Wf', 'bf', 'idx0', 'idx1', 'idx2')}
    del _L0_tok_all

    def _L0_attn_setup():
        import jax, jax.numpy as jnp
        import numpy as np

        def _rotate_half(x):
            a, b = jnp.split(x, 2, axis=-1)
            return jnp.concatenate([-b, a], axis=-1)

        def _rope_tables(L, d, dtype):
            inv = 1.0 / 10000.0 ** (jnp.arange(0, d, 2, dtype=jnp.float32) / d)
            ang = jnp.arange(L, dtype=jnp.float32)[:, None] * inv[None, :]
            cos = jnp.repeat(jnp.cos(ang), 2, axis=-1)[None, :, None, :].astype(dtype)
            sin = jnp.repeat(jnp.sin(ang), 2, axis=-1)[None, :, None, :].astype(dtype)
            return (cos, sin)

        def _forward(X, Wq, Wk, Wv, Wu, Wg, Wo, prior_mu, prior_log_tau):
            B, L, D = X.shape
            h = prior_mu.shape[2]
            d = D // h
            eps = 1e-12
            q = (X @ Wq.T).reshape(B, L, h, d)
            k = (X @ Wk.T).reshape(B, L, h, d)
            v = (X @ Wv.T).reshape(B, L, h, d)
            u = (X @ Wu.T).reshape(B, L, h, d)
            gate = (X @ Wg.T).reshape(B, L, h, 3)
            t = jnp.arange(1, L + 1, dtype=X.dtype).reshape(1, L, 1, 1)
            log_tau = jnp.exp(jnp.clip(prior_log_tau, -50.0, 30.0))
            u_sum = jnp.cumsum(u, axis=1)
            bar_u = (log_tau * prior_mu + u_sum) / (log_tau + t)
            s_i = -jnp.sum(u * bar_u, axis=-1, keepdims=True) / np.float32(np.sqrt(d))
            cos, sin = _rope_tables(L, d, X.dtype)
            q = q * cos + _rotate_half(q) * sin
            k = k * cos + _rotate_half(k) * sin
            q = q / jnp.maximum(jnp.linalg.norm(q, axis=-1, keepdims=True), eps)
            k = k / jnp.maximum(jnp.linalg.norm(k, axis=-1, keepdims=True), eps)
            s_max = jax.lax.stop_gradient(jnp.max(s_i, axis=1, keepdims=True))
            exp_s = jnp.exp(s_i - s_max)
            E_t = jnp.cumsum(exp_s, axis=1)
            P_t = jnp.cumsum(s_i, axis=1)
            kv = jnp.einsum('blhd,blhe->blhde', k, v)
            F_t = jnp.cumsum(exp_s[..., None] * kv, axis=1)
            G_t = jnp.cumsum(s_i[..., None] * kv, axis=1)
            H_t = jnp.cumsum(kv, axis=1)
            sig1 = jax.nn.sigmoid(gate[..., 0:1])
            sigh = jax.nn.sigmoid(gate[..., 1:2])
            alpha = sigh / (E_t + eps)
            beta = (sig1 - sigh) / t
            gamma = -((beta * P_t + sigh) / t)
            M = alpha[..., None] * F_t + beta[..., None] * G_t + gamma[..., None] * H_t
            out = jnp.einsum('blhd,blhde->blhe', q, M)
            mu = jnp.mean(out, axis=-1, keepdims=True)
            var = jnp.mean(jnp.square(out - mu), axis=-1, keepdims=True)
            out = (out - mu) / jnp.sqrt(var + 1e-05)
            return out.reshape(B, L, D) @ Wo.T
        key = jax.random.key(seed)
        ks = jax.random.split(key, 7)
        B, L, D, h = (1, 256, 192, 12)
        d = D // h
        s = 0.02
        return {'X': jax.random.normal(ks[0], (B, L, D), jnp.float32), 'Wq': jax.random.normal(ks[1], (D, D), jnp.float32) * s, 'Wk': jax.random.normal(ks[2], (D, D), jnp.float32) * s, 'Wv': jax.random.normal(ks[3], (D, D), jnp.float32) * s, 'Wu': jax.random.normal(ks[4], (D, D), jnp.float32) * s, 'Wg': jax.random.normal(ks[5], (3 * h, D), jnp.float32) * s, 'Wo': jax.random.normal(ks[6], (D, D), jnp.float32) * s, 'prior_mu': jnp.zeros((1, 1, h, d), jnp.float32), 'prior_log_tau': jnp.zeros((1, 1, h, 1), jnp.float32)}
    _L0_attn_all = _L0_attn_setup()
    _L0_attn_in = {k: v for k, v in _L0_attn_all.items() if k in ('Wq', 'Wk', 'Wv', 'Wu', 'Wg', 'Wo', 'prior_mu', 'prior_log_tau')}
    del _L0_attn_all

    def _L0_ffn_setup():
        import jax, jax.numpy as jnp
        import numpy as np
        D_MODEL = 192
        N_EXPERTS = 16
        TOP_K = 2
        D_FF = 4 * D_MODEL
        B, L = (4, 512)
        key = jax.random.key(seed)
        ks = jax.random.split(key, 6)
        s_in = 1.0 / np.sqrt(D_MODEL)
        s_ff = 1.0 / np.sqrt(D_FF)
        x = jax.random.normal(ks[0], (B, L, D_MODEL), dtype=jnp.float32)
        Wr = jax.random.uniform(ks[1], (N_EXPERTS, D_MODEL), jnp.float32, -s_in, s_in)
        W1 = jax.random.uniform(ks[2], (N_EXPERTS, D_MODEL, D_FF), jnp.float32, -s_in, s_in)
        b1 = jax.random.uniform(ks[3], (N_EXPERTS, D_FF), jnp.float32, -s_in, s_in)
        W2 = jax.random.uniform(ks[4], (N_EXPERTS, D_FF, D_MODEL), jnp.float32, -s_ff, s_ff)
        b2 = jax.random.uniform(ks[5], (N_EXPERTS, D_MODEL), jnp.float32, -s_ff, s_ff)
        return {'x': x, 'Wr': Wr, 'W1': W1, 'b1': b1, 'W2': W2, 'b2': b2}
    _L0_ffn_all = _L0_ffn_setup()
    _L0_ffn_in = {k: v for k, v in _L0_ffn_all.items() if k in ('Wr', 'W1', 'b1', 'W2', 'b2')}
    del _L0_ffn_all

    def _L1_attn_setup():
        import jax, jax.numpy as jnp
        import numpy as np
        B, L, D, H = (2, 256, 192, 12)
        DH = D // H

        def _reference_tuple_inner(x, W_qkv, b_qkv, W_gate, b_gate, W_proj, b_proj, ln_g, ln_b):
            Bx, Lx, Dx = x.shape
            dh = Dx // H
            mu = jnp.mean(x, axis=-1, keepdims=True)
            var = jnp.var(x, axis=-1, keepdims=True)
            xn = (x - mu) / jnp.sqrt(var + 1e-05) * ln_g + ln_b
            qkv = xn @ W_qkv + b_qkv
            q, k, v = jnp.split(qkv, 3, axis=-1)
            gate = jax.nn.sigmoid(x @ W_gate + b_gate)
            k = k * gate

            def heads(t):
                return t.reshape(Bx, Lx, H, dh).transpose(0, 2, 1, 3)
            q_f = jax.nn.elu(heads(q).astype(jnp.float32)) + 1.0
            k_f = jax.nn.elu(heads(k).astype(jnp.float32)) + 1.0
            v_f = heads(v).astype(jnp.float32)
            kv_cum = jnp.cumsum(k_f[..., :, None] * v_f[..., None, :], axis=2)
            out_num = jnp.einsum('bhld,bhlde->bhle', q_f, kv_cum)
            k_cum = jnp.cumsum(k_f, axis=2)
            out_den = jnp.sum(q_f * k_cum, axis=-1, keepdims=True) + 1e-06
            attn = (out_num / out_den).astype(x.dtype)
            attn = attn.transpose(0, 2, 1, 3).reshape(Bx, Lx, Dx)
            return (attn @ W_proj + b_proj, gate)
        key = jax.random.key(seed)
        ks = jax.random.split(key, 4)
        s = 0.02
        return {'x': jax.random.normal(ks[0], (B, L, D), jnp.float32), 'W_qkv': jax.random.normal(ks[1], (D, 3 * D), jnp.float32) * s, 'b_qkv': jnp.zeros((3 * D,), jnp.float32), 'W_gate': jax.random.normal(ks[2], (D, D), jnp.float32) * s, 'b_gate': jnp.zeros((D,), jnp.float32), 'W_proj': jax.random.normal(ks[3], (D, D), jnp.float32) * s, 'b_proj': jnp.zeros((D,), jnp.float32), 'ln_g': jnp.ones((D,), jnp.float32), 'ln_b': jnp.zeros((D,), jnp.float32)}
    _L1_attn_all = _L1_attn_setup()
    _L1_attn_in = {k: v for k, v in _L1_attn_all.items() if k in ('W_qkv', 'b_qkv', 'W_gate', 'b_gate', 'W_proj', 'b_proj', 'ln_g', 'ln_b')}
    del _L1_attn_all

    def _L1_ffn_setup():
        import jax, jax.numpy as jnp
        import numpy as np
        EPS_NORM = 1e-06
        EPS_Q = 1e-05

        def rmsnorm(x, g):
            return x * jax.lax.rsqrt(jnp.mean(x * x, axis=-1, keepdims=True) + EPS_NORM) * g

        def activation_quant(x):
            scale = 127.0 / jnp.maximum(jnp.max(jnp.abs(x), axis=-1, keepdims=True), EPS_Q)
            return jnp.clip(jnp.round(x * scale), -128, 127) / scale

        def weight_quant(w):
            scale = 1.0 / jnp.maximum(jnp.mean(jnp.abs(w)), EPS_Q)
            return jnp.clip(jnp.round(w * scale), -1, 1) / scale

        def bitlinear(x, w, g):
            x_norm = rmsnorm(x, g)
            x_q = x_norm + jax.lax.stop_gradient(activation_quant(x_norm) - x_norm)
            w_q = w + jax.lax.stop_gradient(weight_quant(w) - w)
            return jnp.einsum('bsd,od->bso', x_q, w_q)
        key = jax.random.key(seed)
        k1, k2, k3 = jax.random.split(key, 3)
        B, S, D, H = (8, 1024, 192, 512)
        x = jax.random.normal(k1, (B, S, D), dtype=jnp.float32)
        w_in = jax.random.normal(k2, (2 * H, D), dtype=jnp.float32) * 0.002
        w_out = jax.random.normal(k3, (D, H), dtype=jnp.float32) * 0.002
        g_in = jnp.ones((D,), dtype=jnp.float32)
        g_out = jnp.ones((H,), dtype=jnp.float32)
        return {'x': x, 'w_in': w_in, 'g_in': g_in, 'w_out': w_out, 'g_out': g_out}
    _L1_ffn_all = _L1_ffn_setup()
    _L1_ffn_in = {k: v for k, v in _L1_ffn_all.items() if k in ('w_in', 'g_in', 'w_out', 'g_out')}
    del _L1_ffn_all
    return {'x': x, 'txt': txt, 'L0_tok_W0': _L0_tok_in['W0'], 'L0_tok_b0': _L0_tok_in['b0'], 'L0_tok_W1': _L0_tok_in['W1'], 'L0_tok_b1': _L0_tok_in['b1'], 'L0_tok_W2': _L0_tok_in['W2'], 'L0_tok_b2': _L0_tok_in['b2'], 'L0_tok_Wf': _L0_tok_in['Wf'], 'L0_tok_bf': _L0_tok_in['bf'], 'L0_tok_idx0': _L0_tok_in['idx0'], 'L0_tok_idx1': _L0_tok_in['idx1'], 'L0_tok_idx2': _L0_tok_in['idx2'], 'L0_attn_Wq': _L0_attn_in['Wq'], 'L0_attn_Wk': _L0_attn_in['Wk'], 'L0_attn_Wv': _L0_attn_in['Wv'], 'L0_attn_Wu': _L0_attn_in['Wu'], 'L0_attn_Wg': _L0_attn_in['Wg'], 'L0_attn_Wo': _L0_attn_in['Wo'], 'L0_attn_prior_mu': _L0_attn_in['prior_mu'], 'L0_attn_prior_log_tau': _L0_attn_in['prior_log_tau'], 'L0_ffn_Wr': _L0_ffn_in['Wr'], 'L0_ffn_W1': _L0_ffn_in['W1'], 'L0_ffn_b1': _L0_ffn_in['b1'], 'L0_ffn_W2': _L0_ffn_in['W2'], 'L0_ffn_b2': _L0_ffn_in['b2'], 'L1_attn_W_qkv': _L1_attn_in['W_qkv'], 'L1_attn_b_qkv': _L1_attn_in['b_qkv'], 'L1_attn_W_gate': _L1_attn_in['W_gate'], 'L1_attn_b_gate': _L1_attn_in['b_gate'], 'L1_attn_W_proj': _L1_attn_in['W_proj'], 'L1_attn_b_proj': _L1_attn_in['b_proj'], 'L1_attn_ln_g': _L1_attn_in['ln_g'], 'L1_attn_ln_b': _L1_attn_in['ln_b'], 'L1_ffn_w_in': _L1_ffn_in['w_in'], 'L1_ffn_g_in': _L1_ffn_in['g_in'], 'L1_ffn_w_out': _L1_ffn_in['w_out'], 'L1_ffn_g_out': _L1_ffn_in['g_out']}

def reference(x, txt, L0_tok_W0, L0_tok_b0, L0_tok_W1, L0_tok_b1, L0_tok_W2, L0_tok_b2, L0_tok_Wf, L0_tok_bf, L0_tok_idx0, L0_tok_idx1, L0_tok_idx2, L0_attn_Wq, L0_attn_Wk, L0_attn_Wv, L0_attn_Wu, L0_attn_Wg, L0_attn_Wo, L0_attn_prior_mu, L0_attn_prior_log_tau, L0_ffn_Wr, L0_ffn_W1, L0_ffn_b1, L0_ffn_W2, L0_ffn_b2, L1_attn_W_qkv, L1_attn_b_qkv, L1_attn_W_gate, L1_attn_b_gate, L1_attn_W_proj, L1_attn_b_proj, L1_attn_ln_g, L1_attn_ln_b, L1_ffn_w_in, L1_ffn_g_in, L1_ffn_w_out, L1_ffn_g_out):
    import jax
    import jax.numpy as jnp

    def _L0_tok_ref(x, W0, b0, W1, b1, W2, b2, Wf, bf, idx0, idx1, idx2):
        import jax, jax.numpy as jnp
        import numpy as np
        B = 16
        IMG = 64
        CH = 3
        EMBED = 64
        GP = 16
        PRE = [1, 2, 4]
        N_LEVELS = 3
        FUSED = EMBED * N_LEVELS

        def hilbert_flat_indices(n):
            t = np.arange(n * n, dtype=np.int64)
            x = np.zeros(n * n, dtype=np.int64)
            y = np.zeros(n * n, dtype=np.int64)
            s = 1
            while s < n:
                rx = 1 & t // 2
                ry = 1 & (t ^ rx)
                swap = ry == 0
                flip = swap & (rx == 1)
                x = np.where(flip, s - 1 - x, x)
                y = np.where(flip, s - 1 - y, y)
                x2 = np.where(swap, y, x)
                y2 = np.where(swap, x, y)
                x, y = (x2, y2)
                x = x + s * rx
                y = y + s * ry
                t = t // 4
                s *= 2
            return y * n + x

        def _level(x, idx, W, b, p, gp):
            Bsz, C, H, _ = x.shape
            h = H // p
            t = x.reshape(Bsz, C, h, p, h, p).transpose(0, 2, 4, 3, 5, 1).reshape(Bsz, h * h, p * p * C)
            t = t[:, idx]
            t = t.reshape(Bsz, h * h // gp, gp * p * p * C)
            return t @ W.T + b

        def _interp_linear(x, n_out):
            L = x.shape[1]
            pos = (jnp.arange(n_out, dtype=jnp.float32) + 0.5) * (L / n_out) - 0.5
            pos = jnp.clip(pos, 0.0, L - 1)
            i0 = jnp.floor(pos).astype(jnp.int32)
            i1 = jnp.minimum(i0 + 1, L - 1)
            w = (pos - i0).astype(x.dtype)
            return x[:, i0] * (1.0 - w)[None, :, None] + x[:, i1] * w[None, :, None]
        Ws = [(idx0, W0, b0, PRE[0]), (idx1, W1, b1, PRE[1]), (idx2, W2, b2, PRE[2])]
        outs = [_level(x, idx, W, b, p, GP) for idx, W, b, p in Ws]
        n_tokens = outs[0].shape[1]
        outs = [outs[0]] + [_interp_linear(o, n_tokens) for o in outs[1:]]
        y = jnp.concatenate(outs, axis=-1)
        return y @ Wf.T + bf

    def _L0_attn_ref(X, Wq, Wk, Wv, Wu, Wg, Wo, prior_mu, prior_log_tau):
        import jax, jax.numpy as jnp
        import numpy as np

        def _rotate_half(x):
            a, b = jnp.split(x, 2, axis=-1)
            return jnp.concatenate([-b, a], axis=-1)

        def _rope_tables(L, d, dtype):
            inv = 1.0 / 10000.0 ** (jnp.arange(0, d, 2, dtype=jnp.float32) / d)
            ang = jnp.arange(L, dtype=jnp.float32)[:, None] * inv[None, :]
            cos = jnp.repeat(jnp.cos(ang), 2, axis=-1)[None, :, None, :].astype(dtype)
            sin = jnp.repeat(jnp.sin(ang), 2, axis=-1)[None, :, None, :].astype(dtype)
            return (cos, sin)

        def _forward(X, Wq, Wk, Wv, Wu, Wg, Wo, prior_mu, prior_log_tau):
            B, L, D = X.shape
            h = prior_mu.shape[2]
            d = D // h
            eps = 1e-12
            q = (X @ Wq.T).reshape(B, L, h, d)
            k = (X @ Wk.T).reshape(B, L, h, d)
            v = (X @ Wv.T).reshape(B, L, h, d)
            u = (X @ Wu.T).reshape(B, L, h, d)
            gate = (X @ Wg.T).reshape(B, L, h, 3)
            t = jnp.arange(1, L + 1, dtype=X.dtype).reshape(1, L, 1, 1)
            log_tau = jnp.exp(jnp.clip(prior_log_tau, -50.0, 30.0))
            u_sum = jnp.cumsum(u, axis=1)
            bar_u = (log_tau * prior_mu + u_sum) / (log_tau + t)
            s_i = -jnp.sum(u * bar_u, axis=-1, keepdims=True) / np.float32(np.sqrt(d))
            cos, sin = _rope_tables(L, d, X.dtype)
            q = q * cos + _rotate_half(q) * sin
            k = k * cos + _rotate_half(k) * sin
            q = q / jnp.maximum(jnp.linalg.norm(q, axis=-1, keepdims=True), eps)
            k = k / jnp.maximum(jnp.linalg.norm(k, axis=-1, keepdims=True), eps)
            s_max = jax.lax.stop_gradient(jnp.max(s_i, axis=1, keepdims=True))
            exp_s = jnp.exp(s_i - s_max)
            E_t = jnp.cumsum(exp_s, axis=1)
            P_t = jnp.cumsum(s_i, axis=1)
            kv = jnp.einsum('blhd,blhe->blhde', k, v)
            F_t = jnp.cumsum(exp_s[..., None] * kv, axis=1)
            G_t = jnp.cumsum(s_i[..., None] * kv, axis=1)
            H_t = jnp.cumsum(kv, axis=1)
            sig1 = jax.nn.sigmoid(gate[..., 0:1])
            sigh = jax.nn.sigmoid(gate[..., 1:2])
            alpha = sigh / (E_t + eps)
            beta = (sig1 - sigh) / t
            gamma = -((beta * P_t + sigh) / t)
            M = alpha[..., None] * F_t + beta[..., None] * G_t + gamma[..., None] * H_t
            out = jnp.einsum('blhd,blhde->blhe', q, M)
            mu = jnp.mean(out, axis=-1, keepdims=True)
            var = jnp.mean(jnp.square(out - mu), axis=-1, keepdims=True)
            out = (out - mu) / jnp.sqrt(var + 1e-05)
            return out.reshape(B, L, D) @ Wo.T
        return _forward(X, Wq, Wk, Wv, Wu, Wg, Wo, prior_mu, prior_log_tau)

    def _L0_ffn_ref(x, Wr, W1, b1, W2, b2):
        import jax, jax.numpy as jnp
        import numpy as np
        D_MODEL = 192
        N_EXPERTS = 16
        TOP_K = 2
        D_FF = 4 * D_MODEL
        B, L = (4, 512)
        logits = jnp.einsum('bld,ed->ble', x, Wr)
        probs = jax.nn.softmax(logits, axis=-1)
        top_p, top_idx = jax.lax.top_k(probs, TOP_K)
        gating = jnp.sum(jax.nn.one_hot(top_idx, N_EXPERTS, dtype=probs.dtype) * top_p[..., None], axis=-2)
        gate_e = jnp.moveaxis(gating, -1, 0)

        def step(y, params):
            W1e, b1e, W2e, b2e, ge = params
            h = jax.nn.gelu(jnp.einsum('bld,df->blf', x, W1e) + b1e, approximate=False)
            out = jnp.einsum('blf,fd->bld', h, W2e) + b2e
            return (y + ge[..., None] * out, None)
        y0 = jnp.zeros_like(x)
        y, _ = jax.lax.scan(step, y0, (W1, b1, W2, b2, gate_e))
        return x + y

    def _L1_attn_ref(x, W_qkv, b_qkv, W_gate, b_gate, W_proj, b_proj, ln_g, ln_b):
        import jax, jax.numpy as jnp
        import numpy as np
        B, L, D, H = (2, 256, 192, 12)
        DH = D // H

        def _reference_tuple_inner(x, W_qkv, b_qkv, W_gate, b_gate, W_proj, b_proj, ln_g, ln_b):
            Bx, Lx, Dx = x.shape
            dh = Dx // H
            mu = jnp.mean(x, axis=-1, keepdims=True)
            var = jnp.var(x, axis=-1, keepdims=True)
            xn = (x - mu) / jnp.sqrt(var + 1e-05) * ln_g + ln_b
            qkv = xn @ W_qkv + b_qkv
            q, k, v = jnp.split(qkv, 3, axis=-1)
            gate = jax.nn.sigmoid(x @ W_gate + b_gate)
            k = k * gate

            def heads(t):
                return t.reshape(Bx, Lx, H, dh).transpose(0, 2, 1, 3)
            q_f = jax.nn.elu(heads(q).astype(jnp.float32)) + 1.0
            k_f = jax.nn.elu(heads(k).astype(jnp.float32)) + 1.0
            v_f = heads(v).astype(jnp.float32)
            kv_cum = jnp.cumsum(k_f[..., :, None] * v_f[..., None, :], axis=2)
            out_num = jnp.einsum('bhld,bhlde->bhle', q_f, kv_cum)
            k_cum = jnp.cumsum(k_f, axis=2)
            out_den = jnp.sum(q_f * k_cum, axis=-1, keepdims=True) + 1e-06
            attn = (out_num / out_den).astype(x.dtype)
            attn = attn.transpose(0, 2, 1, 3).reshape(Bx, Lx, Dx)
            return (attn @ W_proj + b_proj, gate)
        return _reference_tuple_inner(x, W_qkv, b_qkv, W_gate, b_gate, W_proj, b_proj, ln_g, ln_b)[0]

    def _L1_ffn_ref(x, w_in, g_in, w_out, g_out):
        import jax, jax.numpy as jnp
        import numpy as np
        EPS_NORM = 1e-06
        EPS_Q = 1e-05

        def rmsnorm(x, g):
            return x * jax.lax.rsqrt(jnp.mean(x * x, axis=-1, keepdims=True) + EPS_NORM) * g

        def activation_quant(x):
            scale = 127.0 / jnp.maximum(jnp.max(jnp.abs(x), axis=-1, keepdims=True), EPS_Q)
            return jnp.clip(jnp.round(x * scale), -128, 127) / scale

        def weight_quant(w):
            scale = 1.0 / jnp.maximum(jnp.mean(jnp.abs(w)), EPS_Q)
            return jnp.clip(jnp.round(w * scale), -1, 1) / scale

        def bitlinear(x, w, g):
            x_norm = rmsnorm(x, g)
            x_q = x_norm + jax.lax.stop_gradient(activation_quant(x_norm) - x_norm)
            w_q = w + jax.lax.stop_gradient(weight_quant(w) - w)
            return jnp.einsum('bsd,od->bso', x_q, w_q)
        h = bitlinear(x, w_in, g_in)
        up, gate = jnp.split(h, 2, axis=-1)
        y = jax.nn.silu(gate) * up
        return bitlinear(y, w_out, g_out)
    h = _L0_tok_ref(x, L0_tok_W0, L0_tok_b0, L0_tok_W1, L0_tok_b1, L0_tok_W2, L0_tok_b2, L0_tok_Wf, L0_tok_bf, L0_tok_idx0, L0_tok_idx1, L0_tok_idx2)
    h = jnp.concatenate([h, txt], axis=1)
    h = h + _L0_attn_ref(_layernorm(h, axis=-1), L0_attn_Wq, L0_attn_Wk, L0_attn_Wv, L0_attn_Wu, L0_attn_Wg, L0_attn_Wo, L0_attn_prior_mu, L0_attn_prior_log_tau)
    h = h + _L0_ffn_ref(_layernorm(h, axis=-1), L0_ffn_Wr, L0_ffn_W1, L0_ffn_b1, L0_ffn_W2, L0_ffn_b2)
    h = h + _L1_attn_ref(_layernorm(h, axis=-1), L1_attn_W_qkv, L1_attn_b_qkv, L1_attn_W_gate, L1_attn_b_gate, L1_attn_W_proj, L1_attn_b_proj, L1_attn_ln_g, L1_attn_ln_b)
    h = h + _L1_ffn_ref(_layernorm(h, axis=-1), L1_ffn_w_in, L1_ffn_g_in, L1_ffn_w_out, L1_ffn_g_out)
    return h

_drawn_inputs = setup_inputs


def setup_inputs(seed=0):
    import zlib

    import numpy as np

    out = dict(_drawn_inputs(seed))
    spreads = {'L0_attn_prior_mu': (0.0, 0.8),
     'L0_attn_prior_log_tau': (0.0, 0.8),
     'L1_attn_b_qkv': (0.0, 0.539),
     'L1_attn_b_gate': (0.0, 0.8),
     'L1_attn_b_proj': (0.0, 0.1),
     'L1_attn_ln_g': (1.0, 0.6),
     'L1_attn_ln_b': (0.0, 0.8),
     'L1_ffn_g_in': (1.0, 0.6),
     'L1_ffn_g_out': (1.0, 0.6)}
    factors = {'L0_tok_b0': 5.133,
     'L0_tok_b1': 5.177,
     'L0_tok_b2': 4.531,
     'L0_tok_bf': 2.67,
     'L0_attn_Wu': 3.097,
     'L0_attn_Wg': 8.0,
     'L0_ffn_Wr': 2.893,
     'L0_ffn_W1': 2.944,
     'L0_ffn_b1': 8.0,
     'L0_ffn_W2': 2.758,
     'L0_ffn_b2': 8.0,
     'L1_attn_W_qkv': 3.987,
     'L1_attn_W_gate': 8.0,
     'L1_attn_W_proj': 2.769,
     'L1_ffn_w_in': 8.0,
     'L1_ffn_w_out': 8.0}
    for name, (base, spread) in spreads.items():
        noise = np.random.default_rng([zlib.crc32(name.encode()), seed]).standard_normal(out[name].shape)
        drawn = base * np.exp(spread * noise) if base else spread * noise
        out[name] = jnp.asarray(drawn.astype(out[name].dtype))
    for name, factor in factors.items():
        out[name] = (out[name] * factor).astype(out[name].dtype)
    return out
```

```python
from contextlib import ExitStack

import numpy as np

import concourse.bass as bass
from concourse import mybir

F32 = mybir.dt.float32
BF16 = mybir.dt.bfloat16
I32 = mybir.dt.int32
ALU = mybir.AluOpType
ACT = mybir.ActivationFunctionType
AX = mybir.AxisListType.X

B, L, D = 8, 333, 192
P, NT = 111, 3
TILES = B * NT
NH, HD = 12, 16
KC = 96
IMG_TOK, TXT = 256, 77
EMB, GP = 64, 16
FEAT = (3, 12, 48)
TOK1, TOK2 = 64, 16
NE, FF = 16, 768
FC = FF // 128
BLK = 128
NB = (2 * B * L - NE) // BLK + NE
MAXB = -(-B * L // BLK)
UNROLL = 3
HID = 512
PAIRS = ((0, 2), (2, 1))
ARENA = 12800
MAGIC = 12582912.0


def shape_constants():
    f = np.float32
    c = {}
    c["ident"] = np.eye(128, dtype=f)
    c["ones"] = np.ones((128, 128), f)
    m = np.arange(P)
    c["tri"] = (m[:, None] <= m[None, :]).astype(f)
    c["tri_strict"] = (m[:, None] < m[None, :]).astype(f)
    pos = np.arange(L, dtype=f)
    inv = f(1.0) / f(10000.0) ** (np.arange(0, HD, 2, dtype=f) / f(HD))
    ang = (pos[:, None] * inv[None, :]).astype(f)
    cos = np.repeat(np.cos(ang), 2, axis=-1).astype(f)
    sin = np.repeat(np.sin(ang), 2, axis=-1).astype(f)
    sin[:, :HD // 2] *= -1
    c["cos"] = cos.reshape(NT, P, HD).transpose(1, 0, 2)
    c["sin"] = sin.reshape(NT, P, HD).transpose(1, 0, 2)
    c["time"] = (pos + 1).reshape(NT, P).T
    for lvl, n in ((1, TOK1), (2, TOK2)):
        at = (np.arange(IMG_TOK, dtype=f) + f(0.5)) * f(n / IMG_TOK) - f(0.5)
        at = np.clip(at, f(0), f(n - 1))
        i0 = np.floor(at).astype(np.int32)
        i1 = np.minimum(i0 + 1, n - 1)
        w = (at - i0).astype(f)
        a = np.zeros((n, IMG_TOK), f)
        np.add.at(a, (i0, np.arange(IMG_TOK)), f(1) - w)
        np.add.at(a, (i1, np.arange(IMG_TOK)), w)
        c[f"interp{lvl}"] = a
    for name, wid in (("head_mask0", 3 * HD), ("head_mask1", HD + 1)):
        c[name] = np.kron(np.eye(4, dtype=f), np.ones((32, wid), f))
    c["iota"] = np.broadcast_to(np.arange(128, dtype=f), (128, 128))
    c["steps"] = np.broadcast_to(BLK * np.arange(MAXB, dtype=f), (P, MAXB))
    c["reset"] = np.broadcast_to(np.tile(np.arange(TILES) > 0, NE), (P, NE * TILES))
    c["token"] = (np.arange(TILES)[None, :] * P + m[:, None])
    return {k: np.ascontiguousarray(v, dtype=f) for k, v in c.items()}


def laid_out(x, txt, w):
    a = {"txt": txt}
    for lvl, p in enumerate((1, 2, 4)):
        g = 64 // p
        t = x.reshape(B, 3, g, p, g, p).transpose(2, 4, 0, 3, 5, 1)
        a[f"patches{lvl}"] = t.reshape(g * g, B * p * p * 3)
        a[f"idx{lvl}"] = w[f"L0_tok_idx{lvl}"]
    a["idx0"] = a["idx0"].reshape(2, 128, GP).transpose(1, 0, 2)
    a["idx1"] = a["idx1"].reshape(TOK1, GP)
    a["idx2"] = a["idx2"].reshape(2, 128).T
    a["tok_w0"] = w["L0_tok_W0"].T
    a["tok_w1"] = w["L0_tok_W1"].T.reshape(2, KC, EMB).transpose(1, 0, 2)
    a["tok_w2"] = w["L0_tok_W2"].T.reshape(GP, 48, EMB).transpose(1, 0, 2)
    a["tok_b"] = np.stack([w[f"L0_tok_b{i}"] for i in range(3)], 1)
    a["tok_wf"] = w["L0_tok_Wf"].T.reshape(3, EMB, D).transpose(1, 0, 2)
    a["tok_bf"] = w["L0_tok_bf"][None, :]

    def chunks(m):
        return m.reshape(2, KC, -1).transpose(1, 0, 2)

    wg = w["L0_attn_Wg"].reshape(NH, 3, D).transpose(1, 0, 2)[:2].reshape(2 * NH, D)
    a["a0_w"] = chunks(np.concatenate(
        [w["L0_attn_Wq"], w["L0_attn_Wk"], w["L0_attn_Wv"], w["L0_attn_Wu"], wg]).T)
    a["a0_wo"] = chunks(w["L0_attn_Wo"].T)
    a["a0_mu"] = w["L0_attn_prior_mu"].reshape(1, D)
    a["a0_tau"] = w["L0_attn_prior_log_tau"].reshape(1, NH)
    a["wr"] = chunks(w["L0_ffn_Wr"].T)
    a["e_w1"] = w["L0_ffn_W1"].reshape(NE, 2, KC, FF).transpose(0, 2, 1, 3)
    a["e_b1"] = w["L0_ffn_b1"][:, None]
    a["e_w2"] = w["L0_ffn_W2"].reshape(NE, FC, 128, D).transpose(0, 2, 1, 3)
    a["e_b2"] = w["L0_ffn_b2"][:, None]

    def with_bias(m, b):
        return chunks(m), b[None, :]

    a["a1_w"], a["a1_b"] = with_bias(w["L1_attn_W_qkv"], w["L1_attn_b_qkv"])
    a["a1_wg"], a["a1_bg"] = with_bias(w["L1_attn_W_gate"], w["L1_attn_b_gate"])
    a["a1_wo"], a["a1_bo"] = with_bias(w["L1_attn_W_proj"], w["L1_attn_b_proj"])
    a["a1_ln"] = np.stack([w["L1_attn_ln_g"], w["L1_attn_ln_b"]], 1).reshape(2, KC, 2).transpose(1, 0, 2)
    a["f_win"] = chunks(w["L1_ffn_w_in"].T)
    a["f_gin"] = w["L1_ffn_g_in"][None, :]
    a["f_wout"] = w["L1_ffn_w_out"].T.reshape(4, 128, D).transpose(1, 0, 2)
    a["f_gout"] = w["L1_ffn_g_out"][None, :]
    return {k: np.ascontiguousarray(v) for k, v in a.items()}


class Chain:

    def __init__(self, eng, sem):
        self.eng, self.sem, self.base, self.per, self.k, self.at = eng, sem, 0, 0, 0, 0

    def turn(self, i):
        self.at = self.base + i * self.per
        self.k = 0

    def step(self, ins):
        ins.then_inc(self.sem, 1)
        self.k += 1
        return self.k

    def wait(self, k):
        self.eng.wait_ge(self.sem, self.at + k)

    def link(self, ins):
        self.wait(self.step(ins))

    def loop(self, n, body):
        self.base += self.k
        self.turn(0)
        body(0, True)
        self.per = self.k
        if n > 1:
            with self.eng.Fori(1, n) as i:
                self.turn(i)
                body(i, False)
        self.base += n * self.per
        self.turn(0)


def early_fusion(nc, dram, out):
    with ExitStack() as ctx:
        def sb(name, shape, dt=F32):
            return ctx.enter_context(nc.sbuf_tensor(name, shape, dt))

        def sem(name):
            return ctx.enter_context(nc.semaphore(name))

        bank = [ctx.enter_context(nc.psum_tensor(f"bank{i}", [128, 512], F32)) for i in range(8)]

        arena = sb("arena", [128, ARENA])

        class Taker:
            def __init__(self, at=0):
                self.at = at

            def __call__(self, shape):
                n = int(np.prod(shape[1:]))
                flat = arena[0:shape[0], self.at:self.at + n]
                self.at += n
                assert self.at <= ARENA, self.at
                names = "abcd"[:len(shape) - 1]
                return flat.rearrange(f"p ({' '.join(names)}) -> p {' '.join(names)}",
                                      **{k: v for k, v in zip(names, shape[1:])})

        tok_buf, attn_buf, moe_buf, ffn_buf = Taker(), Taker(), Taker(), Taker()

        h = sb("h", [P, TILES * D])

        def tile_of(buf, n, count=1):
            return buf[:, bass.ds(n * D, count * D)]

        const, plan = {}, {"tok": [], "a0": [], "route": [], "a1": [], "f": []}

        def load(stage, name, shape, src=None, dt=F32):
            t = sb(f"s_{name}", shape, dt)
            full = t[tuple(slice(None) for _ in shape)]
            plan[stage].append((full, dram[name] if src is None else src))
            return t

        ident = load("tok", "c_ident", [128, 128])
        ones = load("tok", "c_ones", [128, 128])
        idx0 = load("tok", "idx0", [128, 2, GP], dt=I32)
        idx1 = load("tok", "idx1", [TOK1, GP], dt=I32)
        idx2 = load("tok", "idx2", [128, 2], dt=I32)
        w0 = load("tok", "tok_w0", [48, EMB])
        w1 = load("tok", "tok_w1", [KC, 2, EMB])
        w2 = load("tok", "tok_w2", [48, GP, EMB])
        tok_b = load("tok", "tok_b", [EMB, 3])
        wf = load("tok", "tok_wf", [EMB, 3, D])
        bf = load("tok", "tok_bf", [1, D])
        interp1 = load("tok", "c_interp1", [TOK1, IMG_TOK])
        interp2 = load("tok", "c_interp2", [TOK2, IMG_TOK])
        tri = load("a0", "c_tri", [P, P])
        cos = load("a0", "c_cos", [P, NT, HD])
        sin = load("a0", "c_sin", [P, NT, HD])
        time = load("a0", "c_time", [P, NT])
        head_mask0 = load("a0", "c_head_mask0", [128, 12 * HD])
        a0_w = load("a0", "a0_w", [KC, 2, 4 * D + 2 * NH])
        a0_wo = load("a0", "a0_wo", [KC, 2, D])
        mu = load("a0", "a0_mu", [P, D], dram["a0_mu"].to_broadcast([P, D]))
        tau = load("a0", "a0_tau", [P, NH], dram["a0_tau"].to_broadcast([P, NH]))

        wr = load("route", "wr", [KC, 2, NE])
        tri_strict = load("route", "c_tri_strict", [P, P])
        iota = load("route", "c_iota", [P, 128], dram["c_iota"][0:P, :])
        steps = load("route", "c_steps", [P, MAXB])
        reset = load("route", "c_reset", [P, NE * TILES])
        token = load("route", "c_token", [P, TILES])

        def load_biased(stage, name, n, bias):
            t = sb(f"s_{name}", [KC + 1, 2, n])
            plan[stage].append((t[0:KC, :, :], dram[name]))
            plan[stage].append((t[KC:KC + 1, 1, :], dram[bias]))
            return t

        a1_w = load_biased("a1", "a1_w", 3 * D, "a1_b")
        a1_wg = load_biased("a1", "a1_wg", D, "a1_bg")
        a1_wo = load_biased("a1", "a1_wo", D, "a1_bo")
        a1_ln = load("a1", "a1_ln", [KC, 2, 2])
        head_mask1 = load("a1", "c_head_mask1", [128, 4 * (HD + 1)])
        w_in = load("f", "f_win", [KC, 2, 2 * HID])
        w_out = load("f", "f_wout", [128, 4, D])
        g_in = load("f", "f_gin", [P, D], dram["f_gin"].to_broadcast([P, D]))
        g_out = load("f", "f_gout", [P, HID], dram["f_gout"].to_broadcast([P, HID]))

        xn_dram = nc.dram_tensor("xn_dram", (B * L, D), F32, kind="Internal").ap()
        y_dram = nc.dram_tensor("y_dram", (NB * BLK, D), F32, kind="Internal").ap()

        loaded = {k: sem(f"loaded_{k}") for k in plan}
        txt_loaded = sem("txt_loaded")
        idx_loaded = sem("idx_loaded")
        eps_set = sem("eps_set")
        turns_passed = sem("turns_passed")

        g0 = tok_buf([128, 2, GP, 3 * B])
        g1 = tok_buf([TOK1, GP, 12 * B])
        g2 = tok_buf([128, 2, 48 * B])
        x0 = tok_buf([128, 2, 48])
        x1 = tok_buf([TOK1, 2 * KC])
        x2 = tok_buf([128, 2, 48])
        x02T = tok_buf([48, 512])
        x1T = tok_buf([KC, 2, TOK1])
        y1 = tok_buf([TOK1, EMB])
        y2 = tok_buf([TOK2, EMB])
        catT = tok_buf([EMB, 3, IMG_TOK])
        gathered = sem("gathered")
        tok_staged, tok_xT_ps, tok_xT, tok_y_ps = (sem(n) for n in ("tok_staged", "tok_xT_ps", "tok_xT", "tok_y_ps"))
        tok_y, tok_i_ps, tok_cat, tok_h_ps, h_tok = (sem(n) for n in ("tok_y", "tok_i_ps", "tok_cat", "tok_h_ps", "h_tok"))

        rot1 = attn_buf([P, NT, 2 * D])
        qkT = attn_buf([128, NT, 6, P])
        att = attn_buf([P, NH, P])
        a0_buf, a1_buf = Taker(attn_buf.at), Taker(attn_buf.at)
        eps5 = sb("eps5", [128, 1])
        stats = sb("stats", [P, NT, 6])
        mv = sb("mv", [P, NT, 2])
        sd = sb("sd", [P, NT])
        rs = sb("rs", [P, NT])
        xn = sb("xn", [P, NT, D])
        xT = sb("xT", [KC, NT, 2, P])
        vu = a0_buf([P, NT, 2 * D])
        ge = sb("ge", [P, NT, 2 * NH])
        rot2 = a0_buf([P, NT, 2 * D])
        qk = sb("qk", [P, NT, 2 * NH, 32])
        sq = a0_buf([P, NT, 2 * D])
        n2 = sb("n2", [P, NT * 2 * NH])
        nrm = sb("nrm", [P, NT * 2 * NH])
        rn = sb("rn", [P, NT, 2 * NH])
        es = sb("es", [P, NT, 2 * NH])
        mx = sb("mx", [P, NH])
        m12 = sb("m12", [NH, 1])
        diag = sb("diag", [NH, NH])
        dsm = sb("dsm", [P, NT, NH])
        kc = sb("kc", [P, NT, NH, 3])
        v3 = a0_buf([P, NT, NH, 3, HD])
        sg = sb("sg", [P, NT, 2 * NH])
        al = sb("al", [P, NT, NH])
        be = sb("be", [P, NT, NH])
        ga = sb("ga", [P, NT, NH])
        cf = sb("cf", [P, NT, NH, 3])
        stb = a0_buf([128, 3, 12 * HD])
        wo3 = a0_buf([P, NH, 3, HD])
        o3 = sb("o3", [P, NT, D])
        hm = sb("hm", [P, NT * NH])
        hr = sb("hr", [P, NT * NH])
        yT = sb("yT", [KC, NT, 2, P])
        it = sb("it", [P, NT])
        rt = sb("rt", [P, NT, NH])
        taumu = sb("taumu", [P, D])
        a0 = {n: sem("a0_" + n) for n in (
            "set tau var sd xn xnT xT proj vu ge rope sq n2 nrm cum s mx mxT diag mb ds e kc v3 EP cf qkT_ps qkT "
            "S att st stb O w hc hsq hvar hsd y yT_ps yT op h").split()}
        lg = sb("lg", [P, TILES, NE])
        cand = sb("cand", [P, TILES, NE])
        red = sb("red", [P, TILES])
        oh = [sb(f"oh{j}", [P, TILES, NE]) for j in range(2)]
        gate = [sb(f"gate{j}", [P, TILES]) for j in range(2)]
        both = sb("both", [P, TILES, NE])
        tot = sb("tot", [P, NE * TILES])
        inc = sb("inc", [P, NE * TILES])
        pos = sb("pos", [P, TILES, NE])
        cmp = sb("cmp", [P, NB * NE])
        nblk = sb("nblk", [P, NE])
        bend = sb("bend", [P, NE])
        basee = sb("basee", [P, NE])
        onee = sb("onee", [P, NE])
        eb = sb("eb", [P, NB])
        eb_i = sb("eb_i", [P, NB], I32)
        slot = sb("slot", [P, TILES, 2])
        slot_i = sb("slot_i", [P, TILES * 2], I32)
        part_i = sb("part_i", [P, TILES * 2], I32)
        s_blk = sb("s_blk", [P, TILES * 2])
        s_row = sb("s_row", [P, TILES * 2])
        row_hot = [sb(f"row_hot{i}", [P, 128]) for i in range(4)]
        blk_hot = [sb(f"blk_hot{i}", [P, NB]) for i in range(4)]
        idx = sb("idx", [128, NB], I32)
        r = {n: sem("r_" + n) for n in "var sd xn xnT xT lg lg_ps out hot ids both rank idx ready res exp".split()}
        idx_now = [sb(f"idx_now{i}", [128, 1], I32) for i in range(UNROLL)]
        xg = [moe_buf([128, D]) for i in range(UNROLL)]
        e_w1 = [moe_buf([KC + 1, 2, FF]) for i in range(UNROLL)]
        e_w2 = [moe_buf([128, FC, D]) for i in range(UNROLL)]
        e_b2 = [moe_buf([1, D]) for i in range(UNROLL)]
        xgT = moe_buf([KC + 1, 2, BLK])
        hT = [moe_buf([128, FC, BLK]) for i in range(UNROLL)]
        yb = [moe_buf([128, D]) for i in range(UNROLL)]
        m_x = [sem(f"m_x{i}") for i in range(UNROLL)]
        m_w = [sem(f"m_w{i}") for i in range(UNROLL)]
        m_out = [sem(f"m_out{i}") for i in range(UNROLL)]
        m = {n: sem("m_" + n) for n in "xgT_ps xgT hid hT y_ps y".split()}
        slot_now = sb("slot_now", [P, 2 * NT], I32)
        yg = a1_buf([P, NT, 2, D])
        zn = a1_buf([P, NT, D])
        xzT = a1_buf([KC + 1, NT, 4, P])
        v1 = a1_buf([P, NT, NH, HD + 1])
        ge1 = a1_buf([P, NT, D])
        kg = a1_buf([P, NT, D])
        st1 = sb("st1", [128, 3, 4 * (HD + 1)])
        den = sb("den", [P, NT, NH])
        y1T = sb("y1T", [KC + 1, NT, 2, P])
        a1 = {n: sem("a1_" + n) for n in (
            "ones slot yg var sd xn var2 sd2 zn xzT_ps xzT proj v ge min em feat qkT_ps qkT S att st stb O w y yT_ps yT op h").split()}
        w_in_q = sb("w_in_q", [KC, 2, 2 * HID], BF16)
        w_out_q = sb("w_out_q", [128, 4, D], BF16)
        identb = sb("identb", [128, 128], BF16)
        eps6 = sb("eps6", [128, 1])
        wsum = sb("wsum", [128, 2])
        wscale = sb("wscale", [128, 2])
        wback = sb("wback", [128, 2])
        ssq = sb("ssq", [P, NT, 2])
        rms = sb("rms", [P, NT, 2])
        amax = sb("amax", [P, NT, 2])
        qs = sb("qs", [P, NT, 2])
        back = sb("back", [P, NT, 2])
        xr = ffn_buf([P, NT, D])
        xq = sb("xq", [P, NT, D], BF16)
        xqT = sb("xqT", [KC, NT, 2, P], BF16)
        sil = ffn_buf([P, NT, HID])
        yf = ffn_buf([P, NT, HID])
        sqf = ffn_buf([P, NT, HID])
        yq = sb("yq", [P, NT, HID], BF16)
        yqT = sb("yqT", [128, NT, 4, P], BF16)
        fo = ffn_buf([P, NT, D])
        f = {n: sem("f_" + n) for n in (
            "wsum wbc wq var sd xn sq rms xq_ xqT_ps xqT gu sil y sq2 rms2 yq yqT_ps yqT o out st").split()}
        dve_chain, act_chain, pool_chain = sem("dve_chain"), sem("act_chain"), sem("pool_chain")

        def bf16_tiles(i, n):
            return bank[i][:, :].bitcast(BF16)[:, 0:n * (P + 1)].rearrange("p (a l) -> p a l", a=n)

        block = ctx.enter_context(nc.Block())

        def all_loaded(eng, stage):
            eng.wait_ge(loaded[stage], 16 * len(plan[stage]))

        def stand_alone(eng):
            eng.sem_inc(turns_passed, 1)

        @block.sync
        def _(sp):
            for stage in plan:
                for dst, src in plan[stage]:
                    sp.dma_start(dst, src).then_inc(loaded[stage], 16)
                if stage == "tok":
                    sp.dma_start(h[IMG_TOK - 2 * P:P, :].rearrange("p (b t d) -> p b t d", t=NT, d=D)[:, :, 2, :],
                                 dram["txt"].rearrange("b p d -> p b d")).then_inc(txt_loaded, 16)
            def route(b, first):
              sp.wait_ge(r["xn"], 3 * b + 3)
              sp.dma_start(xn_dram[bass.ds(b * L, L), :].rearrange("(t p) d -> p t d", p=P),
                           xn[:, :, :]).then_inc(r["out"], 16)
            Chain(sp, None).loop(B, route)

            sp.wait_ge(r["exp"], 1)

            def store(n, s):
              sp.dma_start(y_dram[bass.ds(n * BLK, BLK), :], yb[s][:, :]).then_inc(m_out[s], 16)

            def blocks(i, first):
              for s in range(UNROLL):
                  n = UNROLL * i + s
                  if not first:
                      sp.wait_ge(m["y"], n - UNROLL + 1)
                      store(n - UNROLL, s)
                  e = sp.value_load(eb_i[0:1, bass.ds(n, 1)], min_val=0, max_val=NE - 1)
                  sp.dma_start(e_w1[s][0:KC, :, :], dram["e_w1"][bass.ds(e, 1)].rearrange("e p k f -> (e p) k f")).then_inc(m_w[s], 16)
                  sp.dma_start(e_w1[s][KC:KC + 1, 1, :], dram["e_b1"][bass.ds(e, 1)].rearrange("e p f -> (e p) f")).then_inc(m_w[s], 16)
                  sp.dma_start(e_w2[s][:, :, :], dram["e_w2"][bass.ds(e, 1)].rearrange("e p k f -> (e p) k f")).then_inc(m_w[s], 16)
                  sp.dma_start(e_b2[s][:, :], dram["e_b2"][bass.ds(e, 1)].rearrange("e p f -> (e p) f")).then_inc(m_w[s], 16)
            Chain(sp, None).loop(NB // UNROLL, blocks)
            for s in range(UNROLL):
              sp.wait_ge(m["y"], NB - UNROLL + s + 1)
              store(NB - UNROLL + s, s)
            def ffn(b, first):
              sp.wait_ge(f["o"], 3 * b + 3)
              sp.dma_start(out[bass.ds(b, 1)].rearrange("b (t p) d -> p (b t) d", p=P), fo[:, :, :]).then_inc(f["out"], 16)
            Chain(sp, None).loop(B, ffn)
            sp.wait_ge(f["out"], 16 * B)

        @block.gpsimd
        def _(pool):
            all_loaded(pool, "tok")
            for half in range(2):
                for j in range(GP):
                    pool.indirect_dma_start(g0[:, half, j, :], None, dram["patches0"],
                                            bass.IndirectOffsetOnAxis(ap=idx0[:, half, j:j + 1], axis=0)
                                            ).then_inc(gathered, 16)
                pool.indirect_dma_start(g2[:, half, :], None, dram["patches2"],
                                        bass.IndirectOffsetOnAxis(ap=idx2[:, half:half + 1], axis=0)
                                        ).then_inc(gathered, 16)
            for j in range(GP):
                pool.indirect_dma_start(g1[:, j, :], None, dram["patches1"],
                                        bass.IndirectOffsetOnAxis(ap=idx1[:, j:j + 1], axis=0)
                                        ).then_inc(gathered, 16)

            def body(b, first):
                for t in range(NT):
                    pool.wait_ge(a0["kc"], b + 1)
                    if not first:
                        pool.wait_ge(a0["O"], 3 * b + t - 2)
                    v = vu[:, t, 0:D].rearrange("p (h a d) -> p h a d", h=NH, a=1)
                    nc.gpsimd.tensor_tensor(v3[:, t], v.to_broadcast([P, NH, 3, HD]),
                                            kc[:, t].rearrange("p h (c a) -> p h c a", a=1).to_broadcast([P, NH, 3, HD]),
                                            ALU.mult).then_inc(a0["v3"], 1)
            Chain(pool, pool_chain).loop(B, body)
            chain = Chain(pool, pool_chain)
            pool.wait_ge(r["idx"], 1)
            pool.wait_ge(r["out"], 16 * B)

            def blocks(i, first):
                for s in range(UNROLL):
                    n = UNROLL * i + s
                    if not first:
                        pool.wait_ge(m["xgT_ps"], n - UNROLL + 1)
                    chain.link(nc.gpsimd.tensor_copy(idx_now[s][:, :], idx[:, bass.ds(n, 1)]))
                    stand_alone(pool)
                    pool.indirect_dma_start(xg[s][:, :], None, xn_dram,
                                            bass.IndirectOffsetOnAxis(ap=idx_now[s][:, :], axis=0)).then_inc(m_x[s], 16)
            chain.loop(NB // UNROLL, blocks)
            for s in range(UNROLL):
                pool.wait_ge(m_out[s], 16 * (NB // UNROLL))

            def rows(b, first):
                if not first:
                    pool.wait_ge(a1["yg"], 16 * 6 * b)
                    pool.wait_ge(a1["h"], 3 * b - 2)
                chain.link(nc.gpsimd.tensor_copy(slot_now[:, :], slot_i[:, bass.ds(b * 2 * NT, 2 * NT)]))
                stand_alone(pool)
                for t in range(NT):
                    for j in range(2):
                        pool.indirect_dma_start(yg[:, t, j, :], None, y_dram, bass.IndirectOffsetOnAxis(
                            ap=slot_now[:, 2 * t + j:2 * t + j + 1], axis=0)).then_inc(a1["yg"], 16)
            chain.loop(B, rows)

        @block.scalar
        def _(act):
            chain = Chain(act, act_chain)
            all_loaded(act, "tok")

            def tok(b, first):
                act.wait_ge(tok_xT_ps, b + 1)
                nc.scalar.copy(x02T[:, :], bank[0][0:48, :]).then_inc(tok_xT, 1)
                nc.scalar.copy(x1T[:, :, :].rearrange("p a t -> p (a t)"), bank[1][0:KC, 0:128]).then_inc(tok_xT, 1)
                act.wait_ge(tok_y_ps, b + 1)
                nc.scalar.copy(y1[:, :], bank[3][0:TOK1, 0:EMB]).then_inc(tok_y, 1)
                nc.scalar.copy(y2[:, :], bank[3][0:TOK2, EMB:2 * EMB]).then_inc(tok_y, 1)
                nc.scalar.activation(catT[:, 0, :], bank[2][0:EMB, 0:IMG_TOK], ACT.Identity,
                                     bias=tok_b[:, 0:1]).then_inc(tok_cat, 1)
                act.wait_ge(tok_i_ps, b + 1)
                for lvl in (1, 2):
                    nc.scalar.activation(catT[:, lvl, :], bank[4][0:EMB, (lvl - 1) * 256:lvl * 256], ACT.Identity,
                                         bias=tok_b[:, lvl:lvl + 1]).then_inc(tok_cat, 1)
            chain.loop(B, tok)

            all_loaded(act, "a0")
            act.wait_ge(a0["set"], 1)
            nc.scalar.activation(tau[:, :], tau[:, :], ACT.Exp).then_inc(a0["tau"], 1)

            def attn0(b, first):
                act.wait_ge(a0["var"], b + 1)
                nc.scalar.activation(sd[:, :], mv[:, :, 1], ACT.Sqrt, bias=eps5[0:P, 0:1]).then_inc(a0["sd"], 1)
                for j, (lo, n) in enumerate(PAIRS):
                    act.wait_ge(a0["xnT"], 2 * b + j + 1)
                    nc.scalar.copy(xT[:, lo:lo + n].rearrange("p t a l -> p (t a l)"),
                                   bank[6 + j][0:KC, 0:2 * P * n]).then_inc(a0["xT"], 1)
                for t in range(NT):
                    act.wait_ge(a0["proj"], 3 * b + t + 1)
                    nc.scalar.copy(vu[:, t], bank[2 * t + 1][0:P, 0:384]).then_inc(a0["vu"], 1)
                for t in range(NT):
                    nc.scalar.activation(ge[:, t], bank[2 * t + 1][0:P, 384:408], ACT.Exp, scale=-1.0).then_inc(a0["ge"], 1)
                for t in range(NT):
                    act.wait_ge(a0["rope"], 3 * b + t + 1)
                    nc.scalar.activation(sq[:, t].rearrange("p (h d) -> p h d", d=HD), qk[:, t, :, 0:HD],
                                         ACT.Square).then_inc(a0["sq"], 1)
                act.wait_ge(a0["ds"], b + 1)
                nc.scalar.activation(es[:, :, 0:NH], dsm[:, :, :], ACT.Exp).then_inc(a0["e"], 1)
                act.wait_ge(a0["n2"], b + 1)
                nc.scalar.activation(nrm[:, :], n2[:, :], ACT.Sqrt).then_inc(a0["nrm"], 1)
                for t in range(NT):
                    for j in range(2):
                        act.wait_ge(a0["qkT_ps"], 6 * b + 2 * t + j + 1)
                        nc.scalar.copy(qkT[:, t, 3 * j:3 * j + 3].rearrange("p a t -> p (a t)"),
                                       bank[2 * t + j][:, 0:333]).then_inc(a0["qkT"], 1)
                act.wait_ge(a0["hc"], b + 1)
                nc.scalar.activation(sq[:, :, 0:D], o3[:, :, :], ACT.Square).then_inc(a0["hsq"], 1)
                act.wait_ge(a0["hvar"], b + 1)
                nc.scalar.activation(hr[:, :], hr[:, :], ACT.Sqrt, bias=eps5[0:P, 0:1], scale=1.0 / HD).then_inc(a0["hsd"], 1)
                for j, (lo, n) in enumerate(PAIRS):
                    act.wait_ge(a0["yT_ps"], 2 * b + j + 1)
                    nc.scalar.copy(yT[:, lo:lo + n].rearrange("p t a l -> p (t a l)"),
                                   bank[7 - j][0:KC, 0:2 * P * n]).then_inc(a0["yT"], 1)
            chain.loop(B, attn0)

            def ln_sd(sems, b, dst, src, eps):
                act.wait_ge(sems[0], b + 1)
                nc.scalar.activation(dst, src, ACT.Sqrt, bias=eps[0:P, 0:1]).then_inc(sems[1], 1)

            def route(b, first):
                ln_sd((r["var"], r["sd"]), b, sd[:, :], mv[:, :, 1], eps5)
                for j, (lo, n) in enumerate(PAIRS):
                    act.wait_ge(r["xnT"], 2 * b + j + 1)
                    nc.scalar.copy(xT[:, lo:lo + n].rearrange("p t a l -> p (t a l)"),
                                   bank[6 + j][0:KC, 0:2 * P * n]).then_inc(r["xT"], 1)
            chain.loop(B, route)
            act.wait_ge(r["lg"], B + 1)
            nc.scalar.activation(lg[:, :, :], lg[:, :, :], ACT.Exp).then_inc(r["ready"], 1)

            def hidden(i, first):
                for s in range(UNROLL):
                    n = UNROLL * i + s
                    if not first:
                        act.wait_ge(m["y_ps"], n - UNROLL + 1)
                    for j in range(2):
                        act.wait_ge(m["hid"], 2 * n + j + 1)
                        nc.scalar.activation(hT[s][:, 3 * j:3 * j + 3, :].rearrange("p c t -> p (c t)"),
                                             bank[2 * s + j][:, 0:384], ACT.Gelu).then_inc(m["hT"], 1)
            chain.loop(NB // UNROLL, hidden)
            all_loaded(act, "a1")

            def attn1(b, first):
                ln_sd((a1["var"], a1["sd"]), b, sd[:, :], mv[:, :, 1], eps5)
                ln_sd((a1["var2"], a1["sd2"]), b, sd[:, :], mv[:, :, 1], eps5)
                for t in range(NT):
                    act.wait_ge(a1["xzT_ps"], 3 * b + t + 1)
                    nc.scalar.copy(xzT[0:KC, t, 0:2].rearrange("p a l -> p (a l)"), bank[5 + t][0:KC, 0:2 * P]).then_inc(a1["xzT"], 1)
                    for k in range(2):
                        nc.scalar.activation(xzT[0:KC, t, 2 + k], bank[5 + t][0:KC, P * (2 + k):P * (3 + k)], ACT.Identity,
                                             scale=a1_ln[:, k, 0:1], bias=a1_ln[:, k, 1:2]).then_inc(a1["xzT"], 1)
                for t in range(NT):
                    act.wait_ge(a1["proj"], 3 * b + t + 1)
                    nc.scalar.copy(v1[:, t, :, 0:HD], bank[2 * t + 1][0:P, 0:D].rearrange("p (h d) -> p h d", d=HD)).then_inc(a1["v"], 1)
                    nc.scalar.activation(ge1[:, t], bank[2 * t + 1][0:P, D:2 * D], ACT.Exp, scale=-1.0).then_inc(a1["ge"], 1)
                for t in range(NT):
                    act.wait_ge(a1["min"], 3 * b + t + 1)
                    nc.scalar.activation(rot1[:, t], rot1[:, t], ACT.Exp).then_inc(a1["em"], 1)
                for t in range(NT):
                    for j in range(2):
                        act.wait_ge(a1["qkT_ps"], 6 * b + 2 * t + j + 1)
                        nc.scalar.copy(qkT[:, t, 3 * j:3 * j + 3].rearrange("p a t -> p (a t)"),
                                       bank[2 * t + j][:, 0:333]).then_inc(a1["qkT"], 1)
                for j, (lo, n) in enumerate(PAIRS):
                    act.wait_ge(a1["yT_ps"], 2 * b + j + 1)
                    nc.scalar.copy(y1T[0:KC, lo:lo + n].rearrange("p t a l -> p (t a l)"),
                                   bank[6 + j][0:KC, 0:2 * P * n]).then_inc(a1["yT"], 1)
            chain.loop(B, attn1)

            def ffn(b, first):
                ln_sd((f["var"], f["sd"]), b, sd[:, :], mv[:, :, 1], eps5)
                for t in range(NT):
                    act.wait_ge(f["xn"], 3 * b + t + 1)
                    nc.scalar.activation(sqf[:, t, 0:D], xn[:, t], ACT.Square, accum_out=ssq[:, t, 0:1]).then_inc(f["sq"], 1)
                act.wait_ge(f["sq"], 3 * b + 3)
                nc.scalar.activation(rms[:, :, 0], ssq[:, :, 0], ACT.Sqrt, bias=eps6[0:P, 0:1], scale=1.0 / D).then_inc(f["rms"], 1)
                for t in range(NT):
                    act.wait_ge(f["xqT_ps"], 3 * b + t + 1)
                    nc.scalar.copy(xqT[:, t], bf16_tiles(6 + t % 2, 2)[0:KC, :, 0:P]).then_inc(f["xqT"], 1)
                for t in range(NT):
                    act.wait_ge(f["gu"], 3 * b + t + 1)
                    nc.scalar.activation(sil[:, t], bank[2 * t + 1][0:P, :], ACT.Silu, scale=back[:, t, 0:1]).then_inc(f["sil"], 1)
                for t in range(NT):
                    act.wait_ge(f["y"], 3 * b + t + 1)
                    nc.scalar.activation(sqf[:, t], yf[:, t], ACT.Square, accum_out=ssq[:, t, 1:2]).then_inc(f["sq2"], 1)
                act.wait_ge(f["sq2"], 3 * b + 3)
                nc.scalar.activation(rms[:, :, 1], ssq[:, :, 1], ACT.Sqrt, bias=eps6[0:P, 0:1], scale=1.0 / HID).then_inc(f["rms2"], 1)
                for t in range(NT):
                    act.wait_ge(f["yqT_ps"], 3 * b + t + 1)
                    nc.scalar.copy(yqT[:, t], bf16_tiles(6 + t % 2, 4)[:, :, 0:P]).then_inc(f["yqT"], 1)
            chain.loop(B, ffn)

        @block.tensor
        def _(pe):
            mm = nc.tensor.matmul
            all_loaded(pe, "tok")

            def tok(b, first):
                pe.wait_ge(tok_staged, 3 * b + 3)
                if not first:
                    pe.wait_ge(tok_xT, 2 * b)
                    stand_alone(pe)
                for half in range(2):
                    nc.tensor.transpose(bank[0][0:48, 128 * half:128 * half + 128], x0[:, half, :], ident[:, :])
                    nc.tensor.transpose(bank[0][0:48, 256 + 128 * half:384 + 128 * half], x2[:, half, :], ident[:, :])
                for k in range(2):
                    last = nc.tensor.transpose(bank[1][0:KC, TOK1 * k:TOK1 * k + TOK1], x1[:, KC * k:KC * k + KC],
                                               ident[0:TOK1, 0:TOK1])
                last.then_inc(tok_xT_ps, 1)
                pe.wait_ge(tok_xT, 2 * b + 2)
                if not first:
                    pe.wait_ge(tok_cat, 3 * b)
                    stand_alone(pe)
                mm(bank[2][0:EMB, 0:IMG_TOK], w0[:, :], x02T[:, 0:256], start=True, stop=True)
                for k in range(2):
                    mm(bank[3][0:TOK1, 0:EMB], x1T[:, k, :], w1[:, k, :], start=(k == 0), stop=(k == 1))
                x2v = x02T[:, 256:512].rearrange("p (t j) -> p t j", j=GP)
                for j in range(GP):
                    last = mm(bank[3][0:TOK2, EMB:2 * EMB], x2v[:, :, j], w2[:, j, :], start=(j == 0), stop=(j == GP - 1))
                last.then_inc(tok_y_ps, 1)
                pe.wait_ge(tok_y, 2 * b + 2)
                stand_alone(pe)
                mm(bank[4][0:EMB, 0:256], y1[:, :], interp1[:, :], start=True, stop=True)
                mm(bank[4][0:EMB, 256:512], y2[:, :], interp2[:, :], start=True, stop=True).then_inc(tok_i_ps, 1)
                pe.wait_ge(tok_cat, 3 * b + 3)
                if not first:
                    pe.wait_ge(h_tok, 2 * b)
                    stand_alone(pe)
                for t in range(NT):
                    n = P if t < 2 else IMG_TOK - 2 * P
                    dst = bank[5][0:P, D * t:D * t + D] if t < 2 else bank[6][0:n, 0:D]
                    for c in range(3):
                        mm(dst, catT[:, c, P * t:P * t + n], wf[:, c, :], start=(c == 0), stop=False)
                    last = mm(dst, ones[0:1, 0:n], bf[:, :], start=False, stop=True)
                last.then_inc(tok_h_ps, 1)
            chain = Chain(pe, None)
            chain.loop(B, tok)

            all_loaded(pe, "a0")
            pe.wait_ge(a0["tau"], 3)
            pe.wait_ge(h_tok, 2 * B)

            def attn0(b, first):
                for t in range(NT):
                    pe.wait_ge(a0["xn"], 3 * b + t + 1)
                    if not first and t == 0:
                        pe.wait_ge(a0["yT"], 2 * b)
                        pe.wait_ge(a0["h"], 3 * b)
                    for k in range(2):
                        dst = bank[6 + t // 2][0:KC, 2 * P * (t % 2) + P * k:2 * P * (t % 2) + P * k + P]
                        last = nc.tensor.transpose(dst, xn[:, t, KC * k:KC * k + KC], ident[0:P, 0:P])
                    if t:
                        last.then_inc(a0["xnT"], 1)
                for t in range(NT):
                    pe.wait_ge(a0["xT"], 2 * b + t // 2 + 1)
                    for j, (lo, n) in enumerate(((0, 384), (384, 408))):
                        for k in range(2):
                            last = mm(bank[2 * t + j][0:P, 0:n], xT[:, t, k, :], a0_w[:, k, lo:lo + n],
                                      start=(k == 0), stop=(k == 1))
                    last.then_inc(a0["proj"], 1)
                for t in range(NT):
                    pe.wait_ge(a0["vu"], 3 * b + t + 1)
                    if t == 0:
                        pe.wait_ge(a0["xT"], 2 * b + 2)
                    dst = bank[6 + t // 2][0:P, D * (t % 2):D * (t % 2) + D]
                    mm(dst, ones[0:1, 0:P], taumu[0:1, :], start=True, stop=False)
                    for s in range(t):
                        mm(dst, ones[0:P, 0:P], vu[:, s, D:2 * D], start=False, stop=False)
                    last = mm(dst, tri[:, :], vu[:, t, D:2 * D], start=False, stop=True)
                    if t:
                        last.then_inc(a0["cum"], 1)
                for t in range(NT):
                    pe.wait_ge(a0["rope"], 3 * b + t + 1)
                    pe.wait_ge(a0["ge"], 3 * b + t + 1)
                    if t == 0:
                        pe.wait_ge(a0["vu"], 3 * b + 3)
                    for j in range(2):
                        for g in range(3):
                            last = nc.tensor.transpose(bank[2 * t + j][:, P * g:P * g + P],
                                                       qk[:, t, NH * j + 4 * g:NH * j + 4 * g + 4].rearrange("p h d -> p (h d)"),
                                                       ident[0:P, 0:P])
                        last.then_inc(a0["qkT_ps"], 1)
                pe.wait_ge(a0["mx"], b + 1)
                nc.tensor.transpose(bank[7][0:NH, 192:192 + P], mx[:, :], ident[0:P, 0:P]).then_inc(a0["mxT"], 1)
                pe.wait_ge(a0["diag"], b + 1)
                mm(bank[7][0:P, 320:332], ones[0:NH, 0:P], diag[:, :], start=True, stop=True).then_inc(a0["mb"], 1)
                pe.wait_ge(a0["e"], b + 1)
                for t in range(NT):
                    dst = bank[7][0:P, 336 + 24 * t:360 + 24 * t]
                    for s in range(t):
                        mm(dst, ones[0:P, 0:P], es[:, s, :], start=(s == 0), stop=False)
                    last = mm(dst, tri[:, :], es[:, t, :], start=(t == 0), stop=True)
                last.then_inc(a0["EP"], 1)
                pe.wait_ge(a0["qkT"], 6 * b + 6)
                pe.wait_ge(a0["cf"], b + 1)
                for t in range(NT):
                    if t:
                        pe.wait_ge(a0["att"], 12 * b + 4 * t)
                    for g in range(3):
                        for i in range(4):
                            last = mm(bank[i][0:P, P * g:P * g + P], qkT[32 * i:32 * i + 32, t, 3 + g, :],
                                      qkT[32 * i:32 * i + 32, t, g, :], start=True, stop=True, tile_position=(32 * i, 0))
                            if g == 2:
                                last.then_inc(a0["S"], 1)
                    pe.wait_ge(a0["v3"], 3 * b + t + 1)
                    if t:
                        pe.wait_ge(a0["w"], 3 * b + t)
                        pe.wait_ge(a0["stb"], 2 * b + t)
                    for g in range(3):
                        if t:
                            mm(bank[4 + g // 2][0:P, 192 * (g % 2):192 * (g % 2) + 192], qkT[:, t, g, :], stb[:, g, :],
                               start=(g != 1), stop=False, skip_group_check=True)
                    for i in range(4):
                        pe.wait_ge(a0["att"], 12 * b + 4 * t + i + 1)
                        for g in range(3):
                            at = 192 * (g % 2) + 48 * i
                            last = mm(bank[4 + g // 2][0:P, at:at + 48], att[:, 4 * g + i, :],
                                      v3[:, t, 4 * g + i].rearrange("p c d -> p (c d)"),
                                      start=(t == 0 and i == 0 and g != 1), stop=True, skip_group_check=True)
                    last.then_inc(a0["O"], 1)
                    if t < 2:
                        if t == 0:
                            pe.wait_ge(a0["s"], 3 * b + 3)
                        for g in range(3):
                            last = mm(bank[6 + g // 2][:, 192 * (g % 2):192 * (g % 2) + 192],
                                      qk[:, t, NH + 4 * g:NH + 4 * g + 4].rearrange("p h d -> p (h d)"),
                                      v3[:, t, 4 * g:4 * g + 4].rearrange("p h c d -> p (h c d)"),
                                      start=(t == 0 and g != 1), stop=True, skip_group_check=True)
                        last.then_inc(a0["st"], 1)
                for t in range(NT):
                    if t == 0:
                        pe.wait_ge(a0["y"], b + 1)
                        pe.wait_ge(a0["cf"], b + 1)
                    for k in range(2):
                        dst = bank[7 - t // 2][0:KC, 2 * P * (t % 2) + P * k:2 * P * (t % 2) + P * k + P]
                        last = nc.tensor.transpose(dst, o3[:, t, KC * k:KC * k + KC], ident[0:P, 0:P])
                    if t:
                        last.then_inc(a0["yT_ps"], 1)
                for t in range(NT):
                    pe.wait_ge(a0["yT"], 2 * b + t // 2 + 1)
                    for k in range(2):
                        last = mm(bank[t][0:P, 0:D], yT[:, t, k, :], a0_wo[:, k, :], start=(k == 0), stop=(k == 1))
                    last.then_inc(a0["op"], 1)
            chain.loop(B, attn0)
            all_loaded(pe, "route")

            def pair_transposes(ready, b, src, done):
                for t in range(NT):
                    pe.wait_ge(ready, 3 * b + t + 1)
                    for k in range(2):
                        dst = bank[6 + t // 2][0:KC, 2 * P * (t % 2) + P * k:2 * P * (t % 2) + P * k + P]
                        last = nc.tensor.transpose(dst, src[:, t, KC * k:KC * k + KC], ident[0:P, 0:P])
                    if t:
                        last.then_inc(done, 1)

            pe.wait_ge(a0["yT"], 2 * B)
            pe.wait_ge(a0["h"], 3 * B)

            def route(b, first):
                if not first:
                    pe.wait_ge(r["xT"], 2 * b)
                    pe.wait_ge(r["lg"], b)
                pair_transposes(r["xn"], b, xn, r["xnT"])
                for t in range(NT):
                    pe.wait_ge(r["xT"], 2 * b + t // 2 + 1)
                    for k in range(2):
                        last = mm(bank[0][0:P, NE * t:NE * t + NE], xT[:, t, k, :], wr[:, k, :], start=(k == 0), stop=(k == 1))
                last.then_inc(r["lg_ps"], 1)
            chain.loop(B, route)
            pe.wait_ge(r["both"], 1)
            mm(bank[0][0:P, 0:TILES * NE], tri_strict[:, :], both[:, :, :].rearrange("p t e -> p (t e)"), start=True, stop=True)
            mm(bank[1][0:P, 0:TILES * NE], ones[0:P, 0:P], both[:, :, :].rearrange("p t e -> p (t e)"),
               start=True, stop=True).then_inc(r["rank"], 1)

            def ids(i, first):
                for s in range(4):
                    pe.wait_ge(r["hot"], 8 * i + 2 * s + 2)
                    mm(bank[2][:, 0:NB], row_hot[s][:, :], blk_hot[s][:, :], start=(first and s == 0), stop=True,
                       skip_group_check=True).then_inc(r["ids"], 1)
            chain.loop(TILES * 2 // 4, ids)
            pe.wait_ge(r["idx"], 1)

            def hid(n, i, s, first):
                pe.wait_ge(m_x[s], 16 * i + 16)
                if not (first and s == 0):
                    pe.wait_ge(m["xgT"], n)
                for k in range(2):
                    last = nc.tensor.transpose(bank[6][0:KC, BLK * k:BLK * k + BLK], xg[s][:, KC * k:KC * k + KC], ident[:, :])
                last.then_inc(m["xgT_ps"], 1)
                pe.wait_ge(m["xgT"], n + 1)
                pe.wait_ge(m_w[s], 64 * i + 64)
                for c in range(FC):
                    for k in range(2):
                        rows = KC + k
                        last = mm(bank[2 * s + c // 3][:, 128 * (c % 3):128 * (c % 3) + BLK],
                                  e_w1[s][0:rows, k, 128 * c:128 * c + 128], xgT[0:rows, k, :], start=(k == 0), stop=(k == 1))
                    if c % 3 == 2:
                        last.then_inc(m["hid"], 1)

            def back_to_d(n, s, started):
                if started:
                    pe.wait_ge(m["y"], n)
                mm(bank[7][:, 0:D], ones[0:1, :], e_b2[s][:, :], start=True, stop=False)
                for c in range(FC):
                    if c % 3 == 0:
                        pe.wait_ge(m["hT"], 2 * n + c // 3 + 1)
                    last = mm(bank[7][:, 0:D], hT[s][:, c, :], e_w2[s][:, c, :], start=False, stop=(c == FC - 1))
                last.then_inc(m["y_ps"], 1)

            def blocks(i, first):
                for s in range(UNROLL):
                    n = UNROLL * i + s
                    hid(n, i, s, first)
                    if not (first and s == 0):
                        back_to_d(n - 1, (s - 1) % UNROLL, not (first and s == 1))
            chain.loop(NB // UNROLL, blocks)
            back_to_d(NB - 1, (NB - 1) % UNROLL, True)
            all_loaded(pe, "a1")
            pe.wait_ge(m["y"], NB)
            pe.wait_ge(a1["ones"], 1)

            def attn1(b, first):
                for t in range(NT):
                    pe.wait_ge(a1["xn"], 3 * b + t + 1)
                    pe.wait_ge(a1["zn"], 3 * b + t + 1)
                    if t == 0 and not first:
                        pe.wait_ge(a1["yT"], 2 * b)
                        pe.wait_ge(a1["h"], 3 * b)
                    for a, src in enumerate((xn, zn)):
                        for k in range(2):
                            last = nc.tensor.transpose(bank[5 + t][0:KC, P * (2 * a + k):P * (2 * a + k + 1)],
                                                       src[:, t, KC * k:KC * k + KC], ident[0:P, 0:P])
                    last.then_inc(a1["xzT_ps"], 1)
                for t in range(NT):
                    pe.wait_ge(a1["xzT"], 9 * b + 3 * t + 3)
                    if t == 2:
                        pe.wait_ge(a1["xzT"], 9 * b + 9)
                    for dst, at, w, lo, n in ((bank[2 * t][0:P, 0:384], 2, a1_w, 0, 384),
                                              (bank[2 * t + 1][0:P, 0:D], 2, a1_w, 384, D),
                                              (bank[2 * t + 1][0:P, D:2 * D], 0, a1_wg, 0, D)):
                        for k in range(2):
                            last = mm(dst, xzT[0:KC + k, t, at + k], w[0:KC + k, k, lo:lo + n], start=(k == 0), stop=(k == 1))
                    last.then_inc(a1["proj"], 1)
                for t in range(NT):
                    pe.wait_ge(a1["feat"], 6 * b + 2 * t + 2)
                    pe.wait_ge(a1["ge"], 3 * b + t + 1)
                    for j in range(2):
                        for g in range(3):
                            last = nc.tensor.transpose(bank[2 * t + j][:, P * g:P * g + P],
                                                       qk[:, t, NH * j + 4 * g:NH * j + 4 * g + 4].rearrange("p h d -> p (h d)"),
                                                       ident[0:P, 0:P])
                        last.then_inc(a1["qkT_ps"], 1)
                pe.wait_ge(a1["qkT"], 6 * b + 6)
                W = 4 * (HD + 1)
                for t in range(NT):
                    if t:
                        pe.wait_ge(a1["att"], 12 * b + 4 * t)
                    for g in range(3):
                        for i in range(4):
                            last = mm(bank[i][0:P, P * g:P * g + P], qkT[32 * i:32 * i + 32, t, 3 + g, :],
                                      qkT[32 * i:32 * i + 32, t, g, :], start=True, stop=True, tile_position=(32 * i, 0))
                            if g == 2:
                                last.then_inc(a1["S"], 1)
                    if t:
                        pe.wait_ge(a1["w"], 3 * b + t)
                        pe.wait_ge(a1["stb"], 2 * b + t)
                        for g in range(3):
                            mm(bank[4][0:P, W * g:W * g + W], qkT[:, t, g, :], st1[:, g, :],
                               start=(g == 0), stop=False, skip_group_check=True)
                    for i in range(4):
                        pe.wait_ge(a1["att"], 12 * b + 4 * t + i + 1)
                        for g in range(3):
                            at = W * g + (HD + 1) * i
                            last = mm(bank[4][0:P, at:at + HD + 1], att[:, 4 * g + i, :], v1[:, t, 4 * g + i],
                                      start=(t == 0 and i == 0 and g == 0), stop=True, skip_group_check=True)
                    last.then_inc(a1["O"], 1)
                    if t < 2:
                        for g in range(3):
                            last = mm(bank[5][:, W * g:W * g + W],
                                      qk[:, t, NH + 4 * g:NH + 4 * g + 4].rearrange("p h d -> p (h d)"),
                                      v1[:, t, 4 * g:4 * g + 4].rearrange("p h d -> p (h d)"),
                                      start=(t == 0 and g == 0), stop=True, skip_group_check=True)
                        last.then_inc(a1["st"], 1)
                pair_transposes(a1["w"], b, o3, a1["yT_ps"])
                for t in range(NT):
                    pe.wait_ge(a1["yT"], 2 * b + t // 2 + 1)
                    for k in range(2):
                        last = mm(bank[t][0:P, 0:D], y1T[0:KC + k, t, k, :], a1_wo[0:KC + k, k, :], start=(k == 0), stop=(k == 1))
                    last.then_inc(a1["op"], 1)
            chain.loop(B, attn1)
            pe.wait_ge(f["wsum"], 2)
            pe.wait_ge(a1["h"], 3 * B)
            pe.wait_ge(a1["yT"], 2 * B)
            mm(bank[0][:, 0:1], ones[0:KC, :], wsum[0:KC, 0:1], start=True, stop=True)
            mm(bank[0][:, 1:2], ones[:, :], wsum[:, 1:2], start=True, stop=True).then_inc(f["wbc"], 1)
            pe.wait_ge(f["wq"], 2)

            def ffn(b, first):
                for t in range(NT):
                    pe.wait_ge(f["xq_"], 3 * b + t + 1)
                    if t == 2:
                        pe.wait_ge(f["xqT"], 3 * b + 1)
                    elif not first:
                        pe.wait_ge(f["yqT"], 3 * b)
                    tb = bf16_tiles(6 + t % 2, 2)
                    for k in range(2):
                        last = nc.tensor.transpose(tb[0:KC, k, 0:P], xq[:, t, KC * k:KC * k + KC], identb[0:P, 0:P])
                    last.then_inc(f["xqT_ps"], 1)
                for t in range(NT):
                    pe.wait_ge(f["xqT"], 3 * b + t + 1)
                    if t == 0 and not first:
                        pe.wait_ge(f["o"], 3 * b)
                    for j in range(2):
                        for k in range(2):
                            last = mm(bank[2 * t + j][0:P, :], xqT[:, t, k, :], w_in_q[:, k, HID * j:HID * j + HID],
                                      start=(k == 0), stop=(k == 1))
                    last.then_inc(f["gu"], 1)
                for t in range(NT):
                    pe.wait_ge(f["yq"], 3 * b + t + 1)
                    if t == 0:
                        pe.wait_ge(f["xqT"], 3 * b + 3)
                    elif t == 2:
                        pe.wait_ge(f["yqT"], 3 * b + 1)
                    tb = bf16_tiles(6 + t % 2, 4)
                    for c in range(4):
                        last = nc.tensor.transpose(tb[:, c, 0:P], yq[:, t, 128 * c:128 * c + 128], identb[0:P, 0:P])
                    last.then_inc(f["yqT_ps"], 1)
                for t in range(NT):
                    pe.wait_ge(f["yqT"], 3 * b + t + 1)
                    for c in range(4):
                        last = mm(bank[t][0:P, 0:D], yqT[:, t, c, :], w_out_q[:, c, :], start=(c == 0), stop=(c == 3))
                    last.then_inc(f["st"], 1)
            chain.loop(B, ffn)

        @block.vector
        def _(dve):
            chain = Chain(dve, dve_chain)
            link, v = chain.link, nc.vector
            v.memset(eps5[:, :], 1e-5).then_inc(eps_set, 1)
            all_loaded(dve, "tok")
            dve.wait_ge(gathered, 16 * (2 * GP + 2 + GP))

            def tok(b, first):
                if not first:
                    dve.wait_ge(tok_xT_ps, b)
                v.tensor_copy(x0[:, :, :].rearrange("p a (j c) -> p a j c", c=3),
                              g0[:, :, :, bass.ds(b * 3, 3)]).then_inc(tok_staged, 1)
                v.tensor_copy(x1[:, :].rearrange("p (j c) -> p j c", c=12),
                              g1[:, :, bass.ds(b * 12, 12)]).then_inc(tok_staged, 1)
                v.tensor_copy(x2[:, :, :], g2[:, :, bass.ds(b * 48, 48)]).then_inc(tok_staged, 1)
                dve.wait_ge(tok_h_ps, b + 1)
                v.tensor_copy(tile_of(h, 3 * b, 2), bank[5][0:P, 0:2 * D]).then_inc(h_tok, 1)
                v.tensor_copy(h[0:IMG_TOK - 2 * P, bass.ds((3 * b + 2) * D, D)],
                              bank[6][0:IMG_TOK - 2 * P, 0:D]).then_inc(h_tok, 1)
            chain.loop(B, tok)
            dve.wait_ge(txt_loaded, 16)

            all_loaded(dve, "a0")
            v.memset(qk[:, :, :, :], 0.0)
            link(v.tensor_scalar(tau[:, :], tau[:, :], -50.0, 30.0, ALU.max, ALU.min))
            dve.sem_inc(a0["set"], 1)
            dve.wait_ge(a0["tau"], 1)
            v.tensor_tensor(taumu[:, :].rearrange("p (h d) -> p h d", d=HD), mu[:, :].rearrange("p (h d) -> p h d", d=HD),
                            tau[:, :].rearrange("p (h a) -> p h a", a=1).to_broadcast([P, NH, HD]), ALU.mult).then_inc(a0["tau"], 1)
            v.reciprocal(it[:, :], time[:, :]).then_inc(a0["tau"], 1)

            def b3(ap2, shape, axis):
                pat = {2: "p (h a) -> p h a", 1: "p (a h) -> p a h"}[axis]
                return ap2.rearrange(pat, a=1).to_broadcast(shape)

            link(v.tensor_tensor(rt[:, :, :], b3(time[:, :], [P, NT, NH], 2), b3(tau[:, :], [P, NT, NH], 1), ALU.add))
            link(v.reciprocal(rt[:, :, :], rt[:, :, :]))
            link(v.tensor_scalar(rt[:, :, :], rt[:, :, :], -1.0 / np.sqrt(HD), None, ALU.mult))

            def attn0(b, first):
                for t in range(NT):
                    k = chain.step(v.bn_stats(stats[:, t, :], tile_of(h, 3 * b + t)))
                chain.wait(k)
                stand_alone(dve)
                for t in range(NT):
                    k = chain.step(v.bn_aggr(mv[:, t, :], stats[:, t, :]))
                chain.wait(k)
                dve.sem_inc(a0["var"], 1)
                dve.wait_ge(a0["sd"], b + 1)
                link(v.reciprocal(rs[:, :], sd[:, :]))
                for t in range(NT):
                    v.tensor_scalar(xn[:, t, :], tile_of(h, 3 * b + t), mv[:, t, 0:1], rs[:, t:t + 1],
                                    ALU.subtract, ALU.mult).then_inc(a0["xn"], 1)
                ks = []
                for t in range(NT):
                    dve.wait_ge(a0["proj"], 3 * b + t + 1)
                    q = bank[2 * t][0:P, 0:384].rearrange("p (h c d) -> p h c d", c=2, d=HD // 2)
                    tab = lambda c, lo, n: c[:, t, lo:lo + n].rearrange("p (a d) -> p a d", a=1).to_broadcast([P, 2 * NH, n])
                    r1 = rot1[:, t].rearrange("p (h d) -> p h d", d=HD)
                    r2 = rot2[:, t].rearrange("p (h c d) -> p h c d", c=2, d=HD // 2)
                    chain.step(v.tensor_tensor(r1, bank[2 * t][0:P, 0:384].rearrange("p (h d) -> p h d", d=HD), tab(cos, 0, HD), ALU.mult))
                    chain.step(v.tensor_tensor(r2[:, :, 0], q[:, :, 1], tab(sin, 0, 8), ALU.mult))
                    k = chain.step(v.tensor_tensor(r2[:, :, 1], q[:, :, 0], tab(sin, 8, 8), ALU.mult))
                    chain.wait(k)
                    v.tensor_tensor(qk[:, t, :, 0:HD], r1, rot2[:, t].rearrange("p (h d) -> p h d", d=HD), ALU.add).then_inc(a0["rope"], 1)
                for t in range(NT):
                    dve.wait_ge(a0["cum"], 2 * b + t // 2 + 1)
                    cum = bank[6 + t // 2][0:P, D * (t % 2):D * (t % 2) + D]
                    link(v.tensor_tensor(rot1[:, t, 0:D], vu[:, t, D:2 * D], cum, ALU.mult))
                    link(v.tensor_reduce(es[:, t, NH:2 * NH], rot1[:, t, 0:D].rearrange("p (h d) -> p h d", d=HD), AX, ALU.add))
                    v.tensor_tensor(es[:, t, NH:2 * NH], es[:, t, NH:2 * NH], rt[:, t, :], ALU.mult).then_inc(a0["s"], 1)
                dve.wait_ge(a0["s"], 3 * b + 3)
                v.tensor_reduce(mx[:, :], es[:, :, NH:2 * NH].rearrange("p t h -> p h t"), AX, ALU.max).then_inc(a0["mx"], 1)
                dve.wait_ge(a0["sq"], 3 * b + 3)
                v.tensor_reduce(n2[:, :], sq[:, :, :].rearrange("p t (h d) -> p (t h) d", d=HD), AX, ALU.add).then_inc(a0["n2"], 1)
                dve.wait_ge(a0["mxT"], b + 1)
                link(v.tensor_reduce(m12[:, :], bank[7][0:NH, 192:192 + P], AX, ALU.max))
                v.tensor_scalar(diag[:, :], ident[0:NH, 0:NH], m12[:, 0:1], None, ALU.mult).then_inc(a0["diag"], 1)
                dve.wait_ge(a0["mb"], b + 1)
                v.tensor_tensor(dsm[:, :, :], es[:, :, NH:2 * NH], b3(bank[7][0:P, 320:332], [P, NT, NH], 1),
                                ALU.subtract).then_inc(a0["ds"], 1)
                dve.wait_ge(a0["nrm"], b + 1)
                link(v.tensor_scalar(nrm[:, :], nrm[:, :], 1e-12, None, ALU.max))
                link(v.reciprocal(rn[:, :, :].rearrange("p t h -> p (t h)"), nrm[:, :]))
                dve.wait_ge(a0["e"], b + 1)
                chain.step(v.tensor_tensor(kc[:, :, :, 0], es[:, :, 0:NH], rn[:, :, NH:2 * NH], ALU.mult))
                k = chain.step(v.tensor_tensor(kc[:, :, :, 1], es[:, :, NH:2 * NH], rn[:, :, NH:2 * NH], ALU.mult))
                chain.wait(k)
                v.tensor_copy(kc[:, :, :, 2], rn[:, :, NH:2 * NH]).then_inc(a0["kc"], 1)
                dve.wait_ge(a0["ge"], 3 * b + 3)
                link(v.tensor_scalar(ge[:, :, :], ge[:, :, :], 1.0, None, ALU.add))
                link(v.reciprocal(sg[:, :, :], ge[:, :, :]))
                dve.wait_ge(a0["EP"], b + 1)
                ep = bank[7][0:P, 336:408].rearrange("p (t h) -> p t h", t=NT)
                itb = b3(it[:, :], [P, NT, NH], 2)
                chain.step(v.tensor_scalar(al[:, :, :], ep[:, :, 0:NH], 1e-12, None, ALU.add))
                link(v.tensor_tensor(be[:, :, :], sg[:, :, 0:NH], sg[:, :, NH:2 * NH], ALU.subtract))
                chain.step(v.reciprocal(al[:, :, :], al[:, :, :]))
                link(v.tensor_tensor(be[:, :, :], be[:, :, :], itb, ALU.mult))
                chain.step(v.tensor_tensor(al[:, :, :], al[:, :, :], sg[:, :, NH:2 * NH], ALU.mult))
                link(v.tensor_tensor(ga[:, :, :], be[:, :, :], ep[:, :, NH:2 * NH], ALU.mult))
                link(v.tensor_tensor(ga[:, :, :], ga[:, :, :], sg[:, :, NH:2 * NH], ALU.add))
                link(v.scalar_tensor_tensor(ga[:, :, :], ga[:, :, :], -1.0, itb, ALU.mult, ALU.mult))
                for c, x in enumerate((al, be, ga)):
                    k = chain.step(v.tensor_tensor(cf[:, :, :, c], x[:, :, :], rn[:, :, 0:NH], ALU.mult))
                chain.wait(k)
                dve.sem_inc(a0["cf"], 1)
                for t in range(NT):
                    if t:
                        dve.wait_ge(a0["O"], 3 * b + t)
                    for i in range(4):
                        dve.wait_ge(a0["S"], 12 * b + 4 * t + i + 1)
                        v.tensor_tensor(att[:, :, :].rearrange("p (g i) l -> p i g l", i=4)[:, i],
                                        bank[i][0:P, 0:3 * P].rearrange("p (g l) -> p g l", g=3),
                                        b3(tri[:, :], [P, 3, P], 1), ALU.mult).then_inc(a0["att"], 1)
                    if t < 2:
                        dve.wait_ge(a0["st"], 2 * b + t + 1)
                        chain.step(v.tensor_tensor(stb[:, 0:2, :], bank[6][:, 0:384].rearrange("p (g n) -> p g n", g=2),
                                                   head_mask0[:, :].rearrange("p (a n) -> p a n", a=1).to_broadcast([128, 2, 192]), ALU.mult))
                        chain.wait(chain.k)
                        v.tensor_tensor(stb[:, 2, :], bank[7][:, 0:192], head_mask0[:, :], ALU.mult).then_inc(a0["stb"], 1)
                    dve.wait_ge(a0["O"], 3 * b + t + 1)
                    cft = cf[:, t].rearrange("p h (c a) -> p h c a", a=1)
                    link(v.tensor_tensor(wo3[:, 0:8], bank[4][0:P, 0:384].rearrange("p (h c d) -> p h c d", c=3, d=HD),
                                         cft[:, 0:8].to_broadcast([P, 8, 3, HD]), ALU.mult))
                    v.tensor_tensor(wo3[:, 8:12], bank[5][0:P, 0:192].rearrange("p (h c d) -> p h c d", c=3, d=HD),
                                    cft[:, 8:12].to_broadcast([P, 4, 3, HD]), ALU.mult).then_inc(a0["w"], 1)
                    dve.wait_ge(a0["w"], 3 * b + t + 1)
                    k = chain.step(v.tensor_reduce(o3[:, t, :].rearrange("p (h d) -> p h d", d=HD),
                                                   wo3[:, :, :, :].rearrange("p h c d -> p h d c"), AX, ALU.add))
                chain.wait(k)
                o = o3[:, :, :].rearrange("p t (h d) -> p (t h) d", d=HD)
                link(v.tensor_reduce(hm[:, :], o, AX, ALU.add))
                link(v.tensor_scalar(hm[:, :], hm[:, :], 1.0 / HD, None, ALU.mult))
                v.tensor_tensor(o, o, b3(hm[:, :], [P, NT * NH, HD], 2), ALU.subtract).then_inc(a0["hc"], 1)
                dve.wait_ge(a0["hsq"], b + 1)
                v.tensor_reduce(hr[:, :], sq[:, :, 0:D].rearrange("p t (h d) -> p t h d", d=HD), AX, ALU.add).then_inc(a0["hvar"], 1)
                dve.wait_ge(a0["hsd"], b + 1)
                link(v.reciprocal(hr[:, :], hr[:, :]))
                v.tensor_tensor(o, o, b3(hr[:, :], [P, NT * NH, HD], 2), ALU.mult).then_inc(a0["y"], 1)
                for t in range(NT):
                    dve.wait_ge(a0["op"], 3 * b + t + 1)
                    v.tensor_tensor(tile_of(h, 3 * b + t), tile_of(h, 3 * b + t), bank[t][0:P, 0:D], ALU.add).then_inc(a0["h"], 1)
            chain.loop(B, attn0)
            all_loaded(dve, "route")

            def layer_norm(b, sems, i, src, dst, dst_sem):
                stand_alone(dve)
                for t in range(NT):
                    k = chain.step(v.bn_stats(stats[:, t, :], src(t)))
                chain.wait(k)
                stand_alone(dve)
                for t in range(NT):
                    k = chain.step(v.bn_aggr(mv[:, t, :], stats[:, t, :]))
                chain.wait(k)
                dve.sem_inc(sems[0], 1)
                dve.wait_ge(sems[1], b + 1)
                link(v.reciprocal(rs[:, :], sd[:, :]))
                for t in range(NT):
                    v.tensor_scalar(dst[:, t, :], src(t), mv[:, t, 0:1], rs[:, t:t + 1],
                                    ALU.subtract, ALU.mult).then_inc(dst_sem, 1)

            def route(b, first):
                if not first:
                    dve.wait_ge(r["out"], 16 * b)
                layer_norm(b, (r["var"], r["sd"]), 0, lambda t: tile_of(h, 3 * b + t), xn, r["xn"])
                dve.wait_ge(r["xn"], 3 * b + 3)
                link(v.tensor_tensor(tile_of(h, 3 * b, 3), tile_of(h, 3 * b, 3), xn[:, :, :].rearrange("p t d -> p (t d)"), ALU.add))
                dve.wait_ge(r["lg_ps"], b + 1)
                v.tensor_copy(lg[:, bass.ds(3 * b, NT), :].rearrange("p t e -> p (t e)"), bank[0][0:P, 0:NT * NE]).then_inc(r["lg"], 1)
            chain.loop(B, route)
            te = [P, TILES, NE]
            dve.wait_ge(r["lg"], B)
            link(v.tensor_reduce(red[:, :], lg[:, :, :], AX, ALU.max))
            v.tensor_tensor(lg[:, :, :], lg[:, :, :], b3(red[:, :], te, 2), ALU.subtract).then_inc(r["lg"], 1)
            dve.wait_ge(r["ready"], 1)
            link(v.tensor_reduce(red[:, :], lg[:, :, :], AX, ALU.add))
            link(v.reciprocal(red[:, :], red[:, :]))
            link(v.tensor_tensor(lg[:, :, :], lg[:, :, :], b3(red[:, :], te, 2), ALU.mult))
            ie = b3(iota[:, 0:NE], te, 1)
            for j in range(2):
                link(v.tensor_reduce(gate[j][:, :], lg[:, :, :], AX, ALU.max))
                link(v.tensor_tensor(cand[:, :, :], lg[:, :, :], b3(gate[j][:, :], te, 2), ALU.is_lt))
                link(v.scalar_tensor_tensor(cand[:, :, :], cand[:, :, :], float(NE), ie, ALU.mult, ALU.add))
                link(v.tensor_reduce(red[:, :], cand[:, :, :], AX, ALU.min))
                link(v.tensor_tensor(oh[j][:, :, :], ie, b3(red[:, :], te, 2), ALU.is_equal))
                if j == 0:
                    link(v.scalar_tensor_tensor(lg[:, :, :], oh[0][:, :, :], -2.0, lg[:, :, :], ALU.mult, ALU.add))
            v.tensor_tensor(both[:, :, :], oh[0][:, :, :], oh[1][:, :, :], ALU.add).then_inc(r["both"], 1)
            link(v.memset(onee[:, :], 1.0))
            dve.wait_ge(r["rank"], 1)
            em = "p (t e) -> p e t"
            link(v.tensor_copy(tot[:, :].rearrange("p (e t) -> p e t", t=TILES), bank[1][0:P, 0:TILES * NE].rearrange(em, e=NE)))
            link(v.tensor_tensor_scan(inc[:, :], reset[:, :], tot[:, :], 0.0, ALU.mult, ALU.add))
            inc3 = inc[:, :].rearrange("p (e t) -> p e t", t=TILES)
            c3 = cmp[:, 0:NE * MAXB].rearrange("p (e n) -> p e n", e=NE)
            link(v.tensor_tensor(c3, inc3[:, :, TILES - 1:TILES].to_broadcast([P, NE, MAXB]), b3(steps[:, :], [P, NE, MAXB], 1), ALU.is_gt))
            link(v.tensor_reduce(nblk[:, :], c3, AX, ALU.add))
            link(v.tensor_tensor_scan(bend[:, :], onee[:, :], nblk[:, :], 0.0, ALU.mult, ALU.add))
            link(v.tensor_tensor(basee[:, :], bend[:, :], nblk[:, :], ALU.subtract))
            link(v.tensor_scalar(basee[:, :], basee[:, :], float(BLK), None, ALU.mult))
            be3 = cmp[:, 0:NB * NE].rearrange("p (n e) -> p n e", e=NE)
            link(v.tensor_tensor(be3, b3(bend[:, :], [P, NB, NE], 1), b3(iota[:, 0:NB], [P, NB, NE], 2), ALU.is_le))
            link(v.tensor_reduce(eb[:, :], be3, AX, ALU.add))
            link(v.tensor_scalar(eb[:, :], eb[:, :], float(NE - 1), None, ALU.min))
            v.tensor_copy(eb_i[:, :], eb[:, :]).then_inc(r["exp"], 1)
            link(v.tensor_tensor(pos[:, :, :].rearrange("p t e -> p e t"), inc3, tot[:, :].rearrange("p (e t) -> p e t", t=TILES), ALU.subtract))
            link(v.tensor_tensor(pos[:, :, :], pos[:, :, :], bank[0][0:P, 0:TILES * NE].rearrange("p (t e) -> p t e", e=NE), ALU.add))
            link(v.tensor_tensor(pos[:, :, :], pos[:, :, :], b3(basee[:, :], te, 1), ALU.add))
            for j in range(2):
                link(v.tensor_tensor(cand[:, :, :], oh[j][:, :, :], pos[:, :, :], ALU.mult))
                link(v.tensor_reduce(slot[:, :, j], cand[:, :, :], AX, ALU.add))
            link(v.tensor_copy(slot_i[:, :], slot[:, :, :].rearrange("p t j -> p (t j)")))
            link(v.tensor_scalar(part_i[:, :], slot_i[:, :], 7, None, ALU.arith_shift_right))
            link(v.tensor_copy(s_blk[:, :], part_i[:, :]))
            link(v.scalar_tensor_tensor(s_row[:, :], s_blk[:, :], -float(BLK), slot[:, :, :].rearrange("p t j -> p (t j)"), ALU.mult, ALU.add))

            def ids(i, first):
                for s in range(4):
                    u = 4 * i + s
                    if not first:
                        dve.wait_ge(r["ids"], u - 3)
                    v.tensor_scalar(row_hot[s][:, :], iota[:, :], s_row[:, bass.ds(u, 1)], None, ALU.is_equal).then_inc(r["hot"], 1)
                    v.tensor_scalar(blk_hot[s][:, :], iota[:, 0:NB], s_blk[:, bass.ds(u, 1)], token[:, bass.ds(2 * i + s // 2, 1)],
                                    ALU.is_equal, ALU.mult).then_inc(r["hot"], 1)
            chain.loop(TILES * 2 // 4, ids)
            dve.wait_ge(r["ids"], 2 * TILES)
            v.memset(xgT[:, :, :], 1.0)
            v.tensor_copy(idx[:, :], bank[2][:, 0:NB]).then_inc(r["idx"], 1)
            dve.wait_ge(r["idx"], 1)

            def y_out(n, i, s, first):
                dve.wait_ge(m["y_ps"], n + 1)
                if not first:
                    dve.wait_ge(m_out[s], 16 * i)
                v.tensor_copy(yb[s][:, :], bank[7][:, 0:D]).then_inc(m["y"], 1)

            def blocks(i, first):
                for s in range(UNROLL):
                    n = UNROLL * i + s
                    dve.wait_ge(m["xgT_ps"], n + 1)
                    if not (first and s == 0):
                        dve.wait_ge(m["hid"], 2 * n)
                    v.tensor_copy(xgT[0:KC, :, :].rearrange("p a t -> p (a t)"), bank[6][0:KC, 0:2 * BLK]).then_inc(m["xgT"], 1)
                    if s:
                        y_out(n - 1, i, s - 1, first)
                    elif not first:
                        y_out(n - 1, i - 1, UNROLL - 1, True)
            def y_last(i, first):
                pass
            chain.loop(NB // UNROLL, blocks)
            y_out(NB - 1, NB // UNROLL - 1, UNROLL - 1, False)
            all_loaded(dve, "a1")
            link(v.memset(v1[:, :, :, :], 1.0))
            link(v.memset(y1T[:, :, :, :], 1.0))
            link(v.memset(xzT[:, :, :, :], 1.0))
            dve.sem_inc(a1["ones"], 1)

            def attn1(b, first):
                tile = lambda t: tile_of(h, 3 * b + t)
                dve.wait_ge(a1["yg"], 96 * b + 96)
                for j in range(2):
                    for t in range(NT):
                        k = chain.step(v.scalar_tensor_tensor(tile(t), yg[:, t, j, :], gate[j][:, bass.ds(3 * b + t, 1)], tile(t),
                                                              ALU.mult, ALU.add))
                    chain.wait(k)
                layer_norm(b, (a1["var"], a1["sd"]), 0, tile, xn, a1["xn"])
                dve.wait_ge(a1["xn"], 3 * b + 3)
                layer_norm(b, (a1["var2"], a1["sd2"]), 0, lambda t: xn[:, t, :], zn, a1["zn"])
                hv = lambda ap: ap.rearrange("p (h d) -> p h d", d=HD)
                for t in range(NT):
                    dve.wait_ge(a1["proj"], 3 * b + t + 1)
                    q, kk = bank[2 * t][0:P, 0:D], bank[2 * t][0:P, D:2 * D]
                    chain.step(v.tensor_scalar(rot1[:, t, 0:D], q, 0.0, None, ALU.min))
                    dve.wait_ge(a1["ge"], 3 * b + t + 1)
                    link(v.tensor_scalar(ge1[:, t], ge1[:, t], 1.0, None, ALU.add))
                    link(v.reciprocal(ge1[:, t], ge1[:, t]))
                    link(v.tensor_tensor(kg[:, t], kk, ge1[:, t], ALU.mult))
                    v.tensor_scalar(rot1[:, t, D:2 * D], kg[:, t], 0.0, None, ALU.min).then_inc(a1["min"], 1)
                for t in range(NT):
                    dve.wait_ge(a1["em"], 3 * b + t + 1)
                    v.scalar_tensor_tensor(qk[:, t, 0:NH, 0:HD], hv(bank[2 * t][0:P, 0:D]), 0.0, hv(rot1[:, t, 0:D]),
                                           ALU.max, ALU.add).then_inc(a1["feat"], 1)
                    v.scalar_tensor_tensor(qk[:, t, NH:2 * NH, 0:HD], hv(kg[:, t]), 0.0, hv(rot1[:, t, D:2 * D]),
                                           ALU.max, ALU.add).then_inc(a1["feat"], 1)
                W = 4 * (HD + 1)
                for t in range(NT):
                    if t:
                        dve.wait_ge(a1["O"], 3 * b + t)
                    for i in range(4):
                        dve.wait_ge(a1["S"], 12 * b + 4 * t + i + 1)
                        v.tensor_tensor(att[:, :, :].rearrange("p (g i) l -> p i g l", i=4)[:, i],
                                        bank[i][0:P, 0:3 * P].rearrange("p (g l) -> p g l", g=3),
                                        b3(tri[:, :], [P, 3, P], 1), ALU.mult).then_inc(a1["att"], 1)
                    if t < 2:
                        dve.wait_ge(a1["st"], 2 * b + t + 1)
                        v.tensor_tensor(st1[:, :, :], bank[5][:, 0:3 * W].rearrange("p (g n) -> p g n", g=3),
                                        b3(head_mask1[:, :], [128, 3, W], 1), ALU.mult).then_inc(a1["stb"], 1)
                    dve.wait_ge(a1["O"], 3 * b + t + 1)
                    oo = bank[4][0:P, 0:3 * W].rearrange("p (h d) -> p h d", d=HD + 1)
                    link(v.tensor_scalar(den[:, t], oo[:, :, HD], 1e-6, None, ALU.add))
                    link(v.reciprocal(den[:, t], den[:, t]))
                    v.tensor_tensor(hv(o3[:, t]), oo[:, :, 0:HD], b3(den[:, t], [P, NH, HD], 2), ALU.mult).then_inc(a1["w"], 1)
                dve.wait_ge(a1["w"], 3 * b + 3)
                for t in range(NT):
                    dve.wait_ge(a1["op"], 3 * b + t + 1)
                    v.tensor_tensor(tile(t), tile(t), bank[t][0:P, 0:D], ALU.add).then_inc(a1["h"], 1)
            chain.loop(B, attn1)
            all_loaded(dve, "f")
            dve.wait_ge(a1["h"], 3 * B)
            v.memset(eps6[:, :], 1e-6)
            chain.step(v.tensor_copy(identb[:, :], ident[:, :]))
            wsets = ((w_in[:, :, :].rearrange("p a n -> p (a n)"), w_in_q[:, :, :].rearrange("p a n -> p (a n)"), KC, D * 2 * HID),
                     (w_out[:, :, :].rearrange("p a n -> p (a n)"), w_out_q[:, :, :].rearrange("p a n -> p (a n)"), 128, D * HID))
            for i, (w, _, rows, _) in enumerate(wsets):
                v.tensor_reduce(wsum[0:rows, i:i + 1], w, AX, ALU.add, apply_absolute_value=True).then_inc(f["wsum"], 1)
            dve.wait_ge(f["wbc"], 1)
            for i, (_, _, _, count) in enumerate(wsets):
                k = chain.step(v.tensor_scalar(wback[:, i:i + 1], bank[0][:, i:i + 1], 1.0 / count, 1e-5, ALU.mult, ALU.max))
            chain.wait(k)
            link(v.reciprocal(wscale[:, :], wback[:, :]))
            for i, (w, wq, rows, _) in enumerate(wsets):
                link(v.tensor_scalar(w, w, wscale[0:rows, i:i + 1], MAGIC, ALU.mult, ALU.add))
                link(v.tensor_scalar(w, w, MAGIC, -1.0, ALU.subtract, ALU.max))
                v.tensor_scalar(wq, w, 1.0, None, ALU.min).then_inc(f["wq"], 1)

            def quantize(src, dst, t, j, sem_):
                link(v.tensor_reduce(amax[:, t, j:j + 1], src, AX, ALU.max, apply_absolute_value=True))
                link(v.tensor_scalar(amax[:, t, j:j + 1], amax[:, t, j:j + 1], 1e-5, None, ALU.max))
                link(v.reciprocal(qs[:, t, j:j + 1], amax[:, t, j:j + 1]))
                link(v.tensor_scalar(qs[:, t, j:j + 1], qs[:, t, j:j + 1], 127.0, None, ALU.mult))
                link(v.tensor_scalar(back[:, t, j:j + 1], amax[:, t, j:j + 1], 1.0 / 127.0, wback[0:P, j:j + 1], ALU.mult, ALU.mult))
                link(v.tensor_scalar(src, src, qs[:, t, j:j + 1], MAGIC, ALU.mult, ALU.add))
                link(v.tensor_scalar(src, src, MAGIC, -128.0, ALU.subtract, ALU.max))
                v.tensor_scalar(dst, src, 127.0, None, ALU.min).then_inc(sem_, 1)

            def ffn(b, first):
                tile = lambda t: tile_of(h, 3 * b + t)
                layer_norm(b, (f["var"], f["sd"]), 0, tile, xn, f["xn"])
                dve.wait_ge(f["rms"], b + 1)
                link(v.reciprocal(rms[:, :, 0], rms[:, :, 0]))
                for t in range(NT):
                    link(v.scalar_tensor_tensor(xr[:, t], xn[:, t], rms[:, t, 0:1], g_in[:, :], ALU.mult, ALU.mult))
                    quantize(xr[:, t], xq[:, t], t, 0, f["xq_"])
                for t in range(NT):
                    dve.wait_ge(f["sil"], 3 * b + t + 1)
                    v.scalar_tensor_tensor(yf[:, t], bank[2 * t][0:P, :], back[:, t, 0:1], sil[:, t], ALU.mult, ALU.mult).then_inc(f["y"], 1)
                dve.wait_ge(f["rms2"], b + 1)
                link(v.reciprocal(rms[:, :, 1], rms[:, :, 1]))
                for t in range(NT):
                    link(v.scalar_tensor_tensor(yf[:, t], yf[:, t], rms[:, t, 1:2], g_out[:, :], ALU.mult, ALU.mult))
                    quantize(yf[:, t], yq[:, t], t, 1, f["yq"])
                if not first:
                    dve.wait_ge(f["out"], 16 * b)
                for t in range(NT):
                    dve.wait_ge(f["st"], 3 * b + t + 1)
                    v.scalar_tensor_tensor(fo[:, t], bank[t][0:P, 0:D], back[:, t, 1:2], tile(t), ALU.mult, ALU.add).then_inc(f["o"], 1)
            chain.loop(B, ffn)


def kernel(**inputs):
    import numpy as _np
    import concourse.bacc as _bacc
    from concourse import mybir as _mybir
    from concourse.bass_utils import run_bass_kernel_spmd as _run

    given = {k: _np.asarray(v) for k, v in inputs.items()}
    arrays = {f"c_{k}": v for k, v in shape_constants().items()}
    arrays.update(laid_out(given["x"], given["txt"], given))
    nc = _bacc.Bacc("TRN2", target_bir_lowering=False, num_devices=1)
    dram = {k: nc.dram_tensor(k, v.shape, _mybir.dt.from_np(v.dtype), kind="ExternalInput").ap()
            for k, v in arrays.items()}
    out = nc.dram_tensor("out", (B, L, D), F32, kind="ExternalOutput").ap()
    early_fusion(nc, dram, out)
    return _run(nc, [arrays], core_ids=[0]).results[0]["out"]
```

```python
from contextlib import ExitStack

import numpy as np

import concourse.bass as bass
from concourse import mybir

F32 = mybir.dt.float32
BF16 = mybir.dt.bfloat16
I32 = mybir.dt.int32
ALU = mybir.AluOpType
ACT = mybir.ActivationFunctionType
AX = mybir.AxisListType.X

B, L, D = 8, 333, 192
P, NT = 111, 3
TILES = B * NT
NH, HD = 12, 16
KC = 96
IMG_TOK, TXT = 256, 77
EMB, GP = 64, 16
FEAT = (3, 12, 48)
TOK1, TOK2 = 64, 16
NE, FF = 16, 768
FC = FF // 128
BLK = 128
NB = (2 * B * L - NE) // BLK + NE
MAXB = -(-B * L // BLK)
UNROLL = 3
HID = 512
PAIRS = ((0, 2), (2, 1))
ARENA = 16500
MAGIC = 12582912.0


def shape_constants():
    f = np.float32
    c = {}
    c["ident"] = np.eye(128, dtype=f)
    c["ones"] = np.ones((128, 128), f)
    m = np.arange(P)
    c["tri"] = (m[:, None] <= m[None, :]).astype(f)
    c["tri_strict"] = (m[:, None] < m[None, :]).astype(f)
    pos = np.arange(L, dtype=f)
    inv = f(1.0) / f(10000.0) ** (np.arange(0, HD, 2, dtype=f) / f(HD))
    ang = (pos[:, None] * inv[None, :]).astype(f)
    cos = np.repeat(np.cos(ang), 2, axis=-1).astype(f)
    sin = np.repeat(np.sin(ang), 2, axis=-1).astype(f)
    sin[:, :HD // 2] *= -1
    c["cos"] = cos.reshape(NT, P, HD).transpose(1, 0, 2)
    c["sin"] = sin.reshape(NT, P, HD).transpose(1, 0, 2)
    c["time"] = (pos + 1).reshape(NT, P).T
    for lvl, n in ((1, TOK1), (2, TOK2)):
        at = (np.arange(IMG_TOK, dtype=f) + f(0.5)) * f(n / IMG_TOK) - f(0.5)
        at = np.clip(at, f(0), f(n - 1))
        i0 = np.floor(at).astype(np.int32)
        i1 = np.minimum(i0 + 1, n - 1)
        w = (at - i0).astype(f)
        a = np.zeros((n, IMG_TOK), f)
        np.add.at(a, (i0, np.arange(IMG_TOK)), f(1) - w)
        np.add.at(a, (i1, np.arange(IMG_TOK)), w)
        c[f"interp{lvl}"] = a
    for name, wid in (("head_mask0", 3 * HD), ("head_mask1", HD + 1)):
        c[name] = np.kron(np.eye(4, dtype=f), np.ones((32, wid), f))
    c["iota"] = np.broadcast_to(np.arange(128, dtype=f), (128, 128))
    c["steps"] = np.broadcast_to(BLK * np.arange(MAXB, dtype=f), (P, MAXB))
    c["reset"] = np.broadcast_to(np.tile(np.arange(TILES) > 0, NE), (P, NE * TILES))
    c["token"] = (np.arange(TILES)[None, :] * P + m[:, None])
    return {k: np.ascontiguousarray(v, dtype=f) for k, v in c.items()}


def laid_out(x, txt, w):
    a = {"txt": txt}
    for lvl, p in enumerate((1, 2, 4)):
        g = 64 // p
        t = x.reshape(B, 3, g, p, g, p).transpose(2, 4, 0, 3, 5, 1)
        a[f"patches{lvl}"] = t.reshape(g * g, B * p * p * 3)
        a[f"idx{lvl}"] = w[f"L0_tok_idx{lvl}"]
    a["idx0"] = a["idx0"].reshape(2, 128, GP).transpose(1, 0, 2)
    a["idx1"] = a["idx1"].reshape(TOK1, GP)
    a["idx2"] = a["idx2"].reshape(2, 128).T
    a["tok_w0"] = w["L0_tok_W0"].T
    a["tok_w1"] = w["L0_tok_W1"].T.reshape(2, KC, EMB).transpose(1, 0, 2)
    a["tok_w2"] = w["L0_tok_W2"].T.reshape(GP, 48, EMB).transpose(1, 0, 2)
    a["tok_b"] = np.stack([w[f"L0_tok_b{i}"] for i in range(3)], 1)
    a["tok_wf"] = w["L0_tok_Wf"].T.reshape(3, EMB, D).transpose(1, 0, 2)
    a["tok_bf"] = w["L0_tok_bf"][None, :]

    def chunks(m):
        return m.reshape(2, KC, -1).transpose(1, 0, 2)

    wg = w["L0_attn_Wg"].reshape(NH, 3, D).transpose(1, 0, 2)[:2].reshape(2 * NH, D)
    a["a0_w"] = chunks(np.concatenate(
        [w["L0_attn_Wq"], w["L0_attn_Wk"], w["L0_attn_Wv"], w["L0_attn_Wu"], wg]).T)
    a["a0_wo"] = chunks(w["L0_attn_Wo"].T)
    a["a0_mu"] = w["L0_attn_prior_mu"].reshape(1, D)
    a["a0_tau"] = w["L0_attn_prior_log_tau"].reshape(1, NH)
    a["wr"] = chunks(w["L0_ffn_Wr"].T)
    a["e_w1"] = w["L0_ffn_W1"].reshape(NE, 2, KC, FF).transpose(0, 2, 1, 3)
    a["e_b1"] = w["L0_ffn_b1"][:, None]
    a["e_w2"] = w["L0_ffn_W2"].reshape(NE, FC, 128, D).transpose(0, 2, 1, 3)
    a["e_b2"] = w["L0_ffn_b2"][:, None]

    def with_bias(m, b):
        return chunks(m), b[None, :]

    a["a1_w"], a["a1_b"] = with_bias(w["L1_attn_W_qkv"], w["L1_attn_b_qkv"])
    a["a1_wg"], a["a1_bg"] = with_bias(w["L1_attn_W_gate"], w["L1_attn_b_gate"])
    a["a1_wo"], a["a1_bo"] = with_bias(w["L1_attn_W_proj"], w["L1_attn_b_proj"])
    a["a1_ln"] = np.stack([w["L1_attn_ln_g"], w["L1_attn_ln_b"]], 1).reshape(2, KC, 2).transpose(1, 0, 2)
    a["f_win"] = chunks(w["L1_ffn_w_in"].T)
    a["f_gin"] = w["L1_ffn_g_in"][None, :]
    a["f_wout"] = w["L1_ffn_w_out"].T.reshape(4, 128, D).transpose(1, 0, 2)
    a["f_gout"] = w["L1_ffn_g_out"][None, :]
    return {k: np.ascontiguousarray(v) for k, v in a.items()}


class Chain:

    def __init__(self, eng, sem):
        self.eng, self.sem, self.base, self.per, self.k, self.at = eng, sem, 0, 0, 0, 0

    def turn(self, i):
        self.at = self.base + i * self.per
        self.k = 0

    def step(self, ins):
        ins.then_inc(self.sem, 1)
        self.k += 1
        return self.k

    def wait(self, k):
        self.eng.wait_ge(self.sem, self.at + k)

    def link(self, ins):
        self.wait(self.step(ins))

    def loop(self, n, body):
        self.base += self.k
        self.turn(0)
        body(0, True)
        self.per = self.k
        if n > 1:
            with self.eng.Fori(1, n) as i:
                self.turn(i)
                body(i, False)
        self.base += n * self.per
        self.turn(0)


class Turns(Chain):

    def __init__(self, eng, sem, steps):
        super().__init__(eng, sem)
        self.per = steps

    def turn(self, i):
        assert self.k in (0, self.per), self.k
        super().turn(i)

    def next_phase(self, turns, steps):
        new = Turns(self.eng, self.sem, steps)
        new.base = self.base + turns * self.per
        return new


def need(eng, sem, n):
    if not isinstance(n, int) or n > 0:
        eng.wait_ge(sem, n)


def pipeline(eng, step, ahead):
    def at(k, parity):
        return (k, parity % 2) if not isinstance(k, int) or 0 <= k < B else None

    def whole(k, parity):
        step(*(at(k + d, parity + d) for d in range(ahead, -2, -1)))

    first = 2
    pairs = (B - ahead - first) // 2
    for k in range(-ahead, first):
        whole(k, k % 2)
    with eng.Fori(0, pairs) as i:
        whole(2 * i + first, 0)
        whole(2 * i + first + 1, 1)
    for k in range(2 * pairs + first, B + 1):
        whole(k, k % 2)


def before_batch(j, Bk, C):
    return (Bk if j == 2 else C)[0]


def slot_tiles(j, Bk, C):
    now = (*C, 2) if j == 0 and C else (*Bk, j - 1) if j and Bk else (None, None, None)
    out_tile = (1, 2, 0)[j]
    batch = Bk if j == 2 else C
    return (*now, out_tile, 3 * batch[0] + out_tile if batch else None)


def early_fusion(nc, dram, out):
    with ExitStack() as ctx:
        def sb(name, shape, dt=F32):
            return ctx.enter_context(nc.sbuf_tensor(name, shape, dt))

        def sem(name):
            return ctx.enter_context(nc.semaphore(name))

        bank = [ctx.enter_context(nc.psum_tensor(f"bank{i}", [128, 512], F32)) for i in range(8)]

        arena = sb("arena", [128, ARENA])

        class Taker:
            def __init__(self, at=0):
                self.at = at

            def __call__(self, shape):
                n = int(np.prod(shape[1:]))
                flat = arena[0:shape[0], self.at:self.at + n]
                self.at += n
                assert self.at <= ARENA, self.at
                names = "abcd"[:len(shape) - 1]
                return flat.rearrange(f"p ({' '.join(names)}) -> p {' '.join(names)}",
                                      **{k: v for k, v in zip(names, shape[1:])})

        tok_buf, attn_buf, moe_buf, ffn_buf = Taker(), Taker(), Taker(), Taker()

        h = sb("h", [P, TILES * D])

        def tile_of(buf, n, count=1):
            return buf[:, bass.ds(n * D, count * D)]

        const, plan = {}, {"tok": [], "f": [], "a0": [], "a1": []}

        def load(stage, name, shape, src=None, dt=F32):
            t = sb(f"s_{name}", shape, dt)
            full = t[tuple(slice(None) for _ in shape)]
            plan[stage].append((full, dram[name] if src is None else src))
            return t

        ident = load("tok", "c_ident", [128, 128])
        ones = load("tok", "c_ones", [128, 128])
        plan["tok"].append((h[IMG_TOK - 2 * P:P, :].rearrange("p (b t d) -> p b t d", t=NT, d=D)[:, :, 2, :],
                            dram["txt"].rearrange("b p d -> p b d")))
        idx0 = load("tok", "idx0", [128, 2, GP], dt=I32)
        idx1 = load("tok", "idx1", [TOK1, GP], dt=I32)
        idx2 = load("tok", "idx2", [128, 2], dt=I32)
        w0 = load("tok", "tok_w0", [48, EMB])
        w1 = load("tok", "tok_w1", [KC, 2, EMB])
        w2 = load("tok", "tok_w2", [48, GP, EMB])
        tok_b = load("tok", "tok_b", [EMB, 3])
        wf = load("tok", "tok_wf", [EMB, 3, D])
        bf = load("tok", "tok_bf", [1, D])
        interp1 = load("tok", "c_interp1", [TOK1, IMG_TOK])
        interp2 = load("tok", "c_interp2", [TOK2, IMG_TOK])
        tri = load("a0", "c_tri", [P, P])
        cos = load("a0", "c_cos", [P, NT, HD])
        sin = load("a0", "c_sin", [P, NT, HD])
        time = load("a0", "c_time", [P, NT])
        head_mask0 = load("a0", "c_head_mask0", [128, 12 * HD])
        a0_w = load("a0", "a0_w", [KC, 2, 4 * D + 2 * NH])
        a0_wo = load("a0", "a0_wo", [KC, 2, D])
        mu = load("a0", "a0_mu", [P, D], dram["a0_mu"].to_broadcast([P, D]))
        tau = load("a0", "a0_tau", [P, NH], dram["a0_tau"].to_broadcast([P, NH]))

        wr = load("a0", "wr", [KC, 2, NE])
        tri_strict = load("a0", "c_tri_strict", [P, P])
        iota = load("a0", "c_iota", [P, 128], dram["c_iota"][0:P, :])
        steps = load("a0", "c_steps", [P, MAXB])
        reset = load("a0", "c_reset", [P, NE * TILES])
        token = load("a0", "c_token", [P, TILES])

        def load_biased(stage, name, n, bias):
            t = sb(f"s_{name}", [KC + 1, 2, n])
            plan[stage].append((t[0:KC, :, :], dram[name]))
            plan[stage].append((t[KC:KC + 1, 1, :], dram[bias]))
            return t

        a1_w = load_biased("a1", "a1_w", 3 * D, "a1_b")
        a1_wg = load_biased("a1", "a1_wg", D, "a1_bg")
        a1_wo = load_biased("a1", "a1_wo", D, "a1_bo")
        a1_ln = load("a1", "a1_ln", [KC, 2, 2])
        head_mask1 = load("a1", "c_head_mask1", [128, 4 * (HD + 1)])
        w_in = load("f", "f_win", [KC, 2, 2 * HID])
        w_out = load("f", "f_wout", [128, 4, D])
        g_in = load("f", "f_gin", [P, D], dram["f_gin"].to_broadcast([P, D]))
        g_out = load("f", "f_gout", [P, HID], dram["f_gout"].to_broadcast([P, HID]))

        xn_dram = nc.dram_tensor("xn_dram", (B * L, D), F32, kind="Internal").ap()
        y_dram = nc.dram_tensor("y_dram", (NB * BLK, D), F32, kind="Internal").ap()

        loaded = {k: sem(f"loaded_{k}") for k in plan}
        turns_passed = sem("turns_passed")

        g0 = tok_buf([128, 2, GP, 3 * B])
        g1 = tok_buf([TOK1, GP, 12 * B])
        g2 = tok_buf([128, 2, 48 * B])
        x0 = tok_buf([128, 2, 48])
        x1 = tok_buf([TOK1, 2 * KC])
        x2 = tok_buf([128, 2, 48])
        x02T = tok_buf([48, 512])
        x1T = tok_buf([KC, 2, TOK1])
        y1 = tok_buf([TOK1, EMB])
        y2 = tok_buf([TOK2, EMB])
        catT = tok_buf([EMB, 3, IMG_TOK])
        gathered = sem("gathered")
        tok_staged, tok_xT_ps, tok_xT, tok_y_ps = (sem(n) for n in ("tok_staged", "tok_xT_ps", "tok_xT", "tok_y_ps"))
        tok_y, tok_i_ps, tok_cat, tok_h_ps, h_tok = (sem(n) for n in ("tok_y", "tok_i_ps", "tok_cat", "tok_h_ps", "h_tok"))

        rot1 = attn_buf([P, NT, 2 * D])
        qkT = [attn_buf([128, NT, 6, P]) for _ in range(2)]
        att = attn_buf([P, NH, P])
        a0_buf, a1_buf = Taker(attn_buf.at), Taker(attn_buf.at)
        eps5 = sb("eps5", [128, 1])
        stats = sb("stats", [P, NT, 6])
        mv = sb("mv", [P, NT, 2])
        mv0 = sb("mv0", [P, TILES * 2])
        rs0 = sb("rs0", [P, TILES])
        sd = sb("sd", [P, NT])
        rs = sb("rs", [P, NT])
        xn = sb("xn", [P, NT, D])
        xT = sb("xT", [KC, NT, 2, P])
        vug = [a0_buf([P, NT, 2 * D + 2 * NH]) for _ in range(2)]
        sqh = a0_buf([P, NT, D])
        ge = sb("ge", [P, NT, 2 * NH])
        rot2 = a0_buf([P, NT, 2 * D])
        qk = [sb(f"qk{i}", [P, NT, 2 * NH, 32]) for i in range(2)]
        sq = a0_buf([P, NT, 2 * D])
        n2 = sb("n2", [P, NT * 2 * NH])
        nrm = sb("nrm", [P, NT * 2 * NH])
        rn = sb("rn", [P, NT, 2 * NH])
        ep = sb("ep", [P, NT, 2 * NH])
        es = [sb(f"es{i}", [P, NT, 2 * NH]) for i in range(2)]
        mx = sb("mx", [P, NH])
        m12 = sb("m12", [NH, 1])
        diag = sb("diag", [NH, NH])
        dsm = sb("dsm", [P, NT, NH])
        kc = sb("kc", [P, NT, NH, 3])
        v3 = [a0_buf([P, NT, NH, 3, HD]) for _ in range(2)]
        sg = sb("sg", [P, NT, 2 * NH])
        al = sb("al", [P, NT, NH])
        be = sb("be", [P, NT, NH])
        ga = sb("ga", [P, NT, NH])
        cf = sb("cf", [P, NT, NH, 3])
        stb = a0_buf([128, 3, 12 * HD])
        wo3 = a0_buf([P, NH, 3, HD])
        o3 = sb("o3", [P, NT, D])
        hm = sb("hm", [P, NT * NH])
        hr = sb("hr", [P, NT * NH])
        yT = sb("yT", [KC, NT, 2, P])
        us = sb("us", [P, D])
        it = sb("it", [P, NT])
        rt = sb("rt", [P, NT, NH])
        taumu = sb("taumu", [P, D])
        a0 = {n: sem("a0_" + n) for n in (
            "set tau var sd ep xn xnT xT proj vu ge rot rope sq n2 nrm cum s mx mxT diag mb ds e kc v3 EP  qkT_ps qkT "
            "S att st stb O w hc hsq hvar hsd y yT_ps yT op h").split()}
        lg = sb("lg", [P, TILES, NE])
        cand = sb("cand", [P, TILES, NE])
        red = sb("red", [P, TILES])
        oh = [sb(f"oh{j}", [P, TILES, NE]) for j in range(2)]
        gate = [sb(f"gate{j}", [P, TILES]) for j in range(2)]
        both = sb("both", [P, TILES, NE])
        tot = sb("tot", [P, NE * TILES])
        inc = sb("inc", [P, NE * TILES])
        pos = sb("pos", [P, TILES, NE])
        cmp = sb("cmp", [P, NB * NE])
        nblk = sb("nblk", [P, NE])
        bend = sb("bend", [P, NE])
        basee = sb("basee", [P, NE])
        onee = sb("onee", [P, NE])
        eb = sb("eb", [P, NB])
        eb_i = sb("eb_i", [P, NB], I32)
        slot = sb("slot", [P, TILES, 2])
        slot_i = sb("slot_i", [P, TILES * 2], I32)
        part_i = sb("part_i", [P, TILES * 2], I32)
        s_blk = sb("s_blk", [P, TILES * 2])
        s_row = sb("s_row", [P, TILES * 2])
        row_hot = [sb(f"row_hot{i}", [P, 128]) for i in range(4)]
        blk_hot = [sb(f"blk_hot{i}", [P, NB]) for i in range(4)]
        idx = sb("idx", [128, NB], I32)
        r = {n: sem("r_" + n) for n in "var sd xn xnT xT lg lg_ps out hot ids both rank idx ready  exp".split()}
        idx_now = [sb(f"idx_now{i}", [128, 1], I32) for i in range(UNROLL)]
        x_blk = [moe_buf([128, D]) for i in range(UNROLL)]
        e_w1 = [moe_buf([KC + 1, 2, FF]) for i in range(UNROLL)]
        e_w2 = [moe_buf([128, FC, D]) for i in range(UNROLL)]
        e_b2 = [moe_buf([1, D]) for i in range(UNROLL)]
        xgT = moe_buf([KC + 1, 2, BLK])
        hT = [moe_buf([128, FC, BLK]) for i in range(UNROLL)]
        yb = [moe_buf([128, D]) for i in range(UNROLL)]
        m_x = [sem(f"m_x{i}") for i in range(UNROLL)]
        m_w = [sem(f"m_w{i}") for i in range(UNROLL)]
        m_out = [sem(f"m_out{i}") for i in range(UNROLL)]
        m = {n: sem("m_" + n) for n in "xgT_ps xgT hid hT y_ps y".split()}
        slot_now = sb("slot_now", [P, 2 * NT], I32)
        yg = a1_buf([P, NT, 2, D])
        xz = [a1_buf([P, NT, 2, D]) for _ in range(2)]
        xzT = a1_buf([KC + 1, NT, 4, P])
        v1 = [a1_buf([P, NT, NH, HD + 1]) for _ in range(2)]
        ge1 = a1_buf([P, NT, D])
        kg = a1_buf([P, NT, D])
        relu = a1_buf([P, NT, 2 * D])
        st1 = sb("st1", [128, 3, 4 * (HD + 1)])
        den = sb("den", [P, NH])
        y1T = sb("y1T", [KC + 1, NT, 2, P])
        a1 = {n: sem("a1_" + n) for n in (
            "ones yg cmb var sd xn zn xzT_ps xzT proj v ge eq kg ek q_ft k_ft qkT_ps qkT S att st stb O w yT_ps yT op h").split()}
        w_in_q = sb("w_in_q", [KC, 2, 2 * HID], BF16)
        w_out_q = sb("w_out_q", [128, 4, D], BF16)
        identb = sb("identb", [128, 128], BF16)
        eps6 = sb("eps6", [128, 1])
        wsum = sb("wsum", [128, 2])
        wscale = sb("wscale", [128, 2])
        wback = sb("wback", [128, 2])
        ssq = sb("ssq", [P, 2, NT])
        rms = sb("rms", [P, 2, NT])
        amax = sb("amax", [P, 2, NT])
        top = sb("top", [P, 2, NT])
        qs = sb("qs", [P, 2, NT])
        back = sb("back", [P, 2, NT])
        xg = [ffn_buf([P, NT, D]) for _ in range(2)]
        xs = ffn_buf([P, NT, D])
        xq = sb("xq", [P, NT, D], BF16)
        xqT = sb("xqT", [KC, NT, 2, P], BF16)
        sil = ffn_buf([P, NT, HID])
        yf = ffn_buf([P, NT, HID])
        yg2 = [ffn_buf([P, NT, HID]) for _ in range(2)]
        ys = ffn_buf([P, NT, HID])
        sqx = ffn_buf([P, NT, D])
        sqy = ffn_buf([P, NT, HID])
        yq = sb("yq", [P, NT, HID], BF16)
        yqT = sb("yqT", [128, NT, 4, P], BF16)
        fo = ffn_buf([P, NT, D])
        f = {n: sem("f_" + n) for n in (
            "wsum wbc wq var sd rs xn xg sq rms ax sc xs x1 xq_ xqT_ps xqT gu sil y z sq2 rms2 ys y1 yq yqT_ps yqT st o out").split()}
        dve_chain, pool_chain = sem("dve_chain"), sem("pool_chain")
        dve_turns = [sem(f"dve_turns{i}") for i in range(3)]

        def bf16_tiles(i, n):
            return bank[i][:, :].bitcast(BF16)[:, 0:n * (P + 1)].rearrange("p (a l) -> p a l", a=n)

        block = ctx.enter_context(nc.Block())

        def all_loaded(eng, stage):
            eng.wait_ge(loaded[stage], 16 * len(plan[stage]))

        def stand_alone(eng):
            eng.sem_inc(turns_passed, 1)

        @block.sync
        def _(sp):
            for stage in plan:
                for dst, src in plan[stage]:
                    sp.dma_start(dst, src).then_inc(loaded[stage], 16)
            def route(b, first):
              sp.wait_ge(r["xn"], 3 * b + 3)
              sp.dma_start(xn_dram[bass.ds(b * L, L), :].rearrange("(t p) d -> p t d", p=P),
                           xn[:, :, :]).then_inc(r["out"], 16)
            Chain(sp, None).loop(B, route)

            sp.wait_ge(r["exp"], 1)

            def store(n, s):
              sp.dma_start(y_dram[bass.ds(n * BLK, BLK), :], yb[s][:, :]).then_inc(m_out[s], 16)

            def blocks(i, first):
              for s in range(UNROLL):
                  n = UNROLL * i + s
                  if not first:
                      sp.wait_ge(m["y"], n - UNROLL + 1)
                      store(n - UNROLL, s)
                  e = sp.value_load(eb_i[0:1, bass.ds(n, 1)], min_val=0, max_val=NE - 1)
                  sp.dma_start(e_w1[s][0:KC, :, :], dram["e_w1"][bass.ds(e, 1)].rearrange("e p k f -> (e p) k f")).then_inc(m_w[s], 16)
                  sp.dma_start(e_w1[s][KC:KC + 1, 1, :], dram["e_b1"][bass.ds(e, 1)].rearrange("e p f -> (e p) f")).then_inc(m_w[s], 16)
                  sp.dma_start(e_w2[s][:, :, :], dram["e_w2"][bass.ds(e, 1)].rearrange("e p k f -> (e p) k f")).then_inc(m_w[s], 16)
                  sp.dma_start(e_b2[s][:, :], dram["e_b2"][bass.ds(e, 1)].rearrange("e p f -> (e p) f")).then_inc(m_w[s], 16)
            Chain(sp, None).loop(NB // UNROLL, blocks)
            for s in range(UNROLL):
              sp.wait_ge(m["y"], NB - UNROLL + s + 1)
              store(NB - UNROLL + s, s)
            def ffn(b, first):
              sp.wait_ge(f["o"], 3 * b + 3)
              sp.dma_start(out[bass.ds(b, 1)].rearrange("b (t p) d -> p (b t) d", p=P), fo[:, :, :]).then_inc(f["out"], 16)
            Chain(sp, None).loop(B, ffn)
            sp.wait_ge(f["out"], 16 * B)

        @block.gpsimd
        def _(pool):
            all_loaded(pool, "tok")
            for half in range(2):
                for j in range(GP):
                    pool.indirect_dma_start(g0[:, half, j, :], None, dram["patches0"],
                                            bass.IndirectOffsetOnAxis(ap=idx0[:, half, j:j + 1], axis=0)
                                            ).then_inc(gathered, 16)
                pool.indirect_dma_start(g2[:, half, :], None, dram["patches2"],
                                        bass.IndirectOffsetOnAxis(ap=idx2[:, half:half + 1], axis=0)
                                        ).then_inc(gathered, 16)
            for j in range(GP):
                pool.indirect_dma_start(g1[:, j, :], None, dram["patches1"],
                                        bass.IndirectOffsetOnAxis(ap=idx1[:, j:j + 1], axis=0)
                                        ).then_inc(gathered, 16)

            def attn0(A, Bk, C):
                if Bk:
                    b, par = Bk
                    for t in range(NT):
                        if t == 0:
                            pool.wait_ge(a0["kc"], b + 1)
                            need(pool, a0["O"], 3 * b - 3)
                        v = vug[par][:, t, 0:D].rearrange("p (h a d) -> p h a d", h=NH, a=1)
                        nc.gpsimd.tensor_tensor(v3[par][:, t], v.to_broadcast([P, NH, 3, HD]),
                                                kc[:, t].rearrange("p h (c a) -> p h c a", a=1).to_broadcast([P, NH, 3, HD]),
                                                ALU.mult).then_inc(a0["v3"], 1)
                        if A and t == 0:
                            rope(A, 0)
                if A:
                    if not Bk:
                        rope(A, 0)
                    rope(A, 1)
                    rope(A, 2)

            def rope(A, t):
                a, par = A
                pool.wait_ge(a0["rot"], 3 * a + t + 1)
                if t == 0:
                    need(pool, a0["st"], 2 * a - 2)
                    need(pool, a0["sq"], 3 * a - 3)
                nc.gpsimd.tensor_tensor(qk[par][:, t, :, 0:HD], rot1[:, t].rearrange("p (h d) -> p h d", d=HD),
                                        rot2[:, t].rearrange("p (h d) -> p h d", d=HD), ALU.add).then_inc(a0["rope"], 1)
            pipeline(pool, attn0, 1)
            chain = Chain(pool, pool_chain)
            pool.wait_ge(r["idx"], 1)
            pool.wait_ge(r["out"], 16 * B)

            def blocks(i, first):
                for s in range(UNROLL):
                    n = UNROLL * i + s
                    if not first:
                        pool.wait_ge(m["xgT_ps"], n - UNROLL + 1)
                    chain.link(nc.gpsimd.tensor_copy(idx_now[s][:, :], idx[:, bass.ds(n, 1)]))
                    stand_alone(pool)
                    pool.indirect_dma_start(x_blk[s][:, :], None, xn_dram,
                                            bass.IndirectOffsetOnAxis(ap=idx_now[s][:, :], axis=0)).then_inc(m_x[s], 16)
            chain.loop(NB // UNROLL, blocks)
            for s in range(UNROLL):
                pool.wait_ge(m_out[s], 16 * (NB // UNROLL))

            def rows(b, first):
                if not first:
                    pool.wait_ge(a1["yg"], 16 * 6 * b)
                    pool.wait_ge(a1["cmb"], b)
                chain.link(nc.gpsimd.tensor_copy(slot_now[:, :], slot_i[:, bass.ds(b * 2 * NT, 2 * NT)]))
                stand_alone(pool)
                for t in range(NT):
                    for j in range(2):
                        pool.indirect_dma_start(yg[:, t, j, :], None, y_dram, bass.IndirectOffsetOnAxis(
                            ap=slot_now[:, 2 * t + j:2 * t + j + 1], axis=0)).then_inc(a1["yg"], 16)
            chain.loop(B, rows)

            def ffn(Z, A, Bk, C):
                for t in range(NT):
                    if A:
                        a, pa = A
                        pool.wait_ge(f["xn"], 3 * a + t + 1)
                        need(pool, f["xs"], 3 * a + t - 5)
                        nc.gpsimd.tensor_tensor(xg[pa][:, t], xn[:, t], g_in[:, :], ALU.mult).then_inc(f["xg"], 1)
                for t in range(NT):
                    if Bk:
                        b, par = Bk
                        pool.wait_ge(f["y"], 3 * b + t + 1)
                        need(pool, f["ys"], 3 * b + t - 5)
                        nc.gpsimd.tensor_tensor(yg2[par][:, t], yf[:, t], g_out[:, :], ALU.mult).then_inc(f["z"], 1)
            pipeline(pool, ffn, 2)

        @block.scalar
        def _(act):
            chain = Chain(act, None)
            all_loaded(act, "tok")

            def tok(b, first):
                act.wait_ge(tok_xT_ps, b + 1)
                nc.scalar.copy(x02T[:, :], bank[0][0:48, :]).then_inc(tok_xT, 1)
                nc.scalar.copy(x1T[:, :, :].rearrange("p a t -> p (a t)"), bank[1][0:KC, 0:128]).then_inc(tok_xT, 1)
                act.wait_ge(tok_y_ps, b + 1)
                nc.scalar.copy(y1[:, :], bank[3][0:TOK1, 0:EMB]).then_inc(tok_y, 1)
                nc.scalar.copy(y2[:, :], bank[3][0:TOK2, EMB:2 * EMB]).then_inc(tok_y, 1)
                nc.scalar.activation(catT[:, 0, :], bank[2][0:EMB, 0:IMG_TOK], ACT.Identity,
                                     bias=tok_b[:, 0:1]).then_inc(tok_cat, 1)
                act.wait_ge(tok_i_ps, b + 1)
                for lvl in (1, 2):
                    nc.scalar.activation(catT[:, lvl, :], bank[4][0:EMB, (lvl - 1) * 256:lvl * 256], ACT.Identity,
                                         bias=tok_b[:, lvl:lvl + 1]).then_inc(tok_cat, 1)
            chain.loop(B, tok)

            all_loaded(act, "a0")
            act.wait_ge(a0["set"], 1)
            nc.scalar.activation(tau[:, :], tau[:, :], ACT.Exp).then_inc(a0["tau"], 1)

            act.wait_ge(a0["var"], 1)
            nc.scalar.activation(rs0[:, :], mv0[:, :].rearrange("p (n c) -> p n c", c=2)[:, :, 1], ACT.Sqrt, bias=eps5[0:P, 0:1]).then_inc(a0["sd"], 1)

            def attn0(A, Bk, C):
                a, pa = A or (None, None)
                b, par = Bk or (None, None)
                c, _ = C or (None, None)

                def x_T(t):
                    act.wait_ge(a0["xnT"], 3 * a + t + 1)
                    need(act, a0["proj"], 3 * a + t - 2)
                    nc.scalar.copy(xT[:, t].rearrange("p a l -> p (a l)"), bank[6][0:KC, 0:2 * P]).then_inc(a0["xT"], 1)

                def vu(t):
                    act.wait_ge(a0["proj"], 3 * a + t + 1)
                    need(act, a0["v3"], 3 * a - 3)
                    nc.scalar.copy(vug[pa][:, t], bank[5][0:P, 0:2 * D + 2 * NH]).then_inc(a0["vu"], 1)

                def squares(t):
                    act.wait_ge(a0["rope"], 3 * a + t + 1)
                    if t == 0:
                        need(act, a0["n2"], a)
                    nc.scalar.activation(sq[:, t].rearrange("p (h d) -> p h d", d=HD), qk[pa][:, t, :, 0:HD],
                                         ACT.Square).then_inc(a0["sq"], 1)

                def heads_T(k, par_, t, j):
                    act.wait_ge(a0["qkT_ps"], 6 * k + 2 * t + j + 1)
                    need(act, a0["O"], 3 * k + t - 5)
                    nc.scalar.copy(qkT[par_][:, t, 3 * j:3 * j + 3].rearrange("p a t -> p (a t)"),
                                   bank[7][:, 0:333]).then_inc(a0["qkT"], 1)

                if A:
                    x_T(0)
                if Bk:
                    heads_T(b, par, 2, 1)
                if Bk:
                    act.wait_ge(a0["n2"], b + 1)
                    nc.scalar.activation(nrm[:, :], n2[:, :], ACT.Sqrt).then_inc(a0["nrm"], 1)
                    act.wait_ge(a0["ds"], b + 1)
                    nc.scalar.activation(es[par][:, :, 0:NH], dsm[:, :, :], ACT.Exp).then_inc(a0["e"], 1)
                    nc.scalar.activation(ge[:, :, :], vug[par][:, :, 2 * D:2 * D + 2 * NH], ACT.Exp, scale=-1.0).then_inc(a0["ge"], 1)
                if A:
                    vu(0)
                    squares(0)
                    heads_T(a, pa, 0, 0)
                    x_T(1)
                    heads_T(a, pa, 0, 1)
                    vu(1)
                if C:
                    act.wait_ge(a0["hc"], c + 1)
                    nc.scalar.activation(sqh[:, :, :], o3[:, :, :], ACT.Square).then_inc(a0["hsq"], 1)
                if A:
                    squares(1)
                if C:
                    act.wait_ge(a0["hvar"], c + 1)
                    nc.scalar.activation(hr[:, :], hr[:, :], ACT.Sqrt, bias=eps5[0:P, 0:1], scale=1.0 / HD).then_inc(a0["hsd"], 1)
                if A:
                    heads_T(a, pa, 1, 0)
                    x_T(2)
                    heads_T(a, pa, 1, 1)
                if C:
                    for j, (lo, n) in enumerate(PAIRS):
                        act.wait_ge(a0["yT_ps"], 2 * c + j + 1)
                        if j == 0:
                            need(act, a0["op"], 2 * c)
                        nc.scalar.copy(yT[:, lo:lo + n].rearrange("p t a l -> p (t a l)"),
                                       bank[2 + j][0:KC, 0:2 * P * n]).then_inc(a0["yT"], 1)
                if A:
                    vu(2)
                    squares(2)
                    heads_T(a, pa, 2, 0)
            pipeline(act, attn0, 1)

            def ln_sd(sems, b, dst, src, eps):
                act.wait_ge(sems[0], b + 1)
                nc.scalar.activation(dst, src, ACT.Sqrt, bias=eps[0:P, 0:1]).then_inc(sems[1], 1)

            def route(b, first):
                ln_sd((r["var"], r["sd"]), b, sd[:, :], mv[:, :, 1], eps5)
                for j, (lo, n) in enumerate(PAIRS):
                    act.wait_ge(r["xnT"], 2 * b + j + 1)
                    nc.scalar.copy(xT[:, lo:lo + n].rearrange("p t a l -> p (t a l)"),
                                   bank[6 + j][0:KC, 0:2 * P * n]).then_inc(r["xT"], 1)
            chain.loop(B, route)
            act.wait_ge(r["lg"], B + 1)
            nc.scalar.activation(lg[:, :, :], lg[:, :, :], ACT.Exp).then_inc(r["ready"], 1)

            def hidden(i, first):
                for s in range(UNROLL):
                    n = UNROLL * i + s
                    if not first:
                        act.wait_ge(m["y_ps"], n - UNROLL + 1)
                    for j in range(2):
                        act.wait_ge(m["hid"], 2 * n + j + 1)
                        nc.scalar.activation(hT[s][:, 3 * j:3 * j + 3, :].rearrange("p c t -> p (c t)"),
                                             bank[2 * s + j][:, 0:384], ACT.Gelu).then_inc(m["hT"], 1)
            chain.loop(NB // UNROLL, hidden)
            all_loaded(act, "a1")

            def attn1(Z, A, Bk, C):
                a, pa = A or (None, None)
                z, _ = Z or (None, None)

                def heads_T(k, par, t, j):
                    act.wait_ge(a1["qkT_ps"], 6 * k + 2 * t + j + 1)
                    need(act, a1["O"], 3 * k + t - 5)
                    nc.scalar.copy(qkT[par][:, t, 3 * j:3 * j + 3].rearrange("p a t -> p (a t)"),
                                   bank[7][:, 0:333]).then_inc(a1["qkT"], 1)

                def relu_exp(src, t, lo, sem_, used):
                    need(act, used, 3 * a + t - 2)
                    nc.scalar.activation(relu[:, t, lo:lo + D], src, ACT.Relu).then_inc(sem_, 1)
                    nc.scalar.activation(rot1[:, t, lo:lo + D], src, ACT.Exp).then_inc(sem_, 1)

                for j in range(NT):
                    n, par, t, out_tile, done = slot_tiles(j, Bk, C)
                    if A:
                        act.wait_ge(a1["xzT_ps"], 3 * a + j + 1)
                        need(act, a1["proj"], 6 * a + 2 * j - 4)
                        nc.scalar.copy(xzT[0:KC, j, 0:2].rearrange("p a l -> p (a l)"), bank[6][0:KC, 0:2 * P]).then_inc(a1["xzT"], 1)
                        for k in range(2):
                            nc.scalar.activation(xzT[0:KC, j, 2 + k], bank[6][0:KC, P * (2 + k):P * (3 + k)], ACT.Identity,
                                                 scale=a1_ln[:, k, 0:1], bias=a1_ln[:, k, 1:2]).then_inc(a1["xzT"], 1)
                    if j == 0 and Bk:
                        heads_T(*Bk, 2, 1)
                    if j and A:
                        heads_T(a, pa, j - 1, 1)
                    if done is not None:
                        act.wait_ge(a1["yT_ps"], done + 1)
                        need(act, a1["op"], done - 2)
                        nc.scalar.copy(y1T[0:KC, out_tile].rearrange("p a l -> p (a l)"), bank[6][0:KC, 0:2 * P]).then_inc(a1["yT"], 1)
                    if A:
                        act.wait_ge(a1["proj"], 6 * a + 2 * j + 1)
                        relu_exp(bank[4][0:P, 0:D], j, 0, a1["eq"], a1["q_ft"])
                        act.wait_ge(a1["proj"], 6 * a + 2 * j + 2)
                        need(act, a1["kg"], 3 * a + j - 2)
                        nc.scalar.activation(ge1[:, j], bank[5][0:P, D:2 * D], ACT.Exp, scale=-1.0).then_inc(a1["ge"], 1)
                        need(act, a1["O"], 3 * a + j - 5)
                        need(act, a1["st"], 2 * a - 2)
                        nc.scalar.copy(v1[pa][:, j, :, 0:HD], bank[5][0:P, 0:D].rearrange("p (h d) -> p h d", d=HD)).then_inc(a1["v"], 1)
                        act.wait_ge(a1["kg"], 3 * a + j + 1)
                        relu_exp(kg[:, j], j, D, a1["ek"], a1["k_ft"])
                    if Z and j == 0:
                        ln_sd((a1["var"], a1["sd"]), 2 * z, sd[:, :], mv[:, :, 1], eps5)
                    if Z and j == 1:
                        ln_sd((a1["var"], a1["sd"]), 2 * z + 1, sd[:, :], mv[:, :, 1], eps5)
                    if A:
                        heads_T(a, pa, j, 0)
            pipeline(act, attn1, 2)

            def ffn(Z, A, Bk, C):
                a, pa = A or (None, None)
                b, par = Bk or (None, None)
                c, pc = C or (None, None)
                if A:
                    ln_sd((f["var"], f["sd"]), a, sd[:, :], mv[:, :, 1], eps5)
                if Bk:
                    act.wait_ge(f["sq"], 3 * b + 3)
                    need(act, f["sc"], b)
                    nc.scalar.activation(rms[:, 0, :], ssq[:, 0, :], ACT.Sqrt, bias=eps6[0:P, 0:1], scale=1.0 / D).then_inc(f["rms"], 1)
                if C:
                    act.wait_ge(f["sq2"], 3 * c + 3)
                    act.wait_ge(f["sc"], c + 1)
                    nc.scalar.activation(rms[:, 1, :], ssq[:, 1, :], ACT.Sqrt, bias=eps6[0:P, 0:1], scale=1.0 / HID).then_inc(f["rms2"], 1)
                act.wait_ge(f["sc"], (b if Bk else c + 1) + 1) if Bk or C else None
                for t in range(NT):
                    if Bk:
                        need(act, f["xq_"], 3 * b + t - 2)
                        nc.scalar.activation(xs[:, t], xg[par][:, t], ACT.Copy, scale=qs[:, 0, t:t + 1]).then_inc(f["xs"], 1)
                    if C:
                        need(act, f["yq"], 3 * c + t - 2)
                        nc.scalar.activation(ys[:, t], yg2[pc][:, t], ACT.Copy, scale=qs[:, 1, t:t + 1]).then_inc(f["ys"], 1)
                    if Bk and t:
                        x_T(b, t - 1)
                if Bk:
                    x_T(b, 2)
                for t in range(NT):
                    if Bk:
                        act.wait_ge(f["gu"], 3 * b + t + 1)
                        need(act, f["y"], 3 * b + t - 2)
                        nc.scalar.activation(sil[:, t], bank[2 * (t % 2) + 1][0:P, :], ACT.Silu, scale=back[:, 0, t:t + 1]).then_inc(f["sil"], 1)
                    if C:
                        act.wait_ge(f["yqT_ps"], 3 * c + t + 1)
                        need(act, f["st"], 3 * c + t - 2)
                        nc.scalar.copy(yqT[:, t], bf16_tiles(7 if t % 2 == 0 else 5, 4)[:, :, 0:P]).then_inc(f["yqT"], 1)
                for t in range(NT):
                    if A:
                        act.wait_ge(f["xn"], 3 * a + t + 1)
                        nc.scalar.activation(sqx[:, t], xn[:, t], ACT.Square, accum_out=ssq[:, 0, t:t + 1]).then_inc(f["sq"], 1)
                for t in range(NT):
                    if Bk:
                        act.wait_ge(f["y"], 3 * b + t + 1)
                        nc.scalar.activation(sqy[:, t], yf[:, t], ACT.Square, accum_out=ssq[:, 1, t:t + 1]).then_inc(f["sq2"], 1)

            def x_T(b, t):
                act.wait_ge(f["xqT_ps"], 3 * b + t + 1)
                need(act, f["gu"], 3 * b + t - 2)
                nc.scalar.copy(xqT[:, t], bf16_tiles(6, 2)[0:KC, :, 0:P]).then_inc(f["xqT"], 1)
            pipeline(act, ffn, 2)

        @block.tensor
        def _(pe):
            mm = nc.tensor.matmul
            pe.wait_ge(f["wsum"], 2)
            all_loaded(pe, "tok")
            mm(bank[0][:, 0:1], ones[0:KC, :], wsum[0:KC, 0:1], start=True, stop=True)
            mm(bank[0][:, 1:2], ones[:, :], wsum[:, 1:2], start=True, stop=True).then_inc(f["wbc"], 1)
            pe.wait_ge(f["wq"], 1)
            all_loaded(pe, "tok")

            def tok(b, first):
                pe.wait_ge(tok_staged, 3 * b + 3)
                if not first:
                    pe.wait_ge(tok_xT, 2 * b)
                    stand_alone(pe)
                for half in range(2):
                    nc.tensor.transpose(bank[0][0:48, 128 * half:128 * half + 128], x0[:, half, :], ident[:, :])
                    nc.tensor.transpose(bank[0][0:48, 256 + 128 * half:384 + 128 * half], x2[:, half, :], ident[:, :])
                for k in range(2):
                    last = nc.tensor.transpose(bank[1][0:KC, TOK1 * k:TOK1 * k + TOK1], x1[:, KC * k:KC * k + KC],
                                               ident[0:TOK1, 0:TOK1])
                last.then_inc(tok_xT_ps, 1)
                pe.wait_ge(tok_xT, 2 * b + 2)
                if not first:
                    pe.wait_ge(tok_cat, 3 * b)
                    stand_alone(pe)
                mm(bank[2][0:EMB, 0:IMG_TOK], w0[:, :], x02T[:, 0:256], start=True, stop=True)
                for k in range(2):
                    mm(bank[3][0:TOK1, 0:EMB], x1T[:, k, :], w1[:, k, :], start=(k == 0), stop=(k == 1))
                x2v = x02T[:, 256:512].rearrange("p (t j) -> p t j", j=GP)
                for j in range(GP):
                    last = mm(bank[3][0:TOK2, EMB:2 * EMB], x2v[:, :, j], w2[:, j, :], start=(j == 0), stop=(j == GP - 1))
                last.then_inc(tok_y_ps, 1)
                pe.wait_ge(tok_y, 2 * b + 2)
                stand_alone(pe)
                mm(bank[4][0:EMB, 0:256], y1[:, :], interp1[:, :], start=True, stop=True)
                mm(bank[4][0:EMB, 256:512], y2[:, :], interp2[:, :], start=True, stop=True).then_inc(tok_i_ps, 1)
                pe.wait_ge(tok_cat, 3 * b + 3)
                if not first:
                    pe.wait_ge(h_tok, 2 * b)
                    stand_alone(pe)
                for t in range(NT):
                    n = P if t < 2 else IMG_TOK - 2 * P
                    dst = bank[5][0:P, D * t:D * t + D] if t < 2 else bank[6][0:n, 0:D]
                    for c in range(3):
                        mm(dst, catT[:, c, P * t:P * t + n], wf[:, c, :], start=(c == 0), stop=False)
                    last = mm(dst, ones[0:1, 0:n], bf[:, :], start=False, stop=True)
                last.then_inc(tok_h_ps, 1)
            chain = Chain(pe, None)
            chain.loop(B, tok)

            all_loaded(pe, "a0")
            pe.wait_ge(a0["tau"], 3)
            pe.wait_ge(h_tok, 2 * B)

            def scores(sems, b, par, t, lo, hi):
                for i in range(lo, hi):
                    if i >= 2:
                        pe.wait_ge(sems["att"], 12 * b + 4 * t + i - 1)
                    for g in range(3):
                        last = mm(bank[i % 2][0:P, P * g:P * g + P], qkT[par][32 * i:32 * i + 32, t, 3 + g, :],
                                  qkT[par][32 * i:32 * i + 32, t, g, :], start=True, stop=True, tile_position=(32 * i, 0))
                    last.then_inc(sems["S"], 1)

            def heads_T(sems, a, pa, t, j):
                if j == 0:
                    need(pe, sems["qkT"], 6 * a + 2 * t)
                else:
                    pe.wait_ge(sems["qkT"], 6 * a + 2 * t + 1)
                for g in range(3):
                    last = nc.tensor.transpose(bank[7][:, P * g:P * g + P],
                                               qk[pa][:, t, NH * j + 4 * g:NH * j + 4 * g + 4].rearrange("p h d -> p (h d)"),
                                               ident[0:P, 0:P])
                last.then_inc(sems["qkT_ps"], 1)

            def pair_transposes(src, done, first_bank):
                for t in range(NT):
                    for k in range(2):
                        dst = bank[first_bank + t // 2][0:KC, 2 * P * (t % 2) + P * k:2 * P * (t % 2) + P * k + P]
                        last = nc.tensor.transpose(dst, src[:, t, KC * k:KC * k + KC], ident[0:P, 0:P])
                    if t:
                        last.then_inc(done, 1)

            def attn0(A, Bk, C):
                a, pa = A or (None, None)
                b, par = Bk or (None, None)
                c, pc = C or (None, None)

                def tile_T(t):
                    pe.wait_ge(a0["xn"], 3 * a + t + 1)
                    need(pe, a0["s"], 3 * a + t)
                    for k in range(2):
                        last = nc.tensor.transpose(bank[6][0:KC, P * k:P * k + P], xn[:, t, KC * k:KC * k + KC], ident[0:P, 0:P])
                    last.then_inc(a0["xnT"], 1)

                def proj(t, j):
                    if j == 0:
                        pe.wait_ge(a0["xT"], 3 * a + t + 1)
                        need(pe, a0["rot"], 3 * a + t)
                    else:
                        need(pe, a0["vu"], 3 * a + t)
                    lo, n = ((0, 384), (384, 408))[j]
                    for k in range(2):
                        last = mm(bank[4 + j][0:P, 0:n], xT[:, t, k, :], a0_w[:, k, lo:lo + n], start=(k == 0), stop=(k == 1))
                    if j:
                        last.then_inc(a0["proj"], 1)

                def cum(t):
                    pe.wait_ge(a0["vu"], 3 * a + t + 1)
                    mm(bank[6][0:P, 0:D], ones[0:1, 0:P], taumu[0:1, :], start=True, stop=False)
                    for s in range(t):
                        mm(bank[6][0:P, 0:D], ones[0:P, 0:P], vug[pa][:, s, D:2 * D], start=False, stop=False)
                    mm(bank[6][0:P, 0:D], tri[:, :], vug[pa][:, t, D:2 * D], start=False, stop=True).then_inc(a0["cum"], 1)

                def q_T(t):
                    pe.wait_ge(a0["rope"], 3 * a + t + 1)
                    if t == 0:
                        need(pe, a0["ep"], a)
                    heads_T(a0, a, pa, t, 0)

                def chunk(b, par, t):
                    need(pe, a0["w"], 3 * b + t)
                    pe.wait_ge(a0["v3"], 3 * b + t + 1)
                    if t == 1:
                        need(pe, a0["h"], 2 * b)
                    for g in range(3):
                        if t:
                            mm(bank[2 + g // 2][0:P, 192 * (g % 2):192 * (g % 2) + 192], qkT[par][:, t, g, :], stb[:, g, :],
                               start=(g != 1), stop=False, skip_group_check=True)
                    for i in range(4):
                        pe.wait_ge(a0["att"], 12 * b + 4 * t + i + 1)
                        for g in range(3):
                            at = 192 * (g % 2) + 48 * i
                            last = mm(bank[2 + g // 2][0:P, at:at + 48], att[:, 4 * g + i, :],
                                      v3[par][:, t, 4 * g + i].rearrange("p c d -> p (c d)"),
                                      start=(t == 0 and i == 0 and g != 1), stop=True, skip_group_check=True)
                    last.then_inc(a0["O"], 1)
                    if t < 2:
                        for g in range(3):
                            for s in range(t + 1):
                                last = mm(bank[g // 2][:, 192 * (g % 2):192 * (g % 2) + 192],
                                          qk[par][:, s, NH + 4 * g:NH + 4 * g + 4].rearrange("p h d -> p (h d)"),
                                          v3[par][:, s, 4 * g:4 * g + 4].rearrange("p h c d -> p (h c d)"),
                                          start=(s == 0), stop=(s == t))
                        last.then_inc(a0["st"], 1)

                for j in range(NT):
                    n, q, t = (c, pc, 2) if j == 0 else (b, par, j - 1)
                    if A:
                        tile_T(j)
                    if j == 0 and Bk:
                        heads_T(a0, b, par, 2, 1)
                    if j and A:
                        heads_T(a0, a, pa, j - 1, 1)
                    if n is not None:
                        if t:
                            pe.wait_ge(a0["stb"], 2 * n + t)
                        else:
                            need(pe, a0["att"], 12 * n)
                            pe.wait_ge(a0["qkT"], 6 * n + 6)
                        scores(a0, n, q, t, 0, 2)
                    if j == 0 and Bk:
                        pe.wait_ge(a0["mx"], b + 1)
                        pe.wait_ge(a0["qkT"], 6 * b + 6)
                        nc.tensor.transpose(bank[7][0:NH, 192:192 + P], mx[:, :], ident[0:P, 0:P]).then_inc(a0["mxT"], 1)
                    if A:
                        proj(j, 0)
                    if j == 2 and C:
                        pe.wait_ge(a0["y"], c + 1)
                        pe.wait_ge(a0["w"], 3 * c + (4 if Bk else 3))
                        pair_transposes(o3, a0["yT_ps"], 2)
                    if j == 0 and Bk:
                        pe.wait_ge(a0["diag"], b + 1)
                        mm(bank[7][0:P, 320:332], ones[0:NH, 0:P], diag[:, :], start=True, stop=True).then_inc(a0["mb"], 1)
                    if A:
                        proj(j, 1)
                    if n is not None:
                        scores(a0, n, q, t, 2, 4)
                    if j == 2 and C:
                        for t2 in range(NT):
                            if t2 != 1:
                                pe.wait_ge(a0["yT"], 2 * c + (1 if t2 == 0 else 2))
                            for k in range(2):
                                last = mm(bank[2 + t2 // 2][0:P, D * (t2 % 2):D * (t2 % 2) + D], yT[:, t2, k, :], a0_wo[:, k, :],
                                          start=(k == 0), stop=(k == 1))
                            if t2:
                                last.then_inc(a0["op"], 1)
                    if A:
                        cum(j)
                    if n is not None:
                        chunk(n, q, t)
                    if j == 0 and Bk:
                        pe.wait_ge(a0["e"], b + 1)
                        for t2 in range(NT):
                            dst = bank[7][0:P, 336 + 24 * t2:360 + 24 * t2]
                            for s in range(t2):
                                mm(dst, ones[0:P, 0:P], es[par][:, s, :], start=(s == 0), stop=False)
                            last = mm(dst, tri[:, :], es[par][:, t2, :], start=(t2 == 0), stop=True)
                        last.then_inc(a0["EP"], 1)
                    if A:
                        q_T(j)
            pipeline(pe, attn0, 1)

            pe.wait_ge(a0["yT"], 2 * B)
            pe.wait_ge(a0["h"], 2 * B)

            def route(b, first):
                if not first:
                    pe.wait_ge(r["xT"], 2 * b)
                    pe.wait_ge(r["lg"], b)
                pe.wait_ge(r["xn"], 3 * b + 3)
                pair_transposes(xn, r["xnT"], 6)
                for t in range(NT):
                    pe.wait_ge(r["xT"], 2 * b + t // 2 + 1)
                    for k in range(2):
                        last = mm(bank[0][0:P, NE * t:NE * t + NE], xT[:, t, k, :], wr[:, k, :], start=(k == 0), stop=(k == 1))
                last.then_inc(r["lg_ps"], 1)
            chain.loop(B, route)
            pe.wait_ge(r["both"], 1)
            mm(bank[0][0:P, 0:TILES * NE], tri_strict[:, :], both[:, :, :].rearrange("p t e -> p (t e)"), start=True, stop=True)
            mm(bank[1][0:P, 0:TILES * NE], ones[0:P, 0:P], both[:, :, :].rearrange("p t e -> p (t e)"),
               start=True, stop=True).then_inc(r["rank"], 1)

            def ids(i, first):
                for s in range(4):
                    pe.wait_ge(r["hot"], 8 * i + 2 * s + 2)
                    mm(bank[2][:, 0:NB], row_hot[s][:, :], blk_hot[s][:, :], start=(first and s == 0), stop=True,
                       skip_group_check=True).then_inc(r["ids"], 1)
            chain.loop(TILES * 2 // 4, ids)
            pe.wait_ge(r["idx"], 1)

            def hid(n, i, s, first):
                pe.wait_ge(m_x[s], 16 * i + 16)
                if not (first and s == 0):
                    pe.wait_ge(m["xgT"], n)
                for k in range(2):
                    last = nc.tensor.transpose(bank[6][0:KC, BLK * k:BLK * k + BLK], x_blk[s][:, KC * k:KC * k + KC], ident[:, :])
                last.then_inc(m["xgT_ps"], 1)
                pe.wait_ge(m["xgT"], n + 1)
                pe.wait_ge(m_w[s], 64 * i + 64)
                for c in range(FC):
                    for k in range(2):
                        rows = KC + k
                        last = mm(bank[2 * s + c // 3][:, 128 * (c % 3):128 * (c % 3) + BLK],
                                  e_w1[s][0:rows, k, 128 * c:128 * c + 128], xgT[0:rows, k, :], start=(k == 0), stop=(k == 1))
                    if c % 3 == 2:
                        last.then_inc(m["hid"], 1)

            def back_to_d(n, s, started):
                if started:
                    pe.wait_ge(m["y"], n)
                mm(bank[7][:, 0:D], ones[0:1, :], e_b2[s][:, :], start=True, stop=False)
                for c in range(FC):
                    if c % 3 == 0:
                        pe.wait_ge(m["hT"], 2 * n + c // 3 + 1)
                    last = mm(bank[7][:, 0:D], hT[s][:, c, :], e_w2[s][:, c, :], start=False, stop=(c == FC - 1))
                last.then_inc(m["y_ps"], 1)

            def blocks(i, first):
                for s in range(UNROLL):
                    n = UNROLL * i + s
                    hid(n, i, s, first)
                    if not (first and s == 0):
                        back_to_d(n - 1, (s - 1) % UNROLL, not (first and s == 1))
            chain.loop(NB // UNROLL, blocks)
            back_to_d(NB - 1, (NB - 1) % UNROLL, True)
            all_loaded(pe, "a1")
            pe.wait_ge(m["y"], NB)
            pe.wait_ge(a1["ones"], 1)

            def attn1(Z, A, Bk, C):
                a, pa = A or (None, None)
                W = 4 * (HD + 1)

                def proj(t, lo, cols):
                    for dst, at, w, w_lo, n in cols:
                        for k in range(2):
                            last = mm(dst, xzT[0:KC + k, t, at + k], w[0:KC + k, k, w_lo:w_lo + n], start=(k == 0), stop=(k == 1))
                    last.then_inc(a1["proj"], 1)

                for j in range(NT):
                    n, par, t, out_tile, done = slot_tiles(j, Bk, C)
                    if A:
                        pe.wait_ge(a1["zn"], 3 * a + j + 1)
                        if Bk:
                            need(pe, a1["h"], 3 * Bk[0] + j - 2)
                        for s in range(4):
                            last = nc.tensor.transpose(bank[6][0:KC, P * s:P * s + P],
                                                       xz[pa][:, j, s // 2, KC * (s % 2):KC * (s % 2) + KC], ident[0:P, 0:P])
                        last.then_inc(a1["xzT_ps"], 1)
                    if j == 0 and Bk:
                        pe.wait_ge(a1["k_ft"], 3 * Bk[0] + 3)
                        heads_T(a1, *Bk, 2, 1)
                    if j and A:
                        pe.wait_ge(a1["k_ft"], 3 * a + j)
                        heads_T(a1, a, pa, j - 1, 1)
                    if n is not None:
                        pe.wait_ge(a1["qkT"], 6 * n + 2 * t + 2)
                        scores(a1, n, par, t, 0, 2)
                    if A:
                        pe.wait_ge(a1["xzT"], 9 * a + 3 * j + 3)
                        need(pe, a1["eq"], 6 * a + 2 * j)
                        need(pe, a1["kg"], 3 * a + j)
                        proj(j, 0, ((bank[4][0:P, 0:384], 2, a1_w, 0, 384),))
                    if done is not None:
                        pe.wait_ge(a1["w"], done + 1)
                        if not A:
                            need(pe, a1["h"], done)
                        for k in range(2):
                            last = nc.tensor.transpose(bank[6][0:KC, P * k:P * k + P], o3[:, out_tile, KC * k:KC * k + KC], ident[0:P, 0:P])
                        last.then_inc(a1["yT_ps"], 1)
                    if A:
                        need(pe, a1["v"], 3 * a + j)
                        proj(j, 1, ((bank[5][0:P, D:2 * D], 0, a1_wg, 0, D), (bank[5][0:P, 0:D], 2, a1_w, 384, D)))
                    if n is not None:
                        scores(a1, n, par, t, 2, 4)
                    if done is not None:
                        pe.wait_ge(a1["yT"], done + 1)
                        for k in range(2):
                            last = mm(bank[6][0:P, 2 * P:2 * P + D], y1T[0:KC + k, out_tile, k, :], a1_wo[0:KC + k, k, :],
                                      start=(k == 0), stop=(k == 1))
                        last.then_inc(a1["op"], 1)
                    if n is not None:
                        need(pe, a1["w"], 3 * n + t)
                        pe.wait_ge(a1["v"], 3 * n + t + 1)
                        if t:
                            pe.wait_ge(a1["stb"], 2 * n + t)
                            for g in range(3):
                                mm(bank[2][0:P, W * g:W * g + W], qkT[par][:, t, g, :], st1[:, g, :],
                                   start=(g == 0), stop=False, skip_group_check=True)
                        for i in range(4):
                            pe.wait_ge(a1["att"], 12 * n + 4 * t + i + 1)
                            for g in range(3):
                                at = W * g + (HD + 1) * i
                                last = mm(bank[2][0:P, at:at + HD + 1], att[:, 4 * g + i, :], v1[par][:, t, 4 * g + i],
                                          start=(t == 0 and i == 0 and g == 0), stop=True, skip_group_check=True)
                        last.then_inc(a1["O"], 1)
                        if t < 2:
                            if t == 0:
                                need(pe, a1["stb"], 2 * n)
                            for g in range(3):
                                last = mm(bank[3][:, W * g:W * g + W],
                                          qk[par][:, t, NH + 4 * g:NH + 4 * g + 4].rearrange("p h d -> p (h d)"),
                                          v1[par][:, t, 4 * g:4 * g + 4].rearrange("p h d -> p (h d)"),
                                          start=(t == 0 and g == 0), stop=True, skip_group_check=True)
                            last.then_inc(a1["st"], 1)
                    if A:
                        pe.wait_ge(a1["q_ft"], 3 * a + j + 1)
                        heads_T(a1, a, pa, j, 0)
            pipeline(pe, attn1, 2)
            pe.wait_ge(a1["h"], 3 * B)
            pe.wait_ge(a1["yT"], 3 * B)
            pe.wait_ge(f["wq"], 2)

            def ffn(Z, A, Bk, C):
                b, _ = Bk or (None, None)
                c, _ = C or (None, None)

                def gate_up(t):
                    pe.wait_ge(f["xqT"], 3 * b + t + 1)
                    need(pe, f["y"], (3 * b, 3 * b - 1, 3 * b + 1)[t])
                    for j in range(2):
                        for k in range(2):
                            last = mm(bank[2 * (t % 2) + j][0:P, :], xqT[:, t, k, :], w_in_q[:, k, HID * j:HID * j + HID],
                                      start=(k == 0), stop=(k == 1))
                    last.then_inc(f["gu"], 1)

                for t in range(NT):
                    if Bk:
                        pe.wait_ge(f["xq_"], 3 * b + t + 1)
                        need(pe, f["xqT"], 3 * b + t)
                        tb = bf16_tiles(6, 2)
                        for k in range(2):
                            last = nc.tensor.transpose(tb[0:KC, k, 0:P], xq[:, t, KC * k:KC * k + KC], identb[0:P, 0:P])
                        last.then_inc(f["xqT_ps"], 1)
                        if t:
                            gate_up(t - 1)
                    if C:
                        pe.wait_ge(f["yq"], 3 * c + t + 1)
                        need(pe, f["yqT"], 3 * c if t < 2 else 3 * c + 1)
                        tb = bf16_tiles(7 if t % 2 == 0 else 5, 4)
                        for i in range(4):
                            last = nc.tensor.transpose(tb[:, i, 0:P], yq[:, t, 128 * i:128 * i + 128], identb[0:P, 0:P])
                        last.then_inc(f["yqT_ps"], 1)
                if Bk:
                    gate_up(2)
                for t in range(NT):
                    if C:
                        pe.wait_ge(f["yqT"], 3 * c + t + 1)
                        need(pe, f["o"], 3 * c + t)
                        for i in range(4):
                            last = mm(bank[4][0:P, 0:D], yqT[:, t, i, :], w_out_q[:, i, :], start=(i == 0), stop=(i == 3))
                        last.then_inc(f["st"], 1)
            pipeline(pe, ffn, 2)

        @block.vector
        def _(dve):
            chain = Chain(dve, dve_chain)
            link, v = chain.link, nc.vector
            link(v.memset(eps5[:, :], 1e-5))
            all_loaded(dve, "tok")
            all_loaded(dve, "f")
            v.memset(eps6[:, :], 1e-6)
            chain.step(v.tensor_copy(identb[:, :], ident[:, :]))
            wsets = ((w_in[:, :, :].rearrange("p a n -> p (a n)"), w_in_q[:, :, :].rearrange("p a n -> p (a n)"), KC, D * 2 * HID),
                     (w_out[:, :, :].rearrange("p a n -> p (a n)"), w_out_q[:, :, :].rearrange("p a n -> p (a n)"), 128, D * HID))
            for i, (w, _, rows, _) in enumerate(wsets):
                v.tensor_reduce(wsum[0:rows, i:i + 1], w, AX, ALU.add, apply_absolute_value=True).then_inc(f["wsum"], 1)
            dve.wait_ge(f["wbc"], 1)
            for i, (_, _, _, count) in enumerate(wsets):
                k = chain.step(v.tensor_scalar(wback[:, i:i + 1], bank[0][:, i:i + 1], 1.0 / count, 1e-5, ALU.mult, ALU.max))
            chain.wait(k)
            link(v.reciprocal(wscale[:, :], wback[:, :]))
            for i, (w, wq, rows, _) in enumerate(wsets):
                link(v.tensor_scalar(w, w, wscale[0:rows, i:i + 1], MAGIC, ALU.mult, ALU.add))
                link(v.tensor_scalar(w, w, MAGIC, -1.0, ALU.subtract, ALU.max))
                v.tensor_scalar(wq, w, 1.0, None, ALU.min).then_inc(f["wq"], 1)
            link(v.memset(amax[:, :, :], 1.0))
            link(v.memset(rms[:, :, :], 1.0))

            dve.wait_ge(gathered, 16 * (2 * GP + 2 + GP))

            def tile_stats(b):
                dve.wait_ge(h_tok, 2 * b + 2)
                stand_alone(dve)
                for t in range(NT):
                    k = chain.step(v.bn_stats(stats[:, t, :], tile_of(h, 3 * b + t)))
                chain.wait(k)
                stand_alone(dve)
                for t in range(NT):
                    k = chain.step(v.bn_aggr(mv[:, t, :], stats[:, t, :]))
                chain.wait(k)
                link(v.tensor_copy(mv0[:, bass.ds(6 * b, 6)], mv[:, :, :].rearrange("p t c -> p (t c)")))


            def tok(b, first):
                if not first:
                    dve.wait_ge(tok_xT_ps, b)
                v.tensor_copy(x0[:, :, :].rearrange("p a (j c) -> p a j c", c=3),
                              g0[:, :, :, bass.ds(b * 3, 3)]).then_inc(tok_staged, 1)
                v.tensor_copy(x1[:, :].rearrange("p (j c) -> p j c", c=12),
                              g1[:, :, bass.ds(b * 12, 12)]).then_inc(tok_staged, 1)
                v.tensor_copy(x2[:, :, :], g2[:, :, bass.ds(b * 48, 48)]).then_inc(tok_staged, 1)
                dve.wait_ge(tok_h_ps, b + 1)
                v.tensor_copy(tile_of(h, 3 * b, 2), bank[5][0:P, 0:2 * D]).then_inc(h_tok, 1)
                v.tensor_copy(h[0:IMG_TOK - 2 * P, bass.ds((3 * b + 2) * D, D)],
                              bank[6][0:IMG_TOK - 2 * P, 0:D]).then_inc(h_tok, 1)
                tile_stats(b)
            chain.loop(B, tok)
            dve.sem_inc(a0["var"], 1)

            all_loaded(dve, "a0")
            link(v.memset(qk[0][:, :, :, :], 0.0))
            link(v.memset(qk[1][:, :, :, :], 0.0))
            link(v.tensor_scalar(tau[:, :], tau[:, :], -50.0, 30.0, ALU.max, ALU.min))
            dve.sem_inc(a0["set"], 1)
            dve.wait_ge(a0["tau"], 1)
            v.tensor_tensor(taumu[:, :].rearrange("p (h d) -> p h d", d=HD), mu[:, :].rearrange("p (h d) -> p h d", d=HD),
                            tau[:, :].rearrange("p (h a) -> p h a", a=1).to_broadcast([P, NH, HD]), ALU.mult).then_inc(a0["tau"], 1)
            v.reciprocal(it[:, :], time[:, :]).then_inc(a0["tau"], 1)

            def b3(ap2, shape, axis):
                pat = {2: "p (h a) -> p h a", 1: "p (a h) -> p a h"}[axis]
                return ap2.rearrange(pat, a=1).to_broadcast(shape)

            link(v.tensor_tensor(rt[:, :, :], b3(time[:, :], [P, NT, NH], 2), b3(tau[:, :], [P, NT, NH], 1), ALU.add))
            link(v.reciprocal(rt[:, :, :], rt[:, :, :]))
            link(v.tensor_scalar(rt[:, :, :], rt[:, :, :], -1.0 / np.sqrt(HD), None, ALU.mult))

            def masks(sems, b, t, lo, hi):
                if lo == 0:
                    need(dve, sems["O"], 3 * b + t)
                for i in range(lo, hi):
                    dve.wait_ge(sems["S"], 12 * b + 4 * t + i + 1)
                    v.tensor_tensor(att[:, :, :].rearrange("p (g i) l -> p i g l", i=4)[:, i],
                                    bank[i % 2][0:P, 0:3 * P].rearrange("p (g l) -> p g l", g=3),
                                    b3(tri[:, :], [P, 3, P], 1), ALU.mult).then_inc(sems["att"], 1)

            dve.wait_ge(a0["sd"], 1)
            link(v.reciprocal(rs0[:, :], rs0[:, :]))
            ch_a, ch_b, ch_c = Turns(dve, dve_turns[0], 15), Turns(dve, dve_turns[1], 23), Turns(dve, dve_turns[2], 7)

            def attn0(A, Bk, C):
                a, pa = A or (None, None)
                b, par = Bk or (None, None)
                c, _ = C or (None, None)
                o = o3[:, :, :].rearrange("p t (h d) -> p (t h) d", d=HD)

                def normalize(t):
                    need(dve, a0["xnT"], 3 * a + t - 2)
                    v.tensor_scalar(xn[:, t, :], tile_of(h, 3 * a + t), mv0[:, bass.ds(6 * a + 2 * t, 1)], rs0[:, bass.ds(3 * a + t, 1)],
                                    ALU.subtract, ALU.mult).then_inc(a0["xn"], 1)

                def rotate(t):
                    dve.wait_ge(a0["proj"], 3 * a + t + 1)
                    need(dve, a0["rope"], 3 * a + t - 2)
                    q = bank[4][0:P, 0:384].rearrange("p (h c d) -> p h c d", c=2, d=HD // 2)
                    tab = lambda m, lo, n: m[:, t, lo:lo + n].rearrange("p (a d) -> p a d", a=1).to_broadcast([P, 2 * NH, n])
                    r2 = rot2[:, t].rearrange("p (h c d) -> p h c d", c=2, d=HD // 2)
                    ch_a.step(v.tensor_tensor(rot1[:, t].rearrange("p (h d) -> p h d", d=HD),
                                              bank[4][0:P, 0:384].rearrange("p (h d) -> p h d", d=HD), tab(cos, 0, HD), ALU.mult))
                    ch_a.step(v.tensor_tensor(r2[:, :, 0], q[:, :, 1], tab(sin, 0, 8), ALU.mult))
                    k = ch_a.step(v.tensor_tensor(r2[:, :, 1], q[:, :, 0], tab(sin, 8, 8), ALU.mult))
                    ch_a.wait(k)
                    dve.sem_inc(a0["rot"], 1)

                def surprise(t):
                    dve.wait_ge(a0["cum"], 3 * a + t + 1)
                    if t == 0:
                        need(dve, a0["EP"], a - 1)
                    e = es[pa]
                    ch_a.link(v.tensor_tensor(us[:, :], vug[pa][:, t, D:2 * D], bank[6][0:P, 0:D], ALU.mult))
                    ch_a.link(v.tensor_reduce(e[:, t, NH:2 * NH], us[:, :].rearrange("p (h d) -> p h d", d=HD), AX, ALU.add))
                    v.tensor_tensor(e[:, t, NH:2 * NH], e[:, t, NH:2 * NH], rt[:, t, :], ALU.mult).then_inc(a0["s"], 1)

                def state(ch, n, t):
                    dve.wait_ge(a0["O"], 3 * n + t + 1)
                    dve.wait_ge(a0["st"], 2 * n + t + 1)
                    k = ch.step(v.tensor_tensor(stb[:, 0:2, :], bank[0][:, 0:384].rearrange("p (g n) -> p g n", g=2),
                                                b3(head_mask0[:, :], [128, 2, 192], 1), ALU.mult))
                    ch.wait(k)
                    v.tensor_tensor(stb[:, 2, :], bank[1][:, 0:192], head_mask0[:, :], ALU.mult).then_inc(a0["stb"], 1)

                def weigh(ch, n, t):
                    dve.wait_ge(a0["O"], 3 * n + t + 1)
                    cft = cf[:, t].rearrange("p h (c a) -> p h c a", a=1)
                    k = ch.step(v.tensor_tensor(wo3[:, 0:8], bank[2][0:P, 0:384].rearrange("p (h c d) -> p h c d", c=3, d=HD),
                                                cft[:, 0:8].to_broadcast([P, 8, 3, HD]), ALU.mult))
                    v.tensor_tensor(wo3[:, 8:12], bank[3][0:P, 0:192].rearrange("p (h c d) -> p h c d", c=3, d=HD),
                                    cft[:, 8:12].to_broadcast([P, 4, 3, HD]), ALU.mult).then_inc(a0["w"], 1)
                    return k

                def add_up(ch, n, t, k):
                    ch.wait(k)
                    dve.wait_ge(a0["w"], 3 * n + t + 1)
                    if t == 0:
                        need(dve, a0["yT_ps"], 2 * n)
                    return ch.step(v.tensor_reduce(o3[:, t, :].rearrange("p (h d) -> p h d", d=HD),
                                                   wo3[:, :, :, :].rearrange("p h c d -> p h d c"), AX, ALU.add))

                if A:
                    ch_a.turn(a)
                if Bk:
                    ch_b.turn(b)
                if C:
                    ch_c.turn(c)
                if A:
                    normalize(0)
                if Bk:
                    dve.wait_ge(a0["s"], 3 * b + 3)
                    v.tensor_reduce(mx[:, :], es[par][:, :, NH:2 * NH].rearrange("p t h -> p h t"), AX, ALU.max).then_inc(a0["mx"], 1)
                if C:
                    kw = weigh(ch_c, c, 1)
                    masks(a0, c, 2, 0, 2)
                    add_up(ch_c, c, 1, kw)
                if Bk:
                    dve.wait_ge(a0["mxT"], b + 1)
                    ch_b.link(v.tensor_reduce(m12[:, :], bank[7][0:NH, 192:192 + P], AX, ALU.max))
                    v.tensor_scalar(diag[:, :], ident[0:NH, 0:NH], m12[:, 0:1], None, ALU.mult).then_inc(a0["diag"], 1)
                    dve.wait_ge(a0["sq"], 3 * b + 3)
                    v.tensor_reduce(n2[:, :], sq[:, :, :].rearrange("p t (h d) -> p (t h) d", d=HD), AX, ALU.add).then_inc(a0["n2"], 1)
                    dve.wait_ge(a0["mb"], b + 1)
                    v.tensor_tensor(dsm[:, :, :], es[par][:, :, NH:2 * NH], b3(bank[7][0:P, 320:332], [P, NT, NH], 1),
                                    ALU.subtract).then_inc(a0["ds"], 1)
                    dve.wait_ge(a0["nrm"], b + 1)
                    ch_b.link(v.tensor_scalar(nrm[:, :], nrm[:, :], 1e-12, None, ALU.max))
                    ch_b.link(v.reciprocal(rn[:, :, :].rearrange("p t h -> p (t h)"), nrm[:, :]))
                    need(dve, a0["v3"], 3 * b)
                    ch_b.step(v.tensor_tensor(kc[:, :, :, 1], es[par][:, :, NH:2 * NH], rn[:, :, NH:2 * NH], ALU.mult))
                    ch_b.step(v.tensor_copy(kc[:, :, :, 2], rn[:, :, NH:2 * NH]))
                if A:
                    rotate(0)
                if Bk:
                    dve.wait_ge(a0["e"], b + 1)
                    k = ch_b.step(v.tensor_tensor(kc[:, :, :, 0], es[par][:, :, 0:NH], rn[:, :, NH:2 * NH], ALU.mult))
                    ch_b.wait(k)
                    dve.sem_inc(a0["kc"], 1)
                if C:
                    masks(a0, c, 2, 2, 4)
                if A:
                    surprise(0)
                    normalize(1)
                if Bk:
                    dve.wait_ge(a0["ge"], b + 1)
                    ch_b.link(v.tensor_scalar(ge[:, :, :], ge[:, :, :], 1.0, None, ALU.add))
                    ch_b.link(v.reciprocal(sg[:, :, :], ge[:, :, :]))
                    ch_b.link(v.tensor_tensor(be[:, :, :], sg[:, :, 0:NH], sg[:, :, NH:2 * NH], ALU.subtract))
                    ch_b.step(v.tensor_tensor(be[:, :, :], be[:, :, :], b3(it[:, :], [P, NT, NH], 2), ALU.mult))
                    dve.wait_ge(a0["EP"], b + 1)
                    v.tensor_copy(ep[:, :, :].rearrange("p t h -> p (t h)"), bank[7][0:P, 336:408]).then_inc(a0["ep"], 1)
                if C:
                    kw = weigh(ch_c, c, 2)
                if Bk:
                    masks(a0, b, 0, 0, 2)
                if C:
                    k = add_up(ch_c, c, 2, kw)
                    ch_c.wait(k)
                    ch_c.link(v.tensor_reduce(hm[:, :], o, AX, ALU.add))
                    ch_c.link(v.tensor_scalar(hm[:, :], hm[:, :], 1.0 / HD, None, ALU.mult))
                    v.tensor_tensor(o, o, b3(hm[:, :], [P, NT * NH, HD], 2), ALU.subtract).then_inc(a0["hc"], 1)
                if Bk:
                    dve.wait_ge(a0["ep"], b + 1)
                    itb = b3(it[:, :], [P, NT, NH], 2)
                    ch_b.link(v.tensor_scalar(al[:, :, :], ep[:, :, 0:NH], 1e-12, None, ALU.add))
                    ch_b.step(v.reciprocal(al[:, :, :], al[:, :, :]))
                    ch_b.link(v.tensor_tensor(ga[:, :, :], be[:, :, :], ep[:, :, NH:2 * NH], ALU.mult))
                    ch_b.step(v.tensor_tensor(al[:, :, :], al[:, :, :], sg[:, :, NH:2 * NH], ALU.mult))
                    ch_b.link(v.tensor_tensor(ga[:, :, :], ga[:, :, :], sg[:, :, NH:2 * NH], ALU.add))
                    ch_b.link(v.scalar_tensor_tensor(ga[:, :, :], ga[:, :, :], -1.0, itb, ALU.mult, ALU.mult))
                    for j, x in enumerate((al, be, ga)):
                        k = ch_b.step(v.tensor_tensor(cf[:, :, :, j], x[:, :, :], rn[:, :, 0:NH], ALU.mult))
                    ch_b.wait(k)
                if A:
                    rotate(1)
                if Bk:
                    masks(a0, b, 0, 2, 4)
                if A:
                    surprise(1)
                    normalize(2)
                if C:
                    dve.wait_ge(a0["hsq"], c + 1)
                    v.tensor_reduce(hr[:, :], sqh[:, :, :].rearrange("p t (h d) -> p t h d", d=HD), AX, ALU.add).then_inc(a0["hvar"], 1)
                if Bk:
                    state(ch_b, b, 0)
                if C:
                    dve.wait_ge(a0["hsd"], c + 1)
                    ch_c.link(v.reciprocal(hr[:, :], hr[:, :]))
                    v.tensor_tensor(o, o, b3(hr[:, :], [P, NT * NH, HD], 2), ALU.mult).then_inc(a0["y"], 1)
                if Bk:
                    kw = weigh(ch_b, b, 0)
                    masks(a0, b, 1, 0, 2)
                    add_up(ch_b, b, 0, kw)
                if A:
                    rotate(2)
                if Bk:
                    masks(a0, b, 1, 2, 4)
                if C:
                    for j, (lo, n) in enumerate(PAIRS):
                        dve.wait_ge(a0["op"], 2 * c + j + 1)
                        v.tensor_tensor(tile_of(h, 3 * c + lo, n), tile_of(h, 3 * c + lo, n), bank[2 + j][0:P, 0:D * n],
                                        ALU.add).then_inc(a0["h"], 1)
                if A:
                    surprise(2)
                if Bk:
                    state(ch_b, b, 1)
            pipeline(dve, attn0, 1)

            def layer_norm(b, sems, i, src, dst, dst_sem):
                stand_alone(dve)
                for t in range(NT):
                    k = chain.step(v.bn_stats(stats[:, t, :], src(t)))
                chain.wait(k)
                stand_alone(dve)
                for t in range(NT):
                    k = chain.step(v.bn_aggr(mv[:, t, :], stats[:, t, :]))
                chain.wait(k)
                dve.sem_inc(sems[0], 1)
                dve.wait_ge(sems[1], b + 1)
                link(v.reciprocal(rs[:, :], sd[:, :]))
                for t in range(NT):
                    v.tensor_scalar(dst[:, t, :], src(t), mv[:, t, 0:1], rs[:, t:t + 1],
                                    ALU.subtract, ALU.mult).then_inc(dst_sem, 1)

            def route(b, first):
                if not first:
                    dve.wait_ge(r["out"], 16 * b)
                layer_norm(b, (r["var"], r["sd"]), 0, lambda t: tile_of(h, 3 * b + t), xn, r["xn"])
                dve.wait_ge(r["xn"], 3 * b + 3)
                link(v.tensor_tensor(tile_of(h, 3 * b, 3), tile_of(h, 3 * b, 3), xn[:, :, :].rearrange("p t d -> p (t d)"), ALU.add))
                dve.wait_ge(r["lg_ps"], b + 1)
                v.tensor_copy(lg[:, bass.ds(3 * b, NT), :].rearrange("p t e -> p (t e)"), bank[0][0:P, 0:NT * NE]).then_inc(r["lg"], 1)
            chain.loop(B, route)
            te = [P, TILES, NE]
            dve.wait_ge(r["lg"], B)
            link(v.tensor_reduce(red[:, :], lg[:, :, :], AX, ALU.max))
            v.tensor_tensor(lg[:, :, :], lg[:, :, :], b3(red[:, :], te, 2), ALU.subtract).then_inc(r["lg"], 1)
            dve.wait_ge(r["ready"], 1)
            link(v.tensor_reduce(red[:, :], lg[:, :, :], AX, ALU.add))
            link(v.reciprocal(red[:, :], red[:, :]))
            link(v.tensor_tensor(lg[:, :, :], lg[:, :, :], b3(red[:, :], te, 2), ALU.mult))
            ie = b3(iota[:, 0:NE], te, 1)
            for j in range(2):
                link(v.tensor_reduce(gate[j][:, :], lg[:, :, :], AX, ALU.max))
                link(v.tensor_tensor(cand[:, :, :], lg[:, :, :], b3(gate[j][:, :], te, 2), ALU.is_lt))
                link(v.scalar_tensor_tensor(cand[:, :, :], cand[:, :, :], float(NE), ie, ALU.mult, ALU.add))
                link(v.tensor_reduce(red[:, :], cand[:, :, :], AX, ALU.min))
                link(v.tensor_tensor(oh[j][:, :, :], ie, b3(red[:, :], te, 2), ALU.is_equal))
                if j == 0:
                    link(v.scalar_tensor_tensor(lg[:, :, :], oh[0][:, :, :], -2.0, lg[:, :, :], ALU.mult, ALU.add))
            v.tensor_tensor(both[:, :, :], oh[0][:, :, :], oh[1][:, :, :], ALU.add).then_inc(r["both"], 1)
            link(v.memset(onee[:, :], 1.0))
            dve.wait_ge(r["rank"], 1)
            em = "p (t e) -> p e t"
            link(v.tensor_copy(tot[:, :].rearrange("p (e t) -> p e t", t=TILES), bank[1][0:P, 0:TILES * NE].rearrange(em, e=NE)))
            link(v.tensor_tensor_scan(inc[:, :], reset[:, :], tot[:, :], 0.0, ALU.mult, ALU.add))
            inc3 = inc[:, :].rearrange("p (e t) -> p e t", t=TILES)
            c3 = cmp[:, 0:NE * MAXB].rearrange("p (e n) -> p e n", e=NE)
            link(v.tensor_tensor(c3, inc3[:, :, TILES - 1:TILES].to_broadcast([P, NE, MAXB]), b3(steps[:, :], [P, NE, MAXB], 1), ALU.is_gt))
            link(v.tensor_reduce(nblk[:, :], c3, AX, ALU.add))
            link(v.tensor_tensor_scan(bend[:, :], onee[:, :], nblk[:, :], 0.0, ALU.mult, ALU.add))
            link(v.tensor_tensor(basee[:, :], bend[:, :], nblk[:, :], ALU.subtract))
            link(v.tensor_scalar(basee[:, :], basee[:, :], float(BLK), None, ALU.mult))
            be3 = cmp[:, 0:NB * NE].rearrange("p (n e) -> p n e", e=NE)
            link(v.tensor_tensor(be3, b3(bend[:, :], [P, NB, NE], 1), b3(iota[:, 0:NB], [P, NB, NE], 2), ALU.is_le))
            link(v.tensor_reduce(eb[:, :], be3, AX, ALU.add))
            link(v.tensor_scalar(eb[:, :], eb[:, :], float(NE - 1), None, ALU.min))
            v.tensor_copy(eb_i[:, :], eb[:, :]).then_inc(r["exp"], 1)
            link(v.tensor_tensor(pos[:, :, :].rearrange("p t e -> p e t"), inc3, tot[:, :].rearrange("p (e t) -> p e t", t=TILES), ALU.subtract))
            link(v.tensor_tensor(pos[:, :, :], pos[:, :, :], bank[0][0:P, 0:TILES * NE].rearrange("p (t e) -> p t e", e=NE), ALU.add))
            link(v.tensor_tensor(pos[:, :, :], pos[:, :, :], b3(basee[:, :], te, 1), ALU.add))
            for j in range(2):
                link(v.tensor_tensor(cand[:, :, :], oh[j][:, :, :], pos[:, :, :], ALU.mult))
                link(v.tensor_reduce(slot[:, :, j], cand[:, :, :], AX, ALU.add))
            link(v.tensor_copy(slot_i[:, :], slot[:, :, :].rearrange("p t j -> p (t j)")))
            link(v.tensor_scalar(part_i[:, :], slot_i[:, :], 7, None, ALU.arith_shift_right))
            link(v.tensor_copy(s_blk[:, :], part_i[:, :]))
            link(v.scalar_tensor_tensor(s_row[:, :], s_blk[:, :], -float(BLK), slot[:, :, :].rearrange("p t j -> p (t j)"), ALU.mult, ALU.add))

            def ids(i, first):
                for s in range(4):
                    u = 4 * i + s
                    if not first:
                        dve.wait_ge(r["ids"], u - 3)
                    v.tensor_scalar(row_hot[s][:, :], iota[:, :], s_row[:, bass.ds(u, 1)], None, ALU.is_equal).then_inc(r["hot"], 1)
                    v.tensor_scalar(blk_hot[s][:, :], iota[:, 0:NB], s_blk[:, bass.ds(u, 1)], token[:, bass.ds(2 * i + s // 2, 1)],
                                    ALU.is_equal, ALU.mult).then_inc(r["hot"], 1)
            chain.loop(TILES * 2 // 4, ids)
            dve.wait_ge(r["ids"], 2 * TILES)
            v.memset(xgT[:, :, :], 1.0)
            v.tensor_copy(idx[:, :], bank[2][:, 0:NB]).then_inc(r["idx"], 1)
            dve.wait_ge(r["idx"], 1)

            def y_out(n, i, s, first):
                dve.wait_ge(m["y_ps"], n + 1)
                if not first:
                    dve.wait_ge(m_out[s], 16 * i)
                v.tensor_copy(yb[s][:, :], bank[7][:, 0:D]).then_inc(m["y"], 1)

            def blocks(i, first):
                for s in range(UNROLL):
                    n = UNROLL * i + s
                    dve.wait_ge(m["xgT_ps"], n + 1)
                    if not (first and s == 0):
                        dve.wait_ge(m["hid"], 2 * n)
                    v.tensor_copy(xgT[0:KC, :, :].rearrange("p a t -> p (a t)"), bank[6][0:KC, 0:2 * BLK]).then_inc(m["xgT"], 1)
                    if s:
                        y_out(n - 1, i, s - 1, first)
                    elif not first:
                        y_out(n - 1, i - 1, UNROLL - 1, True)
            def y_last(i, first):
                pass
            chain.loop(NB // UNROLL, blocks)
            y_out(NB - 1, NB // UNROLL - 1, UNROLL - 1, False)
            all_loaded(dve, "a1")
            for s in range(UNROLL):
                dve.wait_ge(m_out[s], 16 * (NB // UNROLL))
            link(v.memset(v1[0][:, :, :, :], 1.0))
            link(v.memset(v1[1][:, :, :, :], 1.0))
            link(v.memset(y1T[:, :, :, :], 1.0))
            link(v.memset(xzT[:, :, :, :], 1.0))
            dve.sem_inc(a1["ones"], 1)
            ch_a1, ch_z, ch_w = ch_a.next_phase(B, 6), ch_b.next_phase(B, 20), ch_c.next_phase(B, 2)
            hv = lambda ap: ap.rearrange("p (h d) -> p h d", d=HD)

            def attn1(Z, A, Bk, C):
                a, pa = A or (None, None)
                z, pz = Z or (None, None)
                tile = lambda n: tile_of(h, n)
                W = 4 * (HD + 1)

                def moments(src, sem_):
                    for t in range(NT):
                        k = ch_z.step(v.bn_stats(stats[:, t, :], src(t)))
                    ch_z.wait(k)
                    stand_alone(dve)
                    for t in range(NT):
                        k = ch_z.step(v.bn_aggr(mv[:, t, :], stats[:, t, :]))
                    ch_z.wait(k)
                    dve.sem_inc(sem_, 1)

                def normalize(src, i, sem_):
                    dve.wait_ge(a1["sd"], 2 * z + i + 1)
                    ch_z.link(v.reciprocal(rs[:, :], sd[:, :]))
                    for t in range(NT):
                        v.tensor_scalar(xz[pz][:, t, i, :], src(t), mv[:, t, 0:1], rs[:, t:t + 1],
                                        ALU.subtract, ALU.mult).then_inc(sem_, 1)

                if A:
                    ch_a1.turn(a)
                if Z:
                    ch_z.turn(z)
                for j in range(NT):
                    n, par, t, out_tile, done = slot_tiles(j, Bk, C)
                    if done is not None:
                        if out_tile < 2:
                            dve.wait_ge(a1["O"], done + 1)
                            dve.wait_ge(a1["st"], 2 * before_batch(j, Bk, C) + out_tile + 1)
                            v.tensor_tensor(st1[:, :, :], bank[3][:, 0:3 * W].rearrange("p (g n) -> p g n", g=3),
                                            b3(head_mask1[:, :], [128, 3, W], 1), ALU.mult).then_inc(a1["stb"], 1)
                        ch_w.turn(done)
                        dve.wait_ge(a1["O"], done + 1)
                        need(dve, a1["yT_ps"], done - 2)
                        oo = bank[2][0:P, 0:3 * W].rearrange("p (h d) -> p h d", d=HD + 1)
                        ch_w.link(v.tensor_scalar(den[:, :], oo[:, :, HD], 1e-6, None, ALU.add))
                        ch_w.link(v.reciprocal(den[:, :], den[:, :]))
                        v.tensor_tensor(hv(o3[:, out_tile]), oo[:, :, 0:HD], b3(den[:, :], [P, NH, HD], 2), ALU.mult).then_inc(a1["w"], 1)
                    if n is not None:
                        masks(a1, n, t, 0, 2)
                    if A:
                        dve.wait_ge(a1["ge"], 3 * a + j + 1)
                        ch_a1.link(v.tensor_scalar(ge1[:, j], ge1[:, j], 1.0, None, ALU.add))
                        ch_a1.link(v.reciprocal(ge1[:, j], ge1[:, j]))
                        need(dve, a1["ek"], 6 * a + 2 * j - 4)
                        v.tensor_tensor(kg[:, j], bank[4][0:P, D:2 * D], ge1[:, j], ALU.mult).then_inc(a1["kg"], 1)
                        dve.wait_ge(a1["eq"], 6 * a + 2 * j + 2)
                        need(dve, a1["st"], 2 * a - 2)
                        need(dve, a1["qkT_ps"], 6 * a - 6)
                        v.scalar_tensor_tensor(qk[pa][:, j, 0:NH, 0:HD], hv(rot1[:, j, 0:D]), 1.0, hv(relu[:, j, 0:D]),
                                               ALU.min, ALU.add).then_inc(a1["q_ft"], 1)
                    if n is not None:
                        masks(a1, n, t, 2, 4)
                    if A:
                        dve.wait_ge(a1["ek"], 6 * a + 2 * j + 2)
                        v.scalar_tensor_tensor(qk[pa][:, j, NH:2 * NH, 0:HD], hv(rot1[:, j, D:2 * D]), 1.0, hv(relu[:, j, D:2 * D]),
                                               ALU.min, ALU.add).then_inc(a1["k_ft"], 1)
                    if done is not None:
                        dve.wait_ge(a1["op"], done + 1)
                        v.tensor_tensor(tile(done), tile(done), bank[6][0:P, 2 * P:2 * P + D], ALU.add).then_inc(a1["h"], 1)
                    if Z and j == 0:
                        dve.wait_ge(a1["yg"], 96 * z + 96)
                        stand_alone(dve)
                        for e in range(2):
                            for t2 in range(NT):
                                k = ch_z.step(v.scalar_tensor_tensor(tile(3 * z + t2), yg[:, t2, e, :], gate[e][:, bass.ds(3 * z + t2, 1)],
                                                                     tile(3 * z + t2), ALU.mult, ALU.add))
                            ch_z.wait(k)
                            stand_alone(dve)
                        dve.sem_inc(a1["cmb"], 1)
                        moments(lambda t2: tile(3 * z + t2), a1["var"])
                    if Z and j == 1:
                        need(dve, a1["xzT_ps"], 3 * z - 3)
                        normalize(lambda t2: tile(3 * z + t2), 0, a1["xn"])
                        dve.wait_ge(a1["xn"], 3 * z + 3)
                        stand_alone(dve)
                        moments(lambda t2: xz[pz][:, t2, 0, :], a1["var"])
                    if Z and j == 2:
                        normalize(lambda t2: xz[pz][:, t2, 0, :], 1, a1["zn"])
            pipeline(dve, attn1, 2)
            dve.wait_ge(a1["h"], 3 * B)
            ch_z, ch_s = ch_z.next_phase(B, 6), ch_a1.next_phase(B, 6)

            def ffn(Z, A, Bk, C):
                z, _ = Z or (None, None)
                a, pa = A or (None, None)
                b, par = Bk or (None, None)
                c, _ = C or (None, None)
                now = b if Bk else c + 1 if C else None
                tile = lambda n: tile_of(h, n)
                if A:
                    dve.wait_ge(f["sd"], a + 1)
                    v.reciprocal(rs[:, :], sd[:, :]).then_inc(f["rs"], 1)
                    dve.wait_ge(f["rs"], a + 1)
                    need(dve, f["sq"], 3 * a)
                    need(dve, f["xg"], 3 * a)
                    for t in range(NT):
                        v.tensor_scalar(xn[:, t, :], tile(3 * a + t), mv[:, t, 0:1], rs[:, t:t + 1],
                                        ALU.subtract, ALU.mult).then_inc(f["xn"], 1)
                if now is not None:
                    if Bk:
                        dve.wait_ge(f["rms"], b + 1)
                        need(dve, f["xs"], 3 * b)
                        need(dve, f["sil"], 3 * b)
                    if C:
                        dve.wait_ge(f["rms2"], c + 1)
                        need(dve, f["ys"], 3 * c)
                    ch_s.turn(now)
                    ch_s.link(v.reciprocal(rms[:, :, :], rms[:, :, :]))
                    ch_s.link(v.tensor_tensor(top[:, :, :], amax[:, :, :], rms[:, :, :], ALU.mult))
                    ch_s.link(v.tensor_scalar(top[:, :, :], top[:, :, :], 1e-5, None, ALU.max))
                    ch_s.link(v.reciprocal(qs[:, :, :], top[:, :, :]))
                    ch_s.step(v.scalar_tensor_tensor(qs[:, :, :], qs[:, :, :], 127.0, rms[:, :, :], ALU.mult, ALU.mult))
                    k = ch_s.step(v.scalar_tensor_tensor(back[:, :, :], top[:, :, :], 1.0 / 127.0,
                                                         b3(wback[0:P, :], [P, 2, NT], 2), ALU.mult, ALU.mult))
                    ch_s.wait(k)
                    dve.sem_inc(f["sc"], 1)
                for t in range(NT):
                    for on, batch, src, dst, ready, half, sem_ in ((Bk, b, xs, xq, "xs", "x1", "xq_"), (C, c, ys, yq, "ys", "y1", "yq")):
                        if on:
                            dve.wait_ge(f[ready], 3 * batch + t + 1)
                            v.tensor_scalar(src[:, t], src[:, t], MAGIC, MAGIC - 128.0, ALU.add, ALU.max).then_inc(f[half], 1)
                            dve.wait_ge(f[half], 3 * batch + t + 1)
                            used = "xqT_ps" if on is Bk else "yqT_ps"
                            need(dve, f[used], 3 * batch + t - 2)
                            v.tensor_scalar(dst[:, t], src[:, t], MAGIC + 127.0, MAGIC, ALU.min, ALU.subtract).then_inc(f[sem_], 1)
                if C:
                    need(dve, f["out"], 16 * c)
                for t in range(NT):
                    if A:
                        dve.wait_ge(f["xg"], 3 * a + t + 1)
                        v.tensor_reduce(amax[:, 0, t:t + 1], xg[pa][:, t], AX, ALU.max, apply_absolute_value=True).then_inc(f["ax"], 1)
                    if Bk:
                        dve.wait_ge(f["sil"], 3 * b + t + 1)
                        need(dve, f["z"], 3 * b + t - 2)
                        need(dve, f["sq2"], 3 * b + t - 2)
                        v.scalar_tensor_tensor(yf[:, t], bank[2 * (t % 2)][0:P, :], back[:, 0, t:t + 1], sil[:, t], ALU.mult, ALU.mult).then_inc(f["y"], 1)
                    if C:
                        dve.wait_ge(f["st"], 3 * c + t + 1)
                        v.scalar_tensor_tensor(fo[:, t], bank[4][0:P, 0:D], back[:, 1, t:t + 1], tile(3 * c + t), ALU.mult, ALU.add).then_inc(f["o"], 1)
                if Z:
                    ch_z.turn(z)
                    stand_alone(dve)
                    for t in range(NT):
                        k = ch_z.step(v.bn_stats(stats[:, t, :], tile(3 * z + t)))
                    ch_z.wait(k)
                    stand_alone(dve)
                    if A:
                        dve.wait_ge(f["xn"], 3 * a + 3)
                        stand_alone(dve)
                    for t in range(NT):
                        k = ch_z.step(v.bn_aggr(mv[:, t, :], stats[:, t, :]))
                    ch_z.wait(k)
                    dve.sem_inc(f["var"], 1)
                if Bk:
                    for t in range(NT):
                        dve.wait_ge(f["z"], 3 * b + t + 1)
                        v.tensor_reduce(amax[:, 1, t:t + 1], yg2[par][:, t], AX, ALU.max, apply_absolute_value=True).then_inc(f["ax"], 1)
                    dve.wait_ge(f["ax"], 3 * b + 3)
            pipeline(dve, ffn, 2)


def kernel(**inputs):
    import numpy as _np
    import concourse.bacc as _bacc
    from concourse import mybir as _mybir
    from concourse.bass_utils import run_bass_kernel_spmd as _run

    given = {k: _np.asarray(v) for k, v in inputs.items()}
    arrays = {f"c_{k}": v for k, v in shape_constants().items()}
    arrays.update(laid_out(given["x"], given["txt"], given))
    nc = _bacc.Bacc("TRN2", target_bir_lowering=False, num_devices=1)
    dram = {k: nc.dram_tensor(k, v.shape, _mybir.dt.from_np(v.dtype), kind="ExternalInput").ap()
            for k, v in arrays.items()}
    out = nc.dram_tensor("out", (B, L, D), F32, kind="ExternalOutput").ap()
    early_fusion(nc, dram, out)
    return _run(nc, [arrays], core_ids=[0]).results[0]["out"]
```

```python
from contextlib import ExitStack

import numpy as np

import concourse.bass as bass
from concourse import mybir

F32 = mybir.dt.float32
BF16 = mybir.dt.bfloat16
I32 = mybir.dt.int32
ALU = mybir.AluOpType
ACT = mybir.ActivationFunctionType
AX = mybir.AxisListType.X

B, L, D = 8, 333, 192
P, NT = 111, 3
TILES = B * NT
NH, HD = 12, 16
KC = 96
IMG_TOK, TXT = 256, 77
EMB, GP = 64, 16
FEAT = (3, 12, 48)
TOK1, TOK2 = 64, 16
NE, FF = 16, 768
FC = FF // 128
BLK = 128
NB = (2 * B * L - NE) // BLK + NE
MAXB = -(-B * L // BLK)
UNROLL = 3
HID = 512
PAIRS = ((0, 2), (2, 1))
WARM_UP = 66
ARENA = 16500
MAGIC = 12582912.0


def shape_constants():
    f = np.float32
    c = {}
    c["ident"] = np.eye(128, dtype=f)
    c["ones"] = np.ones((128, 128), f)
    m = np.arange(P)
    c["tri"] = (m[:, None] <= m[None, :]).astype(f)
    c["tri_strict"] = (m[:, None] < m[None, :]).astype(f)
    pos = np.arange(L, dtype=f)
    inv = f(1.0) / f(10000.0) ** (np.arange(0, HD, 2, dtype=f) / f(HD))
    ang = (pos[:, None] * inv[None, :]).astype(f)
    cos = np.repeat(np.cos(ang), 2, axis=-1).astype(f)
    sin = np.repeat(np.sin(ang), 2, axis=-1).astype(f)
    sin[:, :HD // 2] *= -1
    c["cos"] = cos.reshape(NT, P, HD).transpose(1, 0, 2)
    c["sin"] = sin.reshape(NT, P, HD).transpose(1, 0, 2)
    c["time"] = (pos + 1).reshape(NT, P).T
    for lvl, n in ((1, TOK1), (2, TOK2)):
        at = (np.arange(IMG_TOK, dtype=f) + f(0.5)) * f(n / IMG_TOK) - f(0.5)
        at = np.clip(at, f(0), f(n - 1))
        i0 = np.floor(at).astype(np.int32)
        i1 = np.minimum(i0 + 1, n - 1)
        w = (at - i0).astype(f)
        a = np.zeros((n, IMG_TOK), f)
        np.add.at(a, (i0, np.arange(IMG_TOK)), f(1) - w)
        np.add.at(a, (i1, np.arange(IMG_TOK)), w)
        c[f"interp{lvl}"] = a
    for name, wid in (("head_mask0", 3 * HD), ("head_mask1", HD + 1)):
        c[name] = np.kron(np.eye(4, dtype=f), np.ones((32, wid), f))
    c["iota"] = np.broadcast_to(np.arange(128, dtype=f), (128, 128))
    c["steps"] = np.broadcast_to(BLK * np.arange(MAXB, dtype=f), (P, MAXB))
    c["reset"] = np.broadcast_to(np.tile(np.arange(TILES) > 0, NE), (P, NE * TILES))
    c["token"] = (np.arange(TILES)[None, :] * P + m[:, None])
    return {k: np.ascontiguousarray(v, dtype=f) for k, v in c.items()}


def laid_out(x, txt, w):
    a = {"txt": txt}
    for lvl, p in enumerate((1, 2, 4)):
        g = 64 // p
        t = x.reshape(B, 3, g, p, g, p).transpose(2, 4, 0, 3, 5, 1)
        a[f"patches{lvl}"] = t.reshape(g * g, B * p * p * 3)
        a[f"idx{lvl}"] = w[f"L0_tok_idx{lvl}"]
    a["idx0"] = a["idx0"].reshape(2, 128, GP).transpose(1, 0, 2)
    a["idx1"] = a["idx1"].reshape(TOK1, 2, GP // 2).transpose(1, 0, 2).reshape(128, GP // 2)
    a["idx2"] = a["idx2"].reshape(2, 128).T
    a["tok_w0"] = w["L0_tok_W0"].T
    a["tok_w1"] = w["L0_tok_W1"].T.reshape(2, KC, EMB).transpose(1, 0, 2)
    a["tok_w2"] = w["L0_tok_W2"].T.reshape(GP, 48, EMB).transpose(1, 0, 2)
    a["tok_b"] = np.stack([w[f"L0_tok_b{i}"] for i in range(3)], 1)
    a["tok_wf"] = w["L0_tok_Wf"].T.reshape(3, EMB, D).transpose(1, 0, 2)
    a["tok_bf"] = w["L0_tok_bf"][None, :]

    def chunks(m):
        return m.reshape(2, KC, -1).transpose(1, 0, 2)

    wg = w["L0_attn_Wg"].reshape(NH, 3, D).transpose(1, 0, 2)[:2].reshape(2 * NH, D)
    a["a0_w"] = chunks(np.concatenate(
        [w["L0_attn_Wq"], w["L0_attn_Wk"], w["L0_attn_Wv"], w["L0_attn_Wu"], wg]).T)
    a["a0_wo"] = chunks(w["L0_attn_Wo"].T)
    a["a0_mu"] = w["L0_attn_prior_mu"].reshape(1, D)
    a["a0_tau"] = w["L0_attn_prior_log_tau"].reshape(1, NH)
    a["wr"] = chunks(w["L0_ffn_Wr"].T)
    a["e_w1"] = w["L0_ffn_W1"].reshape(NE, 2, KC, FF).transpose(0, 2, 1, 3)
    a["e_b1"] = w["L0_ffn_b1"][:, None]
    a["e_w2"] = w["L0_ffn_W2"].reshape(NE, FC, 128, D).transpose(0, 2, 1, 3)
    a["e_b2"] = w["L0_ffn_b2"][:, None]

    def with_bias(m, b):
        return chunks(m), b[None, :]

    a["a1_w"], a["a1_b"] = with_bias(w["L1_attn_W_qkv"], w["L1_attn_b_qkv"])
    a["a1_wg"], a["a1_bg"] = with_bias(w["L1_attn_W_gate"], w["L1_attn_b_gate"])
    a["a1_wo"], a["a1_bo"] = with_bias(w["L1_attn_W_proj"], w["L1_attn_b_proj"])
    a["a1_ln"] = np.stack([w["L1_attn_ln_g"], w["L1_attn_ln_b"]], 1).reshape(2, KC, 2).transpose(1, 0, 2)
    a["f_win"] = chunks(w["L1_ffn_w_in"].T)
    a["f_gin"] = w["L1_ffn_g_in"][None, :]
    a["f_wout"] = w["L1_ffn_w_out"].T.reshape(4, 128, D).transpose(1, 0, 2)
    a["f_gout"] = w["L1_ffn_g_out"][None, :]
    return {k: np.ascontiguousarray(v) for k, v in a.items()}


class Chain:

    def __init__(self, eng, sem):
        self.eng, self.sem, self.base, self.per, self.k, self.at = eng, sem, 0, 0, 0, 0

    def turn(self, i):
        self.at = self.base + i * self.per
        self.k = 0

    def step(self, ins):
        ins.then_inc(self.sem, 1)
        self.k += 1
        return self.k

    def wait(self, k):
        self.eng.wait_ge(self.sem, self.at + k)

    def link(self, ins):
        self.wait(self.step(ins))

    def loop(self, n, body):
        self.base += self.k
        self.turn(0)
        body(0, True)
        self.per = self.k
        if n > 1:
            with self.eng.Fori(1, n) as i:
                self.turn(i)
                body(i, False)
        self.base += n * self.per
        self.turn(0)


class Turns(Chain):

    def __init__(self, eng, sem, steps):
        super().__init__(eng, sem)
        self.per = steps

    def turn(self, i):
        assert self.k in (0, self.per), self.k
        super().turn(i)

    def next_phase(self, turns, steps):
        new = Turns(self.eng, self.sem, steps)
        new.base = self.base + turns * self.per
        return new


def need(eng, sem, n):
    if not isinstance(n, int) or n > 0:
        eng.wait_ge(sem, n)


def pipeline(eng, step, ahead):
    def at(k, parity):
        return (k, parity % 2) if not isinstance(k, int) or 0 <= k < B else None

    def whole(k, parity):
        step(*(at(k + d, parity + d) for d in range(ahead, -2, -1)))

    first = 2
    pairs = (B - ahead - first) // 2
    for k in range(-ahead, first):
        whole(k, k % 2)
    with eng.Fori(0, pairs) as i:
        whole(2 * i + first, 0)
        whole(2 * i + first + 1, 1)
    for k in range(2 * pairs + first, B + 1):
        whole(k, k % 2)


def before_batch(j, Bk, C):
    return (Bk if j == 2 else C)[0]


def slot_tiles(j, Bk, C):
    now = (*C, 2) if j == 0 and C else (*Bk, j - 1) if j and Bk else (None, None, None)
    out_tile = (1, 2, 0)[j]
    batch = Bk if j == 2 else C
    return (*now, out_tile, 3 * batch[0] + out_tile if batch else None)


def early_fusion(nc, dram, out):
    with ExitStack() as ctx:
        def sb(name, shape, dt=F32):
            return ctx.enter_context(nc.sbuf_tensor(name, shape, dt))

        def sem(name):
            return ctx.enter_context(nc.semaphore(name))

        bank = [ctx.enter_context(nc.psum_tensor(f"bank{i}", [128, 512], F32)) for i in range(8)]

        arena = sb("arena", [128, ARENA])

        class Taker:
            def __init__(self, at=0):
                self.at = at

            def __call__(self, shape):
                n = int(np.prod(shape[1:]))
                flat = arena[0:shape[0], self.at:self.at + n]
                self.at += n
                assert self.at <= ARENA, self.at
                names = "abcd"[:len(shape) - 1]
                return flat.rearrange(f"p ({' '.join(names)}) -> p {' '.join(names)}",
                                      **{k: v for k, v in zip(names, shape[1:])})

        tok_buf, attn_buf, moe_buf, ffn_buf = Taker(), Taker(), Taker(), Taker()

        h = sb("h", [P, TILES * D])

        def tile_of(buf, n, count=1):
            return buf[:, bass.ds(n * D, count * D)]

        const, plan = {}, {"tok": [], "f": [], "a0": []}

        def load(stage, name, shape, src=None, dt=F32):
            t = sb(f"s_{name}", shape, dt)
            full = t[tuple(slice(None) for _ in shape)]
            plan[stage].append((full, dram[name] if src is None else src))
            return t

        ident = load("tok", "c_ident", [128, 128])
        ones = load("tok", "c_ones", [128, 128])
        plan["tok"].append((h[IMG_TOK - 2 * P:P, :].rearrange("p (b t d) -> p b t d", t=NT, d=D)[:, :, 2, :],
                            dram["txt"].rearrange("b p d -> p b d")))
        idx0 = load("tok", "idx0", [128, 2, GP], dt=I32)
        idx1 = load("tok", "idx1", [128, GP // 2], dt=I32)
        idx2 = load("tok", "idx2", [128, 2], dt=I32)
        w0 = load("tok", "tok_w0", [48, EMB])
        w1 = load("tok", "tok_w1", [KC, 2, EMB])
        w2 = load("tok", "tok_w2", [48, GP, EMB])
        tok_b = load("tok", "tok_b", [EMB, 3])
        wf = sb("s_tok_wf", [EMB + 1, 3, D])
        plan["tok"].append((wf[0:EMB, :, :], dram["tok_wf"]))
        plan["tok"].append((wf[EMB:EMB + 1, 2, :], dram["tok_bf"]))
        interp1 = load("tok", "c_interp1", [TOK1, IMG_TOK])
        interp2 = load("tok", "c_interp2", [TOK2, IMG_TOK])
        tri = load("a0", "c_tri", [P, P])
        cos = load("a0", "c_cos", [P, NT, HD])
        sin = load("a0", "c_sin", [P, NT, HD])
        time = load("a0", "c_time", [P, NT])
        head_mask0 = load("a0", "c_head_mask0", [128, 12 * HD])
        a0_w = load("a0", "a0_w", [KC, 2, 4 * D + 2 * NH])
        a0_wo = load("a0", "a0_wo", [KC, 2, D])
        mu = load("a0", "a0_mu", [P, D], dram["a0_mu"].to_broadcast([P, D]))
        tau = load("a0", "a0_tau", [P, NH], dram["a0_tau"].to_broadcast([P, NH]))

        wr = load("a0", "wr", [KC, 2, NE])
        tri_strict = load("a0", "c_tri_strict", [P, P])
        iota = load("a0", "c_iota", [P, 128], dram["c_iota"][0:P, :])
        steps = load("a0", "c_steps", [P, MAXB])
        reset = load("a0", "c_reset", [P, NE * TILES])
        token = load("a0", "c_token", [P, TILES])

        def load_biased(stage, name, n, bias):
            t = sb(f"s_{name}", [KC + 1, 2, n])
            plan[stage].append((t[0:KC, :, :], dram[name]))
            plan[stage].append((t[KC:KC + 1, 1, :], dram[bias]))
            return t

        a1_w = load_biased("a0", "a1_w", 3 * D, "a1_b")
        a1_wg = load_biased("a0", "a1_wg", D, "a1_bg")
        a1_wo = load_biased("a0", "a1_wo", D, "a1_bo")
        a1_ln = load("a0", "a1_ln", [KC, 2, 2])
        head_mask1 = load("a0", "c_head_mask1", [128, 4 * (HD + 1)])
        w_in = load("f", "f_win", [KC, 2, 2 * HID])
        w_out = load("f", "f_wout", [128, 4, D])
        g_in = load("f", "f_gin", [P, D], dram["f_gin"].to_broadcast([P, D]))
        g_out = load("f", "f_gout", [P, HID], dram["f_gout"].to_broadcast([P, HID]))

        xn_dram = nc.dram_tensor("xn_dram", (B * L, D), F32, kind="Internal").ap()
        y_dram = nc.dram_tensor("y_dram", (NB * BLK, D), F32, kind="Internal").ap()

        loaded = {k: sem(f"loaded_{k}") for k in plan}
        turns_passed = sem("turns_passed")
        warm = sem("warm")

        g0 = tok_buf([128, 2, GP, 3 * B])
        g1 = tok_buf([128, GP // 2, 12 * B])
        g2 = tok_buf([128, 2, 48 * B])
        x0 = tok_buf([128, 2, 48])
        x1 = tok_buf([128, KC])
        x2 = tok_buf([128, 2, 48])
        x02T = tok_buf([48, 512])
        x1T = tok_buf([KC, 2, TOK1])
        y1 = tok_buf([TOK1, EMB])
        y2 = tok_buf([TOK2, EMB])
        catT = [tok_buf([EMB + 1, 3, IMG_TOK]) for _ in range(2)]
        gathered = sem("gathered")
        tok_staged, tok_xT_ps, tok_xT, tok_y_ps = (sem(n) for n in ("tok_staged", "tok_xT_ps", "tok_xT", "tok_y_ps"))
        tok_y, tok_i_ps, tok_cat, tok_h_ps, h_tok = (sem(n) for n in ("tok_y", "tok_i_ps", "tok_cat", "tok_h_ps", "h_tok"))

        rot1 = attn_buf([P, NT, 2 * D])
        qkT = [attn_buf([128, NT, 6, P]) for _ in range(2)]
        att = attn_buf([P, NH, P])
        a0_buf, a1_buf = Taker(attn_buf.at), Taker(attn_buf.at)
        eps5 = sb("eps5", [128, 1])
        stats = sb("stats", [P, NT, 6])
        mv = sb("mv", [P, NT, 2])
        mv0 = sb("mv0", [P, TILES * 2])
        rs0 = sb("rs0", [P, TILES])
        sd = sb("sd", [P, NT])
        rs = sb("rs", [P, NT])
        xn = sb("xn", [P, NT, D])
        xT = sb("xT", [KC, NT, 2, P])
        vug = [a0_buf([P, NT, 2 * D + 2 * NH]) for _ in range(2)]
        sqh = a0_buf([P, NT, D])
        ge = sb("ge", [P, NT, 2 * NH])
        rot2 = a0_buf([P, NT, 2 * D])
        qk = [sb(f"qk{i}", [P, NT, 2 * NH, 32]) for i in range(2)]
        sq = a0_buf([P, NT, 2 * D])
        n2 = sb("n2", [P, NT * 2 * NH])
        nrm = sb("nrm", [P, NT * 2 * NH])
        rn = sb("rn", [P, NT, 2 * NH])
        ep = sb("ep", [P, NT, 2 * NH])
        es = [sb(f"es{i}", [P, NT, 2 * NH]) for i in range(2)]
        mx = sb("mx", [P, NH])
        m12 = sb("m12", [NH, 1])
        diag = sb("diag", [NH, NH])
        dsm = sb("dsm", [P, NT, NH])
        kc = sb("kc", [P, NT, NH, 3])
        v3 = [a0_buf([P, NT, NH, 3, HD]) for _ in range(2)]
        sg = sb("sg", [P, NT, 2 * NH])
        al = sb("al", [P, NT, NH])
        be = sb("be", [P, NT, NH])
        ga = sb("ga", [P, NT, NH])
        cf = sb("cf", [P, NT, NH, 3])
        stb = a0_buf([128, 3, 12 * HD])
        wo3 = a0_buf([P, NH, 3, HD])
        o3 = sb("o3", [P, NT, D])
        hm = sb("hm", [P, NT * NH])
        hr = sb("hr", [P, NT * NH])
        yT = sb("yT", [KC, NT, 2, P])
        us = sb("us", [P, D])
        it = sb("it", [P, NT])
        rt = sb("rt", [P, NT, NH])
        taumu = sb("taumu", [P, D])
        a0 = {n: sem("a0_" + n) for n in (
            "set tau var sd ep xn xnT xT proj vu ge rot rope sq n2 nrm cum s mx mxT diag mb ds e kc v3 EP  qkT_ps qkT "
            "S att st stb O w hc hsq hvar hsd y yT_ps yT op h").split()}
        xn_all = Taker()([P, TILES, D])
        xT_all = Taker(TILES * D)([KC, TILES, 2, P])
        lg = sb("lg", [P, TILES, NE])
        cand = sb("cand", [P, TILES, NE])
        red = sb("red", [P, TILES])
        oh = [sb(f"oh{j}", [P, TILES, NE]) for j in range(2)]
        gate = [sb(f"gate{j}", [P, TILES]) for j in range(2)]
        both = sb("both", [P, TILES, NE])
        tot = sb("tot", [P, NE * TILES])
        inc = sb("inc", [P, NE * TILES])
        pos = sb("pos", [P, TILES, NE])
        cmp = sb("cmp", [P, NB * NE])
        nblk = sb("nblk", [P, NE])
        bend = sb("bend", [P, NE])
        basee = sb("basee", [P, NE])
        onee = sb("onee", [P, NE])
        eb = sb("eb", [P, NB])
        eb_i = sb("eb_i", [P, NB], I32)
        slot = sb("slot", [P, TILES, 2])
        slot_i = sb("slot_i", [P, TILES * 2], I32)
        part_i = sb("part_i", [P, TILES * 2], I32)
        s_blk = sb("s_blk", [P, TILES * 2])
        s_row = sb("s_row", [P, TILES * 2])
        row_hot = [sb(f"row_hot{i}", [P, 128]) for i in range(4)]
        blk_hot = [sb(f"blk_hot{i}", [P, NB]) for i in range(4)]
        idx = sb("idx", [128, NB], I32)
        r = {n: sem("r_" + n) for n in "sd xn add xnT xT lg lg_ps out hot ids both rank idx ready  exp".split()}
        idx_now = [sb(f"idx_now{i}", [128, 1], I32) for i in range(UNROLL)]
        x_blk = [moe_buf([128, D]) for i in range(UNROLL)]
        e_w1 = [moe_buf([KC + 1, 2, FF]) for i in range(UNROLL)]
        e_w2 = [moe_buf([128, FC, D]) for i in range(UNROLL)]
        e_b2 = [moe_buf([128, D]) for i in range(UNROLL)]
        xgT = moe_buf([KC + 1, 2, BLK])
        hT = [moe_buf([128, FC, BLK]) for i in range(UNROLL)]
        yb = [moe_buf([128, D]) for i in range(UNROLL)]
        m_x = [sem(f"m_x{i}") for i in range(UNROLL)]
        m_w1 = [sem(f"m_w1_{i}") for i in range(UNROLL)]
        m_w2 = [sem(f"m_w2_{i}") for i in range(UNROLL)]
        m_out = [sem(f"m_out{i}") for i in range(UNROLL)]
        m = {n: sem("m_" + n) for n in "xgT_ps xgT hid hT y_ps y".split()}
        slot_now = sb("slot_now", [P, 2 * NT], I32)
        yg = a1_buf([P, 2, NT, D])
        xz = [a1_buf([P, NT, 2, D]) for _ in range(2)]
        xzT = a1_buf([KC + 1, NT, 4, P])
        v1 = [a1_buf([P, NT, NH, HD + 1]) for _ in range(2)]
        ge1 = a1_buf([P, NT, D])
        kg = a1_buf([P, NT, D])
        relu = a1_buf([P, NT, 2 * D])
        st1 = sb("st1", [128, 3, 4 * (HD + 1)])
        den = sb("den", [P, NH])
        y1T = sb("y1T", [KC + 1, NT, 2, P])
        a1 = {n: sem("a1_" + n) for n in (
            "yg cmb var sd xn zn xzT_ps xzT proj v ge eq kg ek q_ft k_ft qkT_ps qkT S att st stb O w yT_ps yT op h").split()}
        w_in_q = sb("w_in_q", [KC, 2, 2 * HID], BF16)
        w_out_q = sb("w_out_q", [128, 4, D], BF16)
        identb = sb("identb", [128, 128], BF16)
        zeros = sb("zeros", [128, 512], BF16)
        eps6 = sb("eps6", [128, 1])
        wsum = sb("wsum", [128, 2])
        wscale = sb("wscale", [128, 2])
        wback = sb("wback", [128, 2])
        ssq = sb("ssq", [P, 2, NT])
        rms = sb("rms", [P, 2, NT])
        amax = sb("amax", [P, 2, NT])
        top = sb("top", [P, 2, NT])
        qs = sb("qs", [P, 2, NT])
        back = sb("back", [P, 2, NT])
        xg = [ffn_buf([P, NT, D]) for _ in range(2)]
        xs = ffn_buf([P, NT, D])
        xq = sb("xq", [P, NT, D], BF16)
        xqT = sb("xqT", [KC, NT, 2, P], BF16)
        sil = ffn_buf([P, NT, HID])
        yf = ffn_buf([P, NT, HID])
        yg2 = [ffn_buf([P, NT, HID]) for _ in range(2)]
        ys = ffn_buf([P, NT, HID])
        sqx = ffn_buf([P, NT, D])
        sqy = ffn_buf([P, NT, HID])
        yq = sb("yq", [P, NT, HID], BF16)
        yqT = sb("yqT", [128, NT, 4, P], BF16)
        fo = ffn_buf([P, NT, D])
        f = {n: sem("f_" + n) for n in (
            "wbc wq var sd rs xn xg sq rms ax sc xs x1 xq_ xqT_ps xqT gu sil y z sq2 rms2 ys y1 yq yqT_ps yqT st o out").split()}
        dve_chain, pool_chain = sem("dve_chain"), sem("pool_chain")
        dve_turns = [sem(f"dve_turns{i}") for i in range(3)]

        def bf16_tiles(i, n):
            return bank[i][:, :].bitcast(BF16)[:, 0:n * (P + 1)].rearrange("p (a l) -> p a l", a=n)

        block = ctx.enter_context(nc.Block())

        def all_loaded(eng, stage):
            eng.wait_ge(loaded[stage], 16 * len(plan[stage]))

        def stand_alone(eng):
            eng.sem_inc(turns_passed, 1)

        @block.sync
        def _(sp):
            for stage in plan:
                for dst, src in plan[stage]:
                    sp.dma_start(dst, src).then_inc(loaded[stage], 16)
            for b in range(B):
              sp.wait_ge(r["xn"], 3 * b + 3)
              sp.dma_start(xn_dram[b * L:b * L + L, :].rearrange("(t p) d -> p t d", p=P),
                           xn_all[:, NT * b:NT * b + NT, :]).then_inc(r["out"], 16)

            sp.wait_ge(r["exp"], 1)
            sp.wait_ge(r["add"], 1)
            sp.wait_ge(r["out"], 16 * B)

            def store(n, s):
              sp.dma_start(y_dram[bass.ds(n * BLK, BLK), :], yb[s][:, :]).then_inc(m_out[s], 16)

            def load_w1(n, s):
              e = sp.value_load(eb_i[0:1, bass.ds(n, 1)], min_val=0, max_val=NE - 1)
              sp.dma_start(e_w1[s][0:KC, :, :], dram["e_w1"][bass.ds(e, 1)].rearrange("e p k f -> (e p) k f")).then_inc(m_w1[s], 16)
              sp.dma_start(e_w1[s][KC:KC + 1, 1, :], dram["e_b1"][bass.ds(e, 1)].rearrange("e p f -> (e p) f")).then_inc(m_w1[s], 16)

            def load_w2(n, s):
              e = sp.value_load(eb_i[0:1, bass.ds(n, 1)], min_val=0, max_val=NE - 1)
              sp.dma_start(e_w2[s][:, :, :], dram["e_w2"][bass.ds(e, 1)].rearrange("e p k f -> (e p) k f")).then_inc(m_w2[s], 16)
              sp.dma_start(e_b2[s][:, :], dram["e_b2"][bass.ds(e, 1)].rearrange("e p f -> (e p) f").to_broadcast([128, D])).then_inc(m_w2[s], 16)

            for s in range(UNROLL):
              load_w1(s, s)
              load_w2(s, s)

            def blocks(i, first):
              for s in range(UNROLL):
                  n = UNROLL * i + s
                  sp.wait_ge(m["hid"], 2 * n + 2)
                  load_w1(n + UNROLL, s)
                  if not (first and s == 0):
                      out_and_w2(n - 1, (s - 1) % UNROLL)

            def out_and_w2(n, s):
              sp.wait_ge(m["y"], n + 1)
              store(n, s)
              load_w2(n + UNROLL, s)
            Chain(sp, None).loop(NB // UNROLL - 1, blocks)
            out_and_w2(NB - UNROLL - 1, UNROLL - 1)
            for s in range(UNROLL):
              sp.wait_ge(m["y"], NB - UNROLL + s + 1)
              store(NB - UNROLL + s, s)
            def ffn(b, first):
              sp.wait_ge(f["o"], 3 * b + 3)
              sp.dma_start(out[bass.ds(b, 1)].rearrange("b (t p) d -> p (b t) d", p=P), fo[:, :, :]).then_inc(f["out"], 16)
            Chain(sp, None).loop(B, ffn)
            sp.wait_ge(f["out"], 16 * B)

        @block.gpsimd
        def _(pool):
            all_loaded(pool, "tok")
            for half in range(2):
                for j in range(GP):
                    pool.indirect_dma_start(g0[:, half, j, :], None, dram["patches0"],
                                            bass.IndirectOffsetOnAxis(ap=idx0[:, half, j:j + 1], axis=0)
                                            ).then_inc(gathered, 16)
                pool.indirect_dma_start(g2[:, half, :], None, dram["patches2"],
                                        bass.IndirectOffsetOnAxis(ap=idx2[:, half:half + 1], axis=0)
                                        ).then_inc(gathered, 16)
            for j in range(GP // 2):
                pool.indirect_dma_start(g1[:, j, :], None, dram["patches1"],
                                        bass.IndirectOffsetOnAxis(ap=idx1[:, j:j + 1], axis=0)
                                        ).then_inc(gathered, 16)
            pool.sem_inc(warm, 1)

            def attn0(A, Bk, C):
                if Bk:
                    b, par = Bk
                    for t in range(NT):
                        if t == 0:
                            pool.wait_ge(a0["kc"], b + 1)
                            need(pool, a0["O"], 3 * b - 3)
                        v = vug[par][:, t, 0:D].rearrange("p (h a d) -> p h a d", h=NH, a=1)
                        nc.gpsimd.tensor_tensor(v3[par][:, t], v.to_broadcast([P, NH, 3, HD]),
                                                kc[:, t].rearrange("p h (c a) -> p h c a", a=1).to_broadcast([P, NH, 3, HD]),
                                                ALU.mult).then_inc(a0["v3"], 1)
                        if A and t == 0:
                            rope(A, 0)
                if A:
                    if not Bk:
                        rope(A, 0)
                    rope(A, 1)
                    rope(A, 2)

            def rope(A, t):
                a, par = A
                pool.wait_ge(a0["rot"], 3 * a + t + 1)
                if t == 0:
                    need(pool, a0["st"], 2 * a - 2)
                    need(pool, a0["sq"], 3 * a - 3)
                nc.gpsimd.tensor_tensor(qk[par][:, t, :, 0:HD], rot1[:, t].rearrange("p (h d) -> p h d", d=HD),
                                        rot2[:, t].rearrange("p (h d) -> p h d", d=HD), ALU.add).then_inc(a0["rope"], 1)
            pipeline(pool, attn0, 1)
            chain = Chain(pool, pool_chain)
            pool.wait_ge(r["xn"], TILES)
            nc.gpsimd.tensor_tensor(h[:, :], h[:, :], xn_all[:, :, :].rearrange("p n d -> p (n d)"), ALU.add).then_inc(r["add"], 1)
            pool.wait_ge(r["idx"], 1)
            pool.wait_ge(r["out"], 16 * B)

            def blocks(i, first):
                for s in range(UNROLL):
                    n = UNROLL * i + s
                    if not first:
                        pool.wait_ge(m["xgT_ps"], n - UNROLL + 1)
                    chain.link(nc.gpsimd.tensor_copy(idx_now[s][:, :], idx[:, bass.ds(n, 1)]))
                    stand_alone(pool)
                    pool.indirect_dma_start(x_blk[s][:, :], None, xn_dram,
                                            bass.IndirectOffsetOnAxis(ap=idx_now[s][:, :], axis=0)).then_inc(m_x[s], 16)
            chain.loop(NB // UNROLL, blocks)
            for s in range(UNROLL):
                pool.wait_ge(m_out[s], 16 * (NB // UNROLL))

            def rows(b, first):
                if not first:
                    pool.wait_ge(a1["yg"], 16 * 6 * b)
                chain.link(nc.gpsimd.tensor_copy(slot_now[:, :], slot_i[:, bass.ds(b * 2 * NT, 2 * NT)]))
                stand_alone(pool)
                for t in range(NT):
                    for j in range(2):
                        pool.indirect_dma_start(yg[:, j, t, :], None, y_dram, bass.IndirectOffsetOnAxis(
                            ap=slot_now[:, 2 * t + j:2 * t + j + 1], axis=0)).then_inc(a1["yg"], 16)
                pool.wait_ge(a1["yg"], 16 * 6 * b + 96)
                stand_alone(pool)
                for j in range(2):
                    g = gate[j][:, bass.ds(NT * b, NT)].rearrange("p (t a) -> p t a", a=1).to_broadcast([P, NT, D])
                    chain.step(nc.gpsimd.tensor_tensor(yg[:, j], yg[:, j], g, ALU.mult))
                chain.wait(chain.k)
                for j in range(2):
                    stand_alone(pool)
                    rows_h = tile_of(h, NT * b, NT)
                    chain.link(nc.gpsimd.tensor_tensor(rows_h, rows_h, yg[:, j].rearrange("p t d -> p (t d)"), ALU.add))
                pool.sem_inc(a1["cmb"], 1)
            chain.loop(B, rows)

            def ffn(Z, A, Bk, C):
                for t in range(NT):
                    if A:
                        a, pa = A
                        pool.wait_ge(f["xn"], 3 * a + t + 1)
                        need(pool, f["xs"], 3 * a + t - 5)
                        nc.gpsimd.tensor_tensor(xg[pa][:, t], xn[:, t], g_in[:, :], ALU.mult).then_inc(f["xg"], 1)
                for t in range(NT):
                    if Bk:
                        b, par = Bk
                        pool.wait_ge(f["y"], 3 * b + t + 1)
                        need(pool, f["ys"], 3 * b + t - 5)
                        nc.gpsimd.tensor_tensor(yg2[par][:, t], yf[:, t], g_out[:, :], ALU.mult).then_inc(f["z"], 1)
            pipeline(pool, ffn, 2)

        @block.scalar
        def _(act):
            chain = Chain(act, None)
            all_loaded(act, "tok")
            all_loaded(act, "a0")

            act.wait_ge(a0["set"], 1)
            nc.scalar.activation(tau[:, :], tau[:, :], ACT.Exp).then_inc(a0["tau"], 1)

            def tok(A, Bk, C):
                if A:
                    a, _ = A
                    act.wait_ge(tok_xT_ps, a + 1)
                    need(act, tok_y_ps, a)
                    nc.scalar.copy(x02T[:, :], bank[0][0:48, :]).then_inc(tok_xT, 1)
                    nc.scalar.copy(x1T[:, :, :].rearrange("p a t -> p (a t)"), bank[1][0:KC, 0:128]).then_inc(tok_xT, 1)
                if Bk:
                    b, par = Bk
                    act.wait_ge(tok_i_ps, b + 1)
                    for lvl in (1, 2):
                        nc.scalar.activation(catT[par][0:EMB, lvl, :], bank[4][0:EMB, (lvl - 1) * 256:lvl * 256], ACT.Identity,
                                             bias=tok_b[:, lvl:lvl + 1]).then_inc(tok_cat, 1)
                if A:
                    a, pa = A
                    act.wait_ge(tok_y_ps, a + 1)
                    nc.scalar.copy(y1[:, :], bank[3][0:TOK1, 0:EMB]).then_inc(tok_y, 1)
                    nc.scalar.copy(y2[:, :], bank[3][0:TOK2, EMB:2 * EMB]).then_inc(tok_y, 1)
                    need(act, tok_h_ps, a - 1)
                    nc.scalar.activation(catT[pa][0:EMB, 0, :], bank[2][0:EMB, 0:IMG_TOK], ACT.Identity,
                                         bias=tok_b[:, 0:1]).then_inc(tok_cat, 1)
            pipeline(act, tok, 1)

            act.wait_ge(a0["var"], 1)
            nc.scalar.activation(rs0[:, :], mv0[:, :].rearrange("p (n c) -> p n c", c=2)[:, :, 1], ACT.Sqrt, bias=eps5[0:P, 0:1]).then_inc(a0["sd"], 1)

            def attn0(A, Bk, C):
                a, pa = A or (None, None)
                b, par = Bk or (None, None)
                c, _ = C or (None, None)

                def x_T(t):
                    act.wait_ge(a0["xnT"], 3 * a + t + 1)
                    need(act, a0["proj"], 3 * a + t - 2)
                    nc.scalar.copy(xT[:, t].rearrange("p a l -> p (a l)"), bank[6][0:KC, 0:2 * P]).then_inc(a0["xT"], 1)

                def vu(t):
                    act.wait_ge(a0["proj"], 3 * a + t + 1)
                    need(act, a0["v3"], 3 * a - 3)
                    nc.scalar.copy(vug[pa][:, t], bank[5][0:P, 0:2 * D + 2 * NH]).then_inc(a0["vu"], 1)

                def squares(t):
                    act.wait_ge(a0["rope"], 3 * a + t + 1)
                    if t == 0:
                        need(act, a0["n2"], a)
                    nc.scalar.activation(sq[:, t].rearrange("p (h d) -> p h d", d=HD), qk[pa][:, t, :, 0:HD],
                                         ACT.Square).then_inc(a0["sq"], 1)

                def heads_T(k, par_, t, j):
                    act.wait_ge(a0["qkT_ps"], 6 * k + 2 * t + j + 1)
                    need(act, a0["O"], 3 * k + t - 5)
                    nc.scalar.copy(qkT[par_][:, t, 3 * j:3 * j + 3].rearrange("p a t -> p (a t)"),
                                   bank[7][:, 0:333]).then_inc(a0["qkT"], 1)

                if A:
                    x_T(0)
                if Bk:
                    heads_T(b, par, 2, 1)
                if Bk:
                    act.wait_ge(a0["n2"], b + 1)
                    nc.scalar.activation(nrm[:, :], n2[:, :], ACT.Sqrt).then_inc(a0["nrm"], 1)
                if A:
                    vu(0)
                if Bk:
                    act.wait_ge(a0["ds"], b + 1)
                    nc.scalar.activation(es[par][:, :, 0:NH], dsm[:, :, :], ACT.Exp).then_inc(a0["e"], 1)
                    nc.scalar.activation(ge[:, :, :], vug[par][:, :, 2 * D:2 * D + 2 * NH], ACT.Exp, scale=-1.0).then_inc(a0["ge"], 1)
                if A:
                    squares(0)
                    heads_T(a, pa, 0, 0)
                    x_T(1)
                    heads_T(a, pa, 0, 1)
                    vu(1)
                if C:
                    act.wait_ge(a0["hc"], c + 1)
                    nc.scalar.activation(sqh[:, :, :], o3[:, :, :], ACT.Square).then_inc(a0["hsq"], 1)
                if A:
                    squares(1)
                if C:
                    act.wait_ge(a0["hvar"], c + 1)
                    nc.scalar.activation(hr[:, :], hr[:, :], ACT.Sqrt, bias=eps5[0:P, 0:1], scale=1.0 / HD).then_inc(a0["hsd"], 1)
                if A:
                    heads_T(a, pa, 1, 0)
                    x_T(2)
                    heads_T(a, pa, 1, 1)
                if C:
                    for j, (lo, n) in enumerate(PAIRS):
                        act.wait_ge(a0["yT_ps"], 2 * c + j + 1)
                        if j == 0:
                            need(act, a0["op"], 2 * c)
                        nc.scalar.copy(yT[:, lo:lo + n].rearrange("p t a l -> p (t a l)"),
                                       bank[2 + j][0:KC, 0:2 * P * n]).then_inc(a0["yT"], 1)
                if A:
                    vu(2)
                    squares(2)
                    heads_T(a, pa, 2, 0)
            pipeline(act, attn0, 1)

            def ln_sd(sems, b, dst, src, eps):
                act.wait_ge(sems[0], b + 1)
                nc.scalar.activation(dst, src, ACT.Sqrt, bias=eps[0:P, 0:1]).then_inc(sems[1], 1)

            act.wait_ge(a0["var"], 2)
            nc.scalar.activation(rs0[:, :], mv0[:, :].rearrange("p (n c) -> p n c", c=2)[:, :, 1], ACT.Sqrt,
                                 bias=eps5[0:P, 0:1]).then_inc(r["sd"], 1)
            for n in range(0, TILES, 2):
                act.wait_ge(r["xnT"], n // 2 + 1)
                nc.scalar.copy(xT_all[:, n:n + 2].rearrange("p t a l -> p (t a l)"),
                               bank[4 + n // 2 % 4][0:KC, 0:4 * P]).then_inc(r["xT"], 1)
            act.wait_ge(r["lg"], 2)
            nc.scalar.activation(lg[:, :, :], lg[:, :, :], ACT.Exp).then_inc(r["ready"], 1)

            def hidden(i, first):
                for s in range(UNROLL):
                    n = UNROLL * i + s
                    if not first:
                        act.wait_ge(m["y_ps"], n - UNROLL + 1)
                    for j in range(2):
                        act.wait_ge(m["hid"], 2 * n + j + 1)
                        nc.scalar.activation(hT[s][:, 3 * j:3 * j + 3, :].rearrange("p c t -> p (c t)"),
                                             bank[2 * s + j][:, 0:384], ACT.Gelu).then_inc(m["hT"], 1)
            chain.loop(NB // UNROLL, hidden)

            def attn1(Z, A, Bk, C):
                a, pa = A or (None, None)
                z, _ = Z or (None, None)

                def heads_T(k, par, t, j):
                    act.wait_ge(a1["qkT_ps"], 6 * k + 2 * t + j + 1)
                    need(act, a1["O"], 3 * k + t - 5)
                    nc.scalar.copy(qkT[par][:, t, 3 * j:3 * j + 3].rearrange("p a t -> p (a t)"),
                                   bank[7][:, 0:333]).then_inc(a1["qkT"], 1)

                def relu_exp(src, t, lo, sem_, used):
                    need(act, used, 3 * a + t - 2)
                    nc.scalar.activation(relu[:, t, lo:lo + D], src, ACT.Relu).then_inc(sem_, 1)
                    nc.scalar.activation(rot1[:, t, lo:lo + D], src, ACT.Exp).then_inc(sem_, 1)

                for j in range(NT):
                    n, par, t, out_tile, done = slot_tiles(j, Bk, C)
                    if A:
                        act.wait_ge(a1["xzT_ps"], 3 * a + j + 1)
                        need(act, a1["proj"], 6 * a + 2 * j - 4)
                        nc.scalar.copy(xzT[0:KC, j, 0:2].rearrange("p a l -> p (a l)"), bank[6][0:KC, 0:2 * P]).then_inc(a1["xzT"], 1)
                        for k in range(2):
                            nc.scalar.activation(xzT[0:KC, j, 2 + k], bank[6][0:KC, P * (2 + k):P * (3 + k)], ACT.Identity,
                                                 scale=a1_ln[:, k, 0:1], bias=a1_ln[:, k, 1:2]).then_inc(a1["xzT"], 1)
                    if j == 0 and Bk:
                        heads_T(*Bk, 2, 1)
                    if j and A:
                        heads_T(a, pa, j - 1, 1)
                    if done is not None:
                        act.wait_ge(a1["yT_ps"], done + 1)
                        need(act, a1["op"], done - 2)
                        nc.scalar.copy(y1T[0:KC, out_tile].rearrange("p a l -> p (a l)"), bank[6][0:KC, 0:2 * P]).then_inc(a1["yT"], 1)
                    if A:
                        act.wait_ge(a1["proj"], 6 * a + 2 * j + 1)
                        relu_exp(bank[4][0:P, 0:D], j, 0, a1["eq"], a1["q_ft"])
                        act.wait_ge(a1["proj"], 6 * a + 2 * j + 2)
                        need(act, a1["kg"], 3 * a + j - 2)
                        nc.scalar.activation(ge1[:, j], bank[5][0:P, D:2 * D], ACT.Exp, scale=-1.0).then_inc(a1["ge"], 1)
                        need(act, a1["O"], 3 * a + j - 5)
                        need(act, a1["st"], 2 * a - 2)
                        nc.scalar.copy(v1[pa][:, j, :, 0:HD], bank[5][0:P, 0:D].rearrange("p (h d) -> p h d", d=HD)).then_inc(a1["v"], 1)
                        act.wait_ge(a1["kg"], 3 * a + j + 1)
                        relu_exp(kg[:, j], j, D, a1["ek"], a1["k_ft"])
                    if Z and j == 0:
                        ln_sd((a1["var"], a1["sd"]), 2 * z, sd[:, :], mv[:, :, 1], eps5)
                    if Z and j == 1:
                        ln_sd((a1["var"], a1["sd"]), 2 * z + 1, sd[:, :], mv[:, :, 1], eps5)
                    if A:
                        heads_T(a, pa, j, 0)
            pipeline(act, attn1, 2)

            def ffn(Z, A, Bk, C):
                a, pa = A or (None, None)
                b, par = Bk or (None, None)
                c, pc = C or (None, None)
                if A:
                    ln_sd((f["var"], f["sd"]), a, sd[:, :], mv[:, :, 1], eps5)
                if Bk:
                    act.wait_ge(f["sq"], 3 * b + 3)
                    need(act, f["sc"], b)
                    nc.scalar.activation(rms[:, 0, :], ssq[:, 0, :], ACT.Sqrt, bias=eps6[0:P, 0:1], scale=1.0 / D).then_inc(f["rms"], 1)
                if C:
                    act.wait_ge(f["sq2"], 3 * c + 3)
                    act.wait_ge(f["sc"], c + 1)
                    nc.scalar.activation(rms[:, 1, :], ssq[:, 1, :], ACT.Sqrt, bias=eps6[0:P, 0:1], scale=1.0 / HID).then_inc(f["rms2"], 1)
                if Bk or C:
                    act.wait_ge(f["sc"], (b if Bk else c + 1) + 1)
                for t in range(NT):
                    if Bk:
                        need(act, f["xq_"], 3 * b + t - 2)
                        nc.scalar.activation(xs[:, t], xg[par][:, t], ACT.Copy, scale=qs[:, 0, t:t + 1]).then_inc(f["xs"], 1)
                    if C:
                        need(act, f["yq"], 3 * c + t - 2)
                        nc.scalar.activation(ys[:, t], yg2[pc][:, t], ACT.Copy, scale=qs[:, 1, t:t + 1]).then_inc(f["ys"], 1)
                    if Bk and t:
                        x_T(b, t - 1)
                if Bk:
                    x_T(b, 2)
                for t in range(NT):
                    if Bk:
                        act.wait_ge(f["gu"], 3 * b + t + 1)
                        need(act, f["y"], 3 * b + t - 2)
                        nc.scalar.activation(sil[:, t], bank[2 * (t % 2) + 1][0:P, :], ACT.Silu, scale=back[:, 0, t:t + 1]).then_inc(f["sil"], 1)
                    if C:
                        act.wait_ge(f["yqT_ps"], 3 * c + t + 1)
                        need(act, f["st"], 3 * c + t - 2)
                        nc.scalar.copy(yqT[:, t], bf16_tiles(7 if t % 2 == 0 else 5, 4)[:, :, 0:P]).then_inc(f["yqT"], 1)
                for t in range(NT):
                    if A:
                        act.wait_ge(f["xn"], 3 * a + t + 1)
                        nc.scalar.activation(sqx[:, t], xn[:, t], ACT.Square, accum_out=ssq[:, 0, t:t + 1]).then_inc(f["sq"], 1)
                for t in range(NT):
                    if Bk:
                        act.wait_ge(f["y"], 3 * b + t + 1)
                        nc.scalar.activation(sqy[:, t], yf[:, t], ACT.Square, accum_out=ssq[:, 1, t:t + 1]).then_inc(f["sq2"], 1)

            def x_T(b, t):
                act.wait_ge(f["xqT_ps"], 3 * b + t + 1)
                need(act, f["gu"], 3 * b + t - 2)
                nc.scalar.copy(xqT[:, t], bf16_tiles(6, 2)[0:KC, :, 0:P]).then_inc(f["xqT"], 1)
            pipeline(act, ffn, 2)

        @block.tensor
        def _(pe):
            mm = nc.tensor.matmul

            def keep_busy(i, n, count, rows=128, start=False):
                for _ in range(count):
                    mm(bank[i][0:rows, 512 - n:512], zeros[:, 0:rows], zeros[:, 0:n], start=start, stop=True, skip_group_check=True)
            pe.wait_ge(f["wq"], 2)
            all_loaded(pe, "tok")
            mm(bank[0][:, 0:1], ones[0:KC, :], wsum[0:KC, 0:1], start=True, stop=True)
            mm(bank[0][:, 1:2], ones[:, :], wsum[:, 1:2], start=True, stop=True).then_inc(f["wbc"], 1)
            pe.wait_ge(f["wq"], 3)
            all_loaded(pe, "tok")

            pe.wait_ge(a0["tau"], 4)

            pe.wait_ge(warm, 2)
            keep_busy(6, 512, WARM_UP, start=True)

            def tok(A, Bk, C):
                if A:
                    a, pa = A
                    pe.wait_ge(tok_staged, 3 * a + 3)
                    need(pe, tok_xT, 2 * a)
                    stand_alone(pe)
                    for half in range(2):
                        nc.tensor.transpose(bank[0][0:48, 128 * half:128 * half + 128], x0[:, half, :], ident[:, :])
                        nc.tensor.transpose(bank[0][0:48, 256 + 128 * half:384 + 128 * half], x2[:, half, :], ident[:, :])
                    nc.tensor.transpose(bank[1][0:KC, 0:2 * TOK1], x1[:, :], ident[:, :]).then_inc(tok_xT_ps, 1)
                if Bk:
                    b, par = Bk
                    pe.wait_ge(tok_y, 2 * b + 2)
                    need(pe, tok_cat, 3 * b)
                    stand_alone(pe)
                    mm(bank[4][0:EMB, 0:256], y1[:, :], interp1[:, :], start=True, stop=True)
                    mm(bank[4][0:EMB, 256:512], y2[:, :], interp2[:, :], start=True, stop=True).then_inc(tok_i_ps, 1)
                if A:
                    pe.wait_ge(tok_xT, 2 * a + 2)
                    need(pe, tok_cat, 3 * a - 2)
                    stand_alone(pe)
                    mm(bank[2][0:EMB, 0:IMG_TOK], w0[:, :], x02T[:, 0:256], start=True, stop=True)
                    for k in range(2):
                        mm(bank[3][0:TOK1, 0:EMB], x1T[:, k, :], w1[:, k, :], start=(k == 0), stop=(k == 1))
                    x2v = x02T[:, 256:512].rearrange("p (t j) -> p t j", j=GP)
                    for j in range(GP):
                        last = mm(bank[3][0:TOK2, EMB:2 * EMB], x2v[:, :, j], w2[:, j, :], start=(j == 0), stop=(j == GP - 1))
                        if j % 4 == 1:
                            keep_busy(3, 384, 1, rows=TOK1)
                    last.then_inc(tok_y_ps, 1)
                if Bk:
                    pe.wait_ge(tok_cat, 3 * b + 3)
                    need(pe, h_tok, 2 * b)
                    stand_alone(pe)
                    for t in range(NT):
                        n = P if t < 2 else IMG_TOK - 2 * P
                        dst = bank[5][0:P, D * t:D * t + D] if t < 2 else bank[6][0:n, 0:D]
                        for c in range(3):
                            rows = EMB + c // 2
                            last = mm(dst, catT[par][0:rows, c, P * t:P * t + n], wf[0:rows, c, :], start=(c == 0), stop=(c == 2))
                    last.then_inc(tok_h_ps, 1)
            pipeline(pe, tok, 1)
            chain = Chain(pe, None)

            all_loaded(pe, "a0")
            pe.wait_ge(a0["tau"], 4)
            pe.wait_ge(h_tok, 2 * B)

            def scores(sems, b, par, t, lo, hi):
                for i in range(lo, hi):
                    if i >= 2:
                        pe.wait_ge(sems["att"], 12 * b + 4 * t + i - 1)
                    for g in range(3):
                        last = mm(bank[i % 2][0:P, P * g:P * g + P], qkT[par][32 * i:32 * i + 32, t, 3 + g, :],
                                  qkT[par][32 * i:32 * i + 32, t, g, :], start=True, stop=True, tile_position=(32 * i, 0))
                    last.then_inc(sems["S"], 1)

            def heads_T(sems, a, pa, t, j):
                if j == 0:
                    need(pe, sems["qkT"], 6 * a + 2 * t)
                else:
                    pe.wait_ge(sems["qkT"], 6 * a + 2 * t + 1)
                for g in range(3):
                    last = nc.tensor.transpose(bank[7][:, P * g:P * g + P],
                                               qk[pa][:, t, NH * j + 4 * g:NH * j + 4 * g + 4].rearrange("p h d -> p (h d)"),
                                               ident[0:P, 0:P])
                last.then_inc(sems["qkT_ps"], 1)

            def pair_transposes(src, done, first_bank):
                for t in range(NT):
                    for k in range(2):
                        dst = bank[first_bank + t // 2][0:KC, 2 * P * (t % 2) + P * k:2 * P * (t % 2) + P * k + P]
                        last = nc.tensor.transpose(dst, src[:, t, KC * k:KC * k + KC], ident[0:P, 0:P])
                    if t:
                        last.then_inc(done, 1)

            def attn0(A, Bk, C):
                a, pa = A or (None, None)
                b, par = Bk or (None, None)
                c, pc = C or (None, None)

                def tile_T(t):
                    pe.wait_ge(a0["xn"], 3 * a + t + 1)
                    need(pe, a0["s"], 3 * a + t)
                    for k in range(2):
                        last = nc.tensor.transpose(bank[6][0:KC, P * k:P * k + P], xn[:, t, KC * k:KC * k + KC], ident[0:P, 0:P])
                    last.then_inc(a0["xnT"], 1)

                def proj(t, j):
                    if j == 0:
                        pe.wait_ge(a0["xT"], 3 * a + t + 1)
                        need(pe, a0["rot"], 3 * a + t)
                    else:
                        need(pe, a0["vu"], 3 * a + t)
                    lo, n = ((0, 384), (384, 408))[j]
                    for k in range(2):
                        last = mm(bank[4 + j][0:P, 0:n], xT[:, t, k, :], a0_w[:, k, lo:lo + n], start=(k == 0), stop=(k == 1))
                    if j:
                        last.then_inc(a0["proj"], 1)

                def cum(t):
                    pe.wait_ge(a0["vu"], 3 * a + t + 1)
                    mm(bank[6][0:P, 0:D], ones[0:1, 0:P], taumu[0:1, :], start=True, stop=False)
                    for s in range(t):
                        mm(bank[6][0:P, 0:D], ones[0:P, 0:P], vug[pa][:, s, D:2 * D], start=False, stop=False)
                    mm(bank[6][0:P, 0:D], tri[:, :], vug[pa][:, t, D:2 * D], start=False, stop=True).then_inc(a0["cum"], 1)

                def q_T(t):
                    pe.wait_ge(a0["rope"], 3 * a + t + 1)
                    if t == 0:
                        need(pe, a0["ep"], a)
                    heads_T(a0, a, pa, t, 0)

                def chunk(b, par, t):
                    need(pe, a0["w"], 3 * b + t)
                    pe.wait_ge(a0["v3"], 3 * b + t + 1)
                    if t == 1:
                        need(pe, a0["h"], 2 * b)
                    for g in range(3):
                        if t:
                            mm(bank[2 + g // 2][0:P, 192 * (g % 2):192 * (g % 2) + 192], qkT[par][:, t, g, :], stb[:, g, :],
                               start=(g != 1), stop=False, skip_group_check=True)
                    for i in range(4):
                        pe.wait_ge(a0["att"], 12 * b + 4 * t + i + 1)
                        for g in range(3):
                            at = 192 * (g % 2) + 48 * i
                            last = mm(bank[2 + g // 2][0:P, at:at + 48], att[:, 4 * g + i, :],
                                      v3[par][:, t, 4 * g + i].rearrange("p c d -> p (c d)"),
                                      start=(t == 0 and i == 0 and g != 1), stop=True, skip_group_check=True)
                    last.then_inc(a0["O"], 1)
                    if t < 2:
                        for g in range(3):
                            for s in range(t + 1):
                                last = mm(bank[g // 2][:, 192 * (g % 2):192 * (g % 2) + 192],
                                          qk[par][:, s, NH + 4 * g:NH + 4 * g + 4].rearrange("p h d -> p (h d)"),
                                          v3[par][:, s, 4 * g:4 * g + 4].rearrange("p h c d -> p (h c d)"),
                                          start=(s == 0), stop=(s == t))
                        last.then_inc(a0["st"], 1)

                for j in range(NT):
                    n, q, t = (c, pc, 2) if j == 0 else (b, par, j - 1)
                    if A:
                        tile_T(j)
                    if n is not None:
                        if t:
                            pe.wait_ge(a0["stb"], 2 * n + t)
                        else:
                            need(pe, a0["att"], 12 * n)
                            pe.wait_ge(a0["qkT"], 6 * n + 6)
                        scores(a0, n, q, t, 0, 2)
                    if j == 0 and Bk:
                        heads_T(a0, b, par, 2, 1)
                    if j and A:
                        heads_T(a0, a, pa, j - 1, 1)
                    if A:
                        proj(j, 0)
                    if j == 2 and C:
                        pe.wait_ge(a0["y"], c + 1)
                        pe.wait_ge(a0["w"], 3 * c + (4 if Bk else 3))
                        pair_transposes(o3, a0["yT_ps"], 2)
                    if j == 0 and Bk:
                        pe.wait_ge(a0["mx"], b + 1)
                        pe.wait_ge(a0["qkT"], 6 * b + 6)
                        nc.tensor.transpose(bank[7][0:NH, 192:192 + P], mx[:, :], ident[0:P, 0:P]).then_inc(a0["mxT"], 1)
                    if A:
                        proj(j, 1)
                    if j == 0 and Bk:
                        pe.wait_ge(a0["diag"], b + 1)
                        mm(bank[7][0:P, 320:332], ones[0:NH, 0:P], diag[:, :], start=True, stop=True).then_inc(a0["mb"], 1)
                    if n is not None:
                        scores(a0, n, q, t, 2, 4)
                    if j == 2 and C:
                        for t2 in range(NT):
                            if t2 != 1:
                                pe.wait_ge(a0["yT"], 2 * c + (1 if t2 == 0 else 2))
                            for k in range(2):
                                last = mm(bank[2 + t2 // 2][0:P, D * (t2 % 2):D * (t2 % 2) + D], yT[:, t2, k, :], a0_wo[:, k, :],
                                          start=(k == 0), stop=(k == 1))
                            if t2:
                                last.then_inc(a0["op"], 1)
                    if A:
                        cum(j)
                    if n is not None:
                        chunk(n, q, t)
                    if j == 0 and Bk:
                        pe.wait_ge(a0["e"], b + 1)
                        for t2 in range(NT):
                            dst = bank[7][0:P, 336 + 24 * t2:360 + 24 * t2]
                            for s in range(t2):
                                mm(dst, ones[0:P, 0:P], es[par][:, s, :], start=(s == 0), stop=False)
                            last = mm(dst, tri[:, :], es[par][:, t2, :], start=(t2 == 0), stop=True)
                        last.then_inc(a0["EP"], 1)
                    if A:
                        q_T(j)
            pipeline(pe, attn0, 1)

            pe.wait_ge(a0["yT"], 2 * B)
            pe.wait_ge(a0["h"], 2 * B)

            def logits(n):
                pe.wait_ge(r["xT"], n // 2 + 1)
                for t in (n, n + 1):
                    for k in range(2):
                        last = mm(bank[0][0:P, NE * t:NE * t + NE], xT_all[:, t, k, :], wr[:, k, :], start=(k == 0), stop=(k == 1))
                return last

            for n in range(0, TILES, 2):
                pe.wait_ge(r["xn"], n + 2)
                need(pe, r["xT"], n // 2 - 3)
                for t in range(2):
                    for k in range(2):
                        last = nc.tensor.transpose(bank[4 + n // 2 % 4][0:KC, P * (2 * t + k):P * (2 * t + k + 1)],
                                                   xn_all[:, n + t, KC * k:KC * k + KC], ident[0:P, 0:P])
                last.then_inc(r["xnT"], 1)
                if n >= 4:
                    logits(n - 4)
            logits(TILES - 4)
            logits(TILES - 2).then_inc(r["lg_ps"], 1)
            pe.wait_ge(r["both"], 1)
            mm(bank[0][0:P, 0:TILES * NE], tri_strict[:, :], both[:, :, :].rearrange("p t e -> p (t e)"), start=True, stop=True)
            mm(bank[1][0:P, 0:TILES * NE], ones[0:P, 0:P], both[:, :, :].rearrange("p t e -> p (t e)"),
               start=True, stop=True).then_inc(r["rank"], 1)

            def ids(i, first):
                for s in range(4):
                    pe.wait_ge(r["hot"], 8 * i + 2 * s + 2)
                    mm(bank[2][:, 0:NB], row_hot[s][:, :], blk_hot[s][:, :], start=(first and s == 0), stop=True,
                       skip_group_check=True).then_inc(r["ids"], 1)
            chain.loop(TILES * 2 // 4, ids)
            pe.wait_ge(r["idx"], 1)

            def rows_T(n, i, s):
                pe.wait_ge(m_x[s], 16 * i + 16)
                need(pe, m["xgT"], n)
                for k in range(2):
                    last = nc.tensor.transpose(bank[6][0:KC, BLK * k:BLK * k + BLK], x_blk[s][:, KC * k:KC * k + KC], ident[:, :])
                last.then_inc(m["xgT_ps"], 1)

            def hid(n, i, s):
                pe.wait_ge(m["xgT"], n + 1)
                pe.wait_ge(m_w1[s], 32 * i + 32)
                for c in range(FC):
                    for k in range(2):
                        rows = KC + k
                        last = mm(bank[2 * s + c // 3][:, 128 * (c % 3):128 * (c % 3) + BLK],
                                  e_w1[s][0:rows, k, 128 * c:128 * c + 128], xgT[0:rows, k, :], start=(k == 0), stop=(k == 1))
                    if c % 3 == 2:
                        last.then_inc(m["hid"], 1)

            def back_to_d(n, i, s, started):
                pe.wait_ge(m_w2[s], 32 * i + 32)
                if started:
                    pe.wait_ge(m["y"], n)
                for c in range(FC):
                    if c % 3 == 0:
                        pe.wait_ge(m["hT"], 2 * n + c // 3 + 1)
                    last = mm(bank[7][:, 0:D], hT[s][:, c, :], e_w2[s][:, c, :], start=(c == 0), stop=(c == FC - 1))
                last.then_inc(m["y_ps"], 1)

            def blocks(i, first, last=False):
                for s in range(UNROLL):
                    n = UNROLL * i + s
                    hid(n, i, s)
                    if not (last and s == UNROLL - 1):
                        rows_T(n + 1, i + (s + 1) // UNROLL, (s + 1) % UNROLL)
                    if not (first and s == 0):
                        back_to_d(n - 1, i if s else i - 1, (s - 1) % UNROLL, not (first and s == 1))
            rows_T(0, 0, 0)
            chain.loop(NB // UNROLL - 1, blocks)
            blocks(NB // UNROLL - 1, False, last=True)
            back_to_d(NB - 1, NB // UNROLL - 1, UNROLL - 1, True)
            pe.wait_ge(m["y"], NB)

            def attn1(Z, A, Bk, C):
                a, pa = A or (None, None)
                W = 4 * (HD + 1)

                def proj(t, lo, cols):
                    for dst, at, w, w_lo, n in cols:
                        for k in range(2):
                            last = mm(dst, xzT[0:KC + k, t, at + k], w[0:KC + k, k, w_lo:w_lo + n], start=(k == 0), stop=(k == 1))
                    last.then_inc(a1["proj"], 1)

                for j in range(NT):
                    n, par, t, out_tile, done = slot_tiles(j, Bk, C)
                    if A:
                        pe.wait_ge(a1["zn"], 3 * a + j + 1)
                        if Bk:
                            need(pe, a1["h"], 3 * Bk[0] + j - 2)
                        for s in range(4):
                            last = nc.tensor.transpose(bank[6][0:KC, P * s:P * s + P],
                                                       xz[pa][:, j, s // 2, KC * (s % 2):KC * (s % 2) + KC], ident[0:P, 0:P])
                        last.then_inc(a1["xzT_ps"], 1)
                    if n is not None:
                        pe.wait_ge(a1["qkT"], 6 * n + 2 * t + 2)
                        scores(a1, n, par, t, 0, 2)
                    if j == 0 and Bk:
                        pe.wait_ge(a1["k_ft"], 3 * Bk[0] + 3)
                        heads_T(a1, *Bk, 2, 1)
                    if j and A:
                        pe.wait_ge(a1["k_ft"], 3 * a + j)
                        heads_T(a1, a, pa, j - 1, 1)
                    if A:
                        pe.wait_ge(a1["xzT"], 9 * a + 3 * j + 3)
                        need(pe, a1["eq"], 6 * a + 2 * j)
                        need(pe, a1["kg"], 3 * a + j)
                        proj(j, 0, ((bank[4][0:P, 0:384], 2, a1_w, 0, 384),))
                    if done is not None:
                        pe.wait_ge(a1["w"], done + 1)
                        if not A:
                            need(pe, a1["h"], done)
                        for k in range(2):
                            last = nc.tensor.transpose(bank[6][0:KC, P * k:P * k + P], o3[:, out_tile, KC * k:KC * k + KC], ident[0:P, 0:P])
                        last.then_inc(a1["yT_ps"], 1)
                    if A:
                        need(pe, a1["v"], 3 * a + j)
                        proj(j, 1, ((bank[5][0:P, D:2 * D], 0, a1_wg, 0, D), (bank[5][0:P, 0:D], 2, a1_w, 384, D)))
                    if n is not None:
                        scores(a1, n, par, t, 2, 4)
                    if done is not None:
                        pe.wait_ge(a1["yT"], done + 1)
                        for k in range(2):
                            last = mm(bank[6][0:P, 2 * P:2 * P + D], y1T[0:KC + k, out_tile, k, :], a1_wo[0:KC + k, k, :],
                                      start=(k == 0), stop=(k == 1))
                        last.then_inc(a1["op"], 1)
                    if n is not None:
                        need(pe, a1["w"], 3 * n + t)
                        pe.wait_ge(a1["v"], 3 * n + t + 1)
                        if t:
                            pe.wait_ge(a1["stb"], 2 * n + t)
                            for g in range(3):
                                mm(bank[2][0:P, W * g:W * g + W], qkT[par][:, t, g, :], st1[:, g, :],
                                   start=(g == 0), stop=False, skip_group_check=True)
                        for i in range(4):
                            pe.wait_ge(a1["att"], 12 * n + 4 * t + i + 1)
                            for g in range(3):
                                at = W * g + (HD + 1) * i
                                last = mm(bank[2][0:P, at:at + HD + 1], att[:, 4 * g + i, :], v1[par][:, t, 4 * g + i],
                                          start=(t == 0 and i == 0 and g == 0), stop=True, skip_group_check=True)
                            if i < 3:
                                keep_busy(2, 512 - 3 * W, 2)
                        last.then_inc(a1["O"], 1)
                        if t < 2:
                            if t == 0:
                                need(pe, a1["stb"], 2 * n)
                            for g in range(3):
                                last = mm(bank[3][:, W * g:W * g + W],
                                          qk[par][:, t, NH + 4 * g:NH + 4 * g + 4].rearrange("p h d -> p (h d)"),
                                          v1[par][:, t, 4 * g:4 * g + 4].rearrange("p h d -> p (h d)"),
                                          start=(t == 0 and g == 0), stop=True, skip_group_check=True)
                            last.then_inc(a1["st"], 1)
                    if A:
                        pe.wait_ge(a1["q_ft"], 3 * a + j + 1)
                        heads_T(a1, a, pa, j, 0)
            pipeline(pe, attn1, 2)
            pe.wait_ge(a1["h"], 3 * B)
            pe.wait_ge(a1["yT"], 3 * B)
            pe.wait_ge(f["wq"], 4)

            def ffn(Z, A, Bk, C):
                b, _ = Bk or (None, None)
                c, _ = C or (None, None)

                def gate_up(t):
                    pe.wait_ge(f["xqT"], 3 * b + t + 1)
                    need(pe, f["y"], (3 * b, 3 * b - 1, 3 * b + 1)[t])
                    for j in range(2):
                        for k in range(2):
                            last = mm(bank[2 * (t % 2) + j][0:P, :], xqT[:, t, k, :], w_in_q[:, k, HID * j:HID * j + HID],
                                      start=(k == 0), stop=(k == 1))
                    last.then_inc(f["gu"], 1)

                for t in range(NT):
                    if Bk:
                        pe.wait_ge(f["xq_"], 3 * b + t + 1)
                        need(pe, f["xqT"], 3 * b + t)
                        tb = bf16_tiles(6, 2)
                        for k in range(2):
                            last = nc.tensor.transpose(tb[0:KC, k, 0:P], xq[:, t, KC * k:KC * k + KC], identb[0:P, 0:P])
                        last.then_inc(f["xqT_ps"], 1)
                        if t:
                            gate_up(t - 1)
                    if C:
                        pe.wait_ge(f["yq"], 3 * c + t + 1)
                        need(pe, f["yqT"], 3 * c if t < 2 else 3 * c + 1)
                        tb = bf16_tiles(7 if t % 2 == 0 else 5, 4)
                        for i in range(4):
                            last = nc.tensor.transpose(tb[:, i, 0:P], yq[:, t, 128 * i:128 * i + 128], identb[0:P, 0:P])
                        last.then_inc(f["yqT_ps"], 1)
                if Bk:
                    gate_up(2)
                for t in range(NT):
                    if C:
                        pe.wait_ge(f["yqT"], 3 * c + t + 1)
                        need(pe, f["o"], 3 * c + t)
                        for i in range(4):
                            last = mm(bank[4][0:P, 0:D], yqT[:, t, i, :], w_out_q[:, i, :], start=(i == 0), stop=(i == 3))
                        last.then_inc(f["st"], 1)
            pipeline(pe, ffn, 2)

        @block.vector
        def _(dve):
            chain = Chain(dve, dve_chain)
            link, v = chain.link, nc.vector
            link(v.memset(eps5[:, :], 1e-5))
            link(v.memset(zeros[:, :], 0.0))
            dve.sem_inc(warm, 1)
            all_loaded(dve, "tok")
            all_loaded(dve, "f")
            v.memset(eps6[:, :], 1e-6)
            chain.step(v.tensor_copy(identb[:, :], ident[:, :]))
            wsets = ((w_in[:, :, :].rearrange("p a n -> p (a n)"), w_in_q[:, :, :].rearrange("p a n -> p (a n)"), KC, D * 2 * HID),
                     (w_out[:, :, :].rearrange("p a n -> p (a n)"), w_out_q[:, :, :].rearrange("p a n -> p (a n)"), 128, D * HID))
            for i, (w, _, rows, _) in enumerate(wsets):
                v.tensor_reduce(wsum[0:rows, i:i + 1], w, AX, ALU.add, apply_absolute_value=True).then_inc(f["wq"], 1)
            dve.wait_ge(f["wbc"], 1)
            for i, (_, _, _, count) in enumerate(wsets):
                k = chain.step(v.tensor_scalar(wback[:, i:i + 1], bank[0][:, i:i + 1], 1.0 / count, 1e-5, ALU.mult, ALU.max))
            chain.wait(k)
            link(v.reciprocal(wscale[:, :], wback[:, :]))
            for i, (w, wq, rows, _) in enumerate(wsets):
                link(v.tensor_scalar(w, w, wscale[0:rows, i:i + 1], MAGIC, ALU.mult, ALU.add))
                link(v.tensor_scalar(w, w, MAGIC, -1.0, ALU.subtract, ALU.max))
                v.tensor_scalar(wq, w, 1.0, None, ALU.min).then_inc(f["wq"], 1)
            link(v.memset(amax[:, :, :], 1.0))
            link(v.memset(rms[:, :, :], 1.0))

            all_loaded(dve, "a0")
            link(v.memset(qk[0][:, :, :, :], 0.0))
            link(v.memset(qk[1][:, :, :, :], 0.0))
            link(v.tensor_scalar(tau[:, :], tau[:, :], -50.0, 30.0, ALU.max, ALU.min))
            dve.sem_inc(a0["set"], 1)
            dve.wait_ge(a0["tau"], 1)
            v.tensor_tensor(taumu[:, :].rearrange("p (h d) -> p h d", d=HD), mu[:, :].rearrange("p (h d) -> p h d", d=HD),
                            tau[:, :].rearrange("p (h a) -> p h a", a=1).to_broadcast([P, NH, HD]), ALU.mult).then_inc(a0["tau"], 1)
            v.reciprocal(it[:, :], time[:, :]).then_inc(a0["tau"], 1)

            def b3(ap2, shape, axis):
                pat = {2: "p (h a) -> p h a", 1: "p (a h) -> p a h"}[axis]
                return ap2.rearrange(pat, a=1).to_broadcast(shape)

            link(v.tensor_tensor(rt[:, :, :], b3(time[:, :], [P, NT, NH], 2), b3(tau[:, :], [P, NT, NH], 1), ALU.add))
            link(v.reciprocal(rt[:, :, :], rt[:, :, :]))
            link(v.tensor_scalar(rt[:, :, :], rt[:, :, :], -1.0 / np.sqrt(HD), None, ALU.mult))
            link(v.memset(catT[0][EMB:EMB + 1, :, :], 1.0))
            v.memset(catT[1][EMB:EMB + 1, :, :], 1.0).then_inc(a0["tau"], 1)

            dve.wait_ge(gathered, 16 * (2 * GP + 2 + GP // 2))

            ch_c = Turns(dve, dve_turns[2], 7)

            def tile_stats(ch, sem_, b):
                dve.wait_ge(sem_, 2 * b + 2)
                stand_alone(dve)
                for t in range(NT):
                    k = ch.step(v.bn_stats(stats[:, t, :], tile_of(h, 3 * b + t)))
                ch.wait(k)
                stand_alone(dve)
                for t in range(NT):
                    k = ch.step(v.bn_aggr(mv[:, t, :], stats[:, t, :]))
                ch.wait(k)
                ch.link(v.tensor_copy(mv0[:, bass.ds(6 * b, 6)], mv[:, :, :].rearrange("p t c -> p (t c)")))

            def tok(A, Bk, C):
                if A:
                    a, _ = A
                    need(dve, tok_xT_ps, a)
                    v.tensor_copy(x0[:, :, :].rearrange("p a (j c) -> p a j c", c=3),
                                  g0[:, :, :, bass.ds(a * 3, 3)]).then_inc(tok_staged, 1)
                    v.tensor_copy(x1[:, :].rearrange("p (j c) -> p j c", c=12),
                                  g1[:, :, bass.ds(a * 12, 12)]).then_inc(tok_staged, 1)
                    v.tensor_copy(x2[:, :, :], g2[:, :, bass.ds(a * 48, 48)]).then_inc(tok_staged, 1)
                if C:
                    c, _ = C
                    ch_c.turn(c)
                    dve.wait_ge(tok_h_ps, c + 1)
                    v.tensor_copy(tile_of(h, 3 * c, 2), bank[5][0:P, 0:2 * D]).then_inc(h_tok, 1)
                    v.tensor_copy(h[0:IMG_TOK - 2 * P, bass.ds((3 * c + 2) * D, D)],
                                  bank[6][0:IMG_TOK - 2 * P, 0:D]).then_inc(h_tok, 1)
                    tile_stats(ch_c, h_tok, c)
            pipeline(dve, tok, 1)
            dve.sem_inc(a0["var"], 1)

            def masks(sems, b, t, lo, hi):
                if lo == 0:
                    need(dve, sems["O"], 3 * b + t)
                for i in range(lo, hi):
                    dve.wait_ge(sems["S"], 12 * b + 4 * t + i + 1)
                    v.tensor_tensor(att[:, :, :].rearrange("p (g i) l -> p i g l", i=4)[:, i],
                                    bank[i % 2][0:P, 0:3 * P].rearrange("p (g l) -> p g l", g=3),
                                    b3(tri[:, :], [P, 3, P], 1), ALU.mult).then_inc(sems["att"], 1)

            dve.wait_ge(a0["sd"], 1)
            link(v.reciprocal(rs0[:, :], rs0[:, :]))
            ch_a, ch_b, ch_c = Turns(dve, dve_turns[0], 15), Turns(dve, dve_turns[1], 23), ch_c.next_phase(B, 14)

            def attn0(Z, A, Bk, C):
                a, pa = A or (None, None)
                b, par = Bk or (None, None)
                c, _ = C or (None, None)
                o = o3[:, :, :].rearrange("p t (h d) -> p (t h) d", d=HD)

                def normalize(a, t):
                    need(dve, a0["xnT"], 3 * a + t - 2)
                    v.tensor_scalar(xn[:, t, :], tile_of(h, 3 * a + t), mv0[:, bass.ds(6 * a + 2 * t, 1)], rs0[:, bass.ds(3 * a + t, 1)],
                                    ALU.subtract, ALU.mult).then_inc(a0["xn"], 1)

                def rotate(t):
                    dve.wait_ge(a0["proj"], 3 * a + t + 1)
                    need(dve, a0["rope"], 3 * a + t - 2)
                    q = bank[4][0:P, 0:384].rearrange("p (h c d) -> p h c d", c=2, d=HD // 2)
                    tab = lambda m, lo, n: m[:, t, lo:lo + n].rearrange("p (a d) -> p a d", a=1).to_broadcast([P, 2 * NH, n])
                    r2 = rot2[:, t].rearrange("p (h c d) -> p h c d", c=2, d=HD // 2)
                    ch_a.step(v.tensor_tensor(rot1[:, t].rearrange("p (h d) -> p h d", d=HD),
                                              bank[4][0:P, 0:384].rearrange("p (h d) -> p h d", d=HD), tab(cos, 0, HD), ALU.mult))
                    ch_a.step(v.tensor_tensor(r2[:, :, 0], q[:, :, 1], tab(sin, 0, 8), ALU.mult))
                    k = ch_a.step(v.tensor_tensor(r2[:, :, 1], q[:, :, 0], tab(sin, 8, 8), ALU.mult))
                    ch_a.wait(k)
                    dve.sem_inc(a0["rot"], 1)

                def surprise(t):
                    dve.wait_ge(a0["cum"], 3 * a + t + 1)
                    if t == 0:
                        need(dve, a0["EP"], a - 1)
                    e = es[pa]
                    ch_a.link(v.tensor_tensor(us[:, :], vug[pa][:, t, D:2 * D], bank[6][0:P, 0:D], ALU.mult))
                    ch_a.link(v.tensor_reduce(e[:, t, NH:2 * NH], us[:, :].rearrange("p (h d) -> p h d", d=HD), AX, ALU.add))
                    v.tensor_tensor(e[:, t, NH:2 * NH], e[:, t, NH:2 * NH], rt[:, t, :], ALU.mult).then_inc(a0["s"], 1)

                def state(ch, n, t):
                    dve.wait_ge(a0["O"], 3 * n + t + 1)
                    dve.wait_ge(a0["st"], 2 * n + t + 1)
                    k = ch.step(v.tensor_tensor(stb[:, 0:2, :], bank[0][:, 0:384].rearrange("p (g n) -> p g n", g=2),
                                                b3(head_mask0[:, :], [128, 2, 192], 1), ALU.mult))
                    ch.wait(k)
                    v.tensor_tensor(stb[:, 2, :], bank[1][:, 0:192], head_mask0[:, :], ALU.mult).then_inc(a0["stb"], 1)

                def weigh(ch, n, t):
                    dve.wait_ge(a0["O"], 3 * n + t + 1)
                    cft = cf[:, t].rearrange("p h (c a) -> p h c a", a=1)
                    k = ch.step(v.tensor_tensor(wo3[:, 0:8], bank[2][0:P, 0:384].rearrange("p (h c d) -> p h c d", c=3, d=HD),
                                                cft[:, 0:8].to_broadcast([P, 8, 3, HD]), ALU.mult))
                    v.tensor_tensor(wo3[:, 8:12], bank[3][0:P, 0:192].rearrange("p (h c d) -> p h c d", c=3, d=HD),
                                    cft[:, 8:12].to_broadcast([P, 4, 3, HD]), ALU.mult).then_inc(a0["w"], 1)
                    return k

                def add_up(ch, n, t, k):
                    ch.wait(k)
                    dve.wait_ge(a0["w"], 3 * n + t + 1)
                    if t == 0:
                        need(dve, a0["yT_ps"], 2 * n)
                    return ch.step(v.tensor_reduce(o3[:, t, :].rearrange("p (h d) -> p h d", d=HD),
                                                   wo3[:, :, :, :].rearrange("p h c d -> p h d c"), AX, ALU.add))

                if A:
                    ch_a.turn(a)
                if Bk:
                    ch_b.turn(b)
                if C:
                    ch_c.turn(c)
                if Bk:
                    dve.wait_ge(a0["s"], 3 * b + 3)
                    v.tensor_reduce(mx[:, :], es[par][:, :, NH:2 * NH].rearrange("p t h -> p h t"), AX, ALU.max).then_inc(a0["mx"], 1)
                if C:
                    kw = weigh(ch_c, c, 1)
                    masks(a0, c, 2, 0, 2)
                    add_up(ch_c, c, 1, kw)
                if Bk:
                    dve.wait_ge(a0["mxT"], b + 1)
                    ch_b.link(v.tensor_reduce(m12[:, :], bank[7][0:NH, 192:192 + P], AX, ALU.max))
                    v.tensor_scalar(diag[:, :], ident[0:NH, 0:NH], m12[:, 0:1], None, ALU.mult).then_inc(a0["diag"], 1)
                    dve.wait_ge(a0["sq"], 3 * b + 3)
                    v.tensor_reduce(n2[:, :], sq[:, :, :].rearrange("p t (h d) -> p (t h) d", d=HD), AX, ALU.add).then_inc(a0["n2"], 1)
                    dve.wait_ge(a0["mb"], b + 1)
                    v.tensor_tensor(dsm[:, :, :], es[par][:, :, NH:2 * NH], b3(bank[7][0:P, 320:332], [P, NT, NH], 1),
                                    ALU.subtract).then_inc(a0["ds"], 1)
                    dve.wait_ge(a0["nrm"], b + 1)
                    ch_b.link(v.tensor_scalar(nrm[:, :], nrm[:, :], 1e-12, None, ALU.max))
                    ch_b.link(v.reciprocal(rn[:, :, :].rearrange("p t h -> p (t h)"), nrm[:, :]))
                    need(dve, a0["v3"], 3 * b)
                    ch_b.step(v.tensor_tensor(kc[:, :, :, 1], es[par][:, :, NH:2 * NH], rn[:, :, NH:2 * NH], ALU.mult))
                    ch_b.step(v.tensor_copy(kc[:, :, :, 2], rn[:, :, NH:2 * NH]))
                if A:
                    rotate(0)
                if Bk:
                    dve.wait_ge(a0["e"], b + 1)
                    k = ch_b.step(v.tensor_tensor(kc[:, :, :, 0], es[par][:, :, 0:NH], rn[:, :, NH:2 * NH], ALU.mult))
                    ch_b.wait(k)
                    dve.sem_inc(a0["kc"], 1)
                if C:
                    masks(a0, c, 2, 2, 4)
                if A:
                    surprise(0)
                    normalize(a, 1)
                if Bk:
                    dve.wait_ge(a0["ge"], b + 1)
                    ch_b.link(v.tensor_scalar(ge[:, :, :], ge[:, :, :], 1.0, None, ALU.add))
                    ch_b.link(v.reciprocal(sg[:, :, :], ge[:, :, :]))
                    ch_b.link(v.tensor_tensor(be[:, :, :], sg[:, :, 0:NH], sg[:, :, NH:2 * NH], ALU.subtract))
                    ch_b.step(v.tensor_tensor(be[:, :, :], be[:, :, :], b3(it[:, :], [P, NT, NH], 2), ALU.mult))
                    dve.wait_ge(a0["EP"], b + 1)
                    v.tensor_copy(ep[:, :, :].rearrange("p t h -> p (t h)"), bank[7][0:P, 336:408]).then_inc(a0["ep"], 1)
                if C:
                    kw = weigh(ch_c, c, 2)
                if Bk:
                    masks(a0, b, 0, 0, 2)
                if C:
                    k = add_up(ch_c, c, 2, kw)
                    ch_c.wait(k)
                    ch_c.link(v.tensor_reduce(hm[:, :], o, AX, ALU.add))
                    ch_c.link(v.tensor_scalar(hm[:, :], hm[:, :], 1.0 / HD, None, ALU.mult))
                    v.tensor_tensor(o, o, b3(hm[:, :], [P, NT * NH, HD], 2), ALU.subtract).then_inc(a0["hc"], 1)
                if Bk:
                    dve.wait_ge(a0["ep"], b + 1)
                    itb = b3(it[:, :], [P, NT, NH], 2)
                    ch_b.link(v.tensor_scalar(al[:, :, :], ep[:, :, 0:NH], 1e-12, None, ALU.add))
                    ch_b.step(v.reciprocal(al[:, :, :], al[:, :, :]))
                    ch_b.link(v.tensor_tensor(ga[:, :, :], be[:, :, :], ep[:, :, NH:2 * NH], ALU.mult))
                    ch_b.step(v.tensor_tensor(al[:, :, :], al[:, :, :], sg[:, :, NH:2 * NH], ALU.mult))
                    ch_b.link(v.tensor_tensor(ga[:, :, :], ga[:, :, :], sg[:, :, NH:2 * NH], ALU.add))
                    ch_b.link(v.scalar_tensor_tensor(ga[:, :, :], ga[:, :, :], -1.0, itb, ALU.mult, ALU.mult))
                    for j, x in enumerate((al, be, ga)):
                        k = ch_b.step(v.tensor_tensor(cf[:, :, :, j], x[:, :, :], rn[:, :, 0:NH], ALU.mult))
                    ch_b.wait(k)
                if A:
                    rotate(1)
                if Bk:
                    masks(a0, b, 0, 2, 4)
                if A:
                    surprise(1)
                    normalize(a, 2)
                if C:
                    dve.wait_ge(a0["hsq"], c + 1)
                    v.tensor_reduce(hr[:, :], sqh[:, :, :].rearrange("p t (h d) -> p t h d", d=HD), AX, ALU.add).then_inc(a0["hvar"], 1)
                if Bk:
                    state(ch_b, b, 0)
                if C:
                    dve.wait_ge(a0["hsd"], c + 1)
                    ch_c.link(v.reciprocal(hr[:, :], hr[:, :]))
                    v.tensor_tensor(o, o, b3(hr[:, :], [P, NT * NH, HD], 2), ALU.mult).then_inc(a0["y"], 1)
                if Bk:
                    kw = weigh(ch_b, b, 0)
                    masks(a0, b, 1, 0, 2)
                    add_up(ch_b, b, 0, kw)
                if A:
                    rotate(2)
                if Bk:
                    masks(a0, b, 1, 2, 4)
                if C:
                    for j, (lo, n) in enumerate(PAIRS):
                        dve.wait_ge(a0["op"], 2 * c + j + 1)
                        v.tensor_tensor(tile_of(h, 3 * c + lo, n), tile_of(h, 3 * c + lo, n), bank[2 + j][0:P, 0:D * n],
                                        ALU.add).then_inc(a0["h"], 1)
                if A:
                    surprise(2)
                if Z:
                    normalize(Z[0], 0)
                if C:
                    tile_stats(ch_c, a0["h"], c)
                if Bk:
                    state(ch_b, b, 1)
            pipeline(dve, attn0, 2)
            dve.sem_inc(a0["var"], 1)

            dve.wait_ge(r["sd"], 1)
            link(v.reciprocal(rs0[:, :], rs0[:, :]))
            for n in range(TILES):
                v.tensor_scalar(xn_all[:, n, :], h[:, n * D:n * D + D], mv0[:, 2 * n:2 * n + 1], rs0[:, n:n + 1],
                                ALU.subtract, ALU.mult).then_inc(r["xn"], 1)
            dve.wait_ge(r["lg_ps"], 1)
            v.tensor_copy(lg[:, :, :].rearrange("p t e -> p (t e)"), bank[0][0:P, 0:TILES * NE]).then_inc(r["lg"], 1)
            te = [P, TILES, NE]
            dve.wait_ge(r["lg"], 1)
            link(v.tensor_reduce(red[:, :], lg[:, :, :], AX, ALU.max))
            v.tensor_tensor(lg[:, :, :], lg[:, :, :], b3(red[:, :], te, 2), ALU.subtract).then_inc(r["lg"], 1)
            dve.wait_ge(r["ready"], 1)
            link(v.tensor_reduce(red[:, :], lg[:, :, :], AX, ALU.add))
            link(v.reciprocal(red[:, :], red[:, :]))
            link(v.tensor_tensor(lg[:, :, :], lg[:, :, :], b3(red[:, :], te, 2), ALU.mult))
            ie = b3(iota[:, 0:NE], te, 1)
            for j in range(2):
                link(v.tensor_reduce(gate[j][:, :], lg[:, :, :], AX, ALU.max))
                link(v.tensor_tensor(cand[:, :, :], lg[:, :, :], b3(gate[j][:, :], te, 2), ALU.is_lt))
                link(v.scalar_tensor_tensor(cand[:, :, :], cand[:, :, :], float(NE), ie, ALU.mult, ALU.add))
                link(v.tensor_reduce(red[:, :], cand[:, :, :], AX, ALU.min))
                link(v.tensor_tensor(oh[j][:, :, :], ie, b3(red[:, :], te, 2), ALU.is_equal))
                if j == 0:
                    link(v.scalar_tensor_tensor(lg[:, :, :], oh[0][:, :, :], -2.0, lg[:, :, :], ALU.mult, ALU.add))
            v.tensor_tensor(both[:, :, :], oh[0][:, :, :], oh[1][:, :, :], ALU.add).then_inc(r["both"], 1)
            link(v.memset(onee[:, :], 1.0))
            dve.wait_ge(r["rank"], 1)
            em = "p (t e) -> p e t"
            link(v.tensor_copy(tot[:, :].rearrange("p (e t) -> p e t", t=TILES), bank[1][0:P, 0:TILES * NE].rearrange(em, e=NE)))
            link(v.tensor_tensor_scan(inc[:, :], reset[:, :], tot[:, :], 0.0, ALU.mult, ALU.add))
            inc3 = inc[:, :].rearrange("p (e t) -> p e t", t=TILES)
            c3 = cmp[:, 0:NE * MAXB].rearrange("p (e n) -> p e n", e=NE)
            link(v.tensor_tensor(c3, inc3[:, :, TILES - 1:TILES].to_broadcast([P, NE, MAXB]), b3(steps[:, :], [P, NE, MAXB], 1), ALU.is_gt))
            link(v.tensor_reduce(nblk[:, :], c3, AX, ALU.add))
            link(v.tensor_tensor_scan(bend[:, :], onee[:, :], nblk[:, :], 0.0, ALU.mult, ALU.add))
            link(v.tensor_tensor(basee[:, :], bend[:, :], nblk[:, :], ALU.subtract))
            link(v.tensor_scalar(basee[:, :], basee[:, :], float(BLK), None, ALU.mult))
            be3 = cmp[:, 0:NB * NE].rearrange("p (n e) -> p n e", e=NE)
            link(v.tensor_tensor(be3, b3(bend[:, :], [P, NB, NE], 1), b3(iota[:, 0:NB], [P, NB, NE], 2), ALU.is_le))
            link(v.tensor_reduce(eb[:, :], be3, AX, ALU.add))
            link(v.tensor_scalar(eb[:, :], eb[:, :], float(NE - 1), None, ALU.min))
            v.tensor_copy(eb_i[:, :], eb[:, :]).then_inc(r["exp"], 1)
            link(v.tensor_tensor(pos[:, :, :].rearrange("p t e -> p e t"), inc3, tot[:, :].rearrange("p (e t) -> p e t", t=TILES), ALU.subtract))
            link(v.tensor_tensor(pos[:, :, :], pos[:, :, :], bank[0][0:P, 0:TILES * NE].rearrange("p (t e) -> p t e", e=NE), ALU.add))
            link(v.tensor_tensor(pos[:, :, :], pos[:, :, :], b3(basee[:, :], te, 1), ALU.add))
            for j in range(2):
                link(v.tensor_tensor(cand[:, :, :], oh[j][:, :, :], pos[:, :, :], ALU.mult))
                link(v.tensor_reduce(slot[:, :, j], cand[:, :, :], AX, ALU.add))
            link(v.tensor_copy(slot_i[:, :], slot[:, :, :].rearrange("p t j -> p (t j)")))
            link(v.tensor_scalar(part_i[:, :], slot_i[:, :], 7, None, ALU.arith_shift_right))
            link(v.tensor_copy(s_blk[:, :], part_i[:, :]))
            link(v.scalar_tensor_tensor(s_row[:, :], s_blk[:, :], -float(BLK), slot[:, :, :].rearrange("p t j -> p (t j)"), ALU.mult, ALU.add))

            def ids(i, first):
                for s in range(4):
                    u = 4 * i + s
                    if not first:
                        dve.wait_ge(r["ids"], u - 3)
                    v.tensor_scalar(row_hot[s][:, :], iota[:, :], s_row[:, bass.ds(u, 1)], None, ALU.is_equal).then_inc(r["hot"], 1)
                    v.tensor_scalar(blk_hot[s][:, :], iota[:, 0:NB], s_blk[:, bass.ds(u, 1)], token[:, bass.ds(2 * i + s // 2, 1)],
                                    ALU.is_equal, ALU.mult).then_inc(r["hot"], 1)
            chain.loop(TILES * 2 // 4, ids)
            dve.wait_ge(r["ids"], 2 * TILES)
            v.memset(xgT[:, :, :], 1.0)
            v.tensor_copy(idx[:, :], bank[2][:, 0:NB]).then_inc(r["idx"], 1)
            dve.wait_ge(r["idx"], 1)

            def y_out(n, i, s):
                dve.wait_ge(m["y_ps"], n + 1)
                need(dve, m_out[s], 16 * i)
                v.tensor_tensor(yb[s][:, :], bank[7][:, 0:D], e_b2[s][:, :], ALU.add).then_inc(m["y"], 1)

            def blocks(i):
                for s in range(UNROLL):
                    n = UNROLL * i + s
                    dve.wait_ge(m["xgT_ps"], n + 1)
                    need(dve, m["hid"], 2 * n)
                    v.tensor_copy(xgT[0:KC, :, :].rearrange("p a t -> p (a t)"), bank[6][0:KC, 0:2 * BLK]).then_inc(m["xgT"], 1)
                    if not isinstance(n, int) or n >= 2:
                        y_out(n - 2, i if s == 2 else i - 1, (s + 1) % UNROLL)
            blocks(0)
            blocks(1)
            with dve.Fori(2, NB // UNROLL) as i:
                blocks(i)
            for n in (NB - 2, NB - 1):
                y_out(n, n // UNROLL, n % UNROLL)
            for s in range(UNROLL):
                dve.wait_ge(m_out[s], 16 * (NB // UNROLL))
            link(v.memset(v1[0][:, :, :, :], 1.0))
            link(v.memset(v1[1][:, :, :, :], 1.0))
            link(v.memset(y1T[:, :, :, :], 1.0))
            link(v.memset(xzT[:, :, :, :], 1.0))
            ch_a1, ch_z, ch_w = ch_a.next_phase(B, 6), ch_b.next_phase(B, 14), ch_c.next_phase(B, 2)
            hv = lambda ap: ap.rearrange("p (h d) -> p h d", d=HD)

            def attn1(Z, A, Bk, C):
                a, pa = A or (None, None)
                z, pz = Z or (None, None)
                tile = lambda n: tile_of(h, n)
                W = 4 * (HD + 1)

                def moments(src, sem_):
                    for t in range(NT):
                        k = ch_z.step(v.bn_stats(stats[:, t, :], src(t)))
                    ch_z.wait(k)
                    stand_alone(dve)
                    for t in range(NT):
                        k = ch_z.step(v.bn_aggr(mv[:, t, :], stats[:, t, :]))
                    ch_z.wait(k)
                    dve.sem_inc(sem_, 1)

                def normalize(src, i, sem_):
                    dve.wait_ge(a1["sd"], 2 * z + i + 1)
                    ch_z.link(v.reciprocal(rs[:, :], sd[:, :]))
                    for t in range(NT):
                        v.tensor_scalar(xz[pz][:, t, i, :], src(t), mv[:, t, 0:1], rs[:, t:t + 1],
                                        ALU.subtract, ALU.mult).then_inc(sem_, 1)

                if A:
                    ch_a1.turn(a)
                if Z:
                    ch_z.turn(z)
                for j in range(NT):
                    n, par, t, out_tile, done = slot_tiles(j, Bk, C)
                    if done is not None:
                        if out_tile < 2:
                            dve.wait_ge(a1["O"], done + 1)
                            dve.wait_ge(a1["st"], 2 * before_batch(j, Bk, C) + out_tile + 1)
                            v.tensor_tensor(st1[:, :, :], bank[3][:, 0:3 * W].rearrange("p (g n) -> p g n", g=3),
                                            b3(head_mask1[:, :], [128, 3, W], 1), ALU.mult).then_inc(a1["stb"], 1)
                        ch_w.turn(done)
                        dve.wait_ge(a1["O"], done + 1)
                        need(dve, a1["yT_ps"], done - 2)
                        oo = bank[2][0:P, 0:3 * W].rearrange("p (h d) -> p h d", d=HD + 1)
                        ch_w.link(v.tensor_scalar(den[:, :], oo[:, :, HD], 1e-6, None, ALU.add))
                        ch_w.link(v.reciprocal(den[:, :], den[:, :]))
                        v.tensor_tensor(hv(o3[:, out_tile]), oo[:, :, 0:HD], b3(den[:, :], [P, NH, HD], 2), ALU.mult).then_inc(a1["w"], 1)
                    if n is not None:
                        masks(a1, n, t, 0, 2)
                    if A:
                        dve.wait_ge(a1["eq"], 6 * a + 2 * j + 2)
                        need(dve, a1["st"], 2 * a - 2)
                        need(dve, a1["qkT_ps"], 6 * a - 6)
                        v.scalar_tensor_tensor(qk[pa][:, j, 0:NH, 0:HD], hv(rot1[:, j, 0:D]), 1.0, hv(relu[:, j, 0:D]),
                                               ALU.min, ALU.add).then_inc(a1["q_ft"], 1)
                        dve.wait_ge(a1["ge"], 3 * a + j + 1)
                        ch_a1.link(v.tensor_scalar(ge1[:, j], ge1[:, j], 1.0, None, ALU.add))
                        ch_a1.link(v.reciprocal(ge1[:, j], ge1[:, j]))
                        need(dve, a1["ek"], 6 * a + 2 * j - 4)
                        v.tensor_tensor(kg[:, j], bank[4][0:P, D:2 * D], ge1[:, j], ALU.mult).then_inc(a1["kg"], 1)
                    if n is not None:
                        masks(a1, n, t, 2, 4)
                    if A:
                        dve.wait_ge(a1["ek"], 6 * a + 2 * j + 2)
                        v.scalar_tensor_tensor(qk[pa][:, j, NH:2 * NH, 0:HD], hv(rot1[:, j, D:2 * D]), 1.0, hv(relu[:, j, D:2 * D]),
                                               ALU.min, ALU.add).then_inc(a1["k_ft"], 1)
                    if done is not None:
                        dve.wait_ge(a1["op"], done + 1)
                        v.tensor_tensor(tile(done), tile(done), bank[6][0:P, 2 * P:2 * P + D], ALU.add).then_inc(a1["h"], 1)
                    if Z and j == 0:
                        dve.wait_ge(a1["cmb"], z + 1)
                        stand_alone(dve)
                        moments(lambda t2: tile(3 * z + t2), a1["var"])
                    if Z and j == 1:
                        need(dve, a1["xzT_ps"], 3 * z - 3)
                        normalize(lambda t2: tile(3 * z + t2), 0, a1["xn"])
                        dve.wait_ge(a1["xn"], 3 * z + 3)
                        stand_alone(dve)
                        moments(lambda t2: xz[pz][:, t2, 0, :], a1["var"])
                    if Z and j == 2:
                        normalize(lambda t2: xz[pz][:, t2, 0, :], 1, a1["zn"])
            pipeline(dve, attn1, 2)
            dve.wait_ge(a1["h"], 3 * B)
            ch_z, ch_s = ch_z.next_phase(B, 6), ch_a1.next_phase(B, 6)

            def ffn(Z, A, Bk, C):
                z, _ = Z or (None, None)
                a, pa = A or (None, None)
                b, par = Bk or (None, None)
                c, _ = C or (None, None)
                now = b if Bk else c + 1 if C else None
                tile = lambda n: tile_of(h, n)
                if A:
                    dve.wait_ge(f["sd"], a + 1)
                    v.reciprocal(rs[:, :], sd[:, :]).then_inc(f["rs"], 1)
                if now is not None:
                    if Bk:
                        dve.wait_ge(f["rms"], b + 1)
                        need(dve, f["xs"], 3 * b)
                        need(dve, f["sil"], 3 * b)
                    if C:
                        dve.wait_ge(f["rms2"], c + 1)
                        need(dve, f["ys"], 3 * c)
                    ch_s.turn(now)
                    ch_s.link(v.reciprocal(rms[:, :, :], rms[:, :, :]))
                    ch_s.link(v.tensor_tensor(top[:, :, :], amax[:, :, :], rms[:, :, :], ALU.mult))
                    ch_s.link(v.tensor_scalar(top[:, :, :], top[:, :, :], 1e-5, None, ALU.max))
                    ch_s.link(v.reciprocal(qs[:, :, :], top[:, :, :]))
                    ch_s.step(v.scalar_tensor_tensor(qs[:, :, :], qs[:, :, :], 127.0, rms[:, :, :], ALU.mult, ALU.mult))
                    k = ch_s.step(v.scalar_tensor_tensor(back[:, :, :], top[:, :, :], 1.0 / 127.0,
                                                         b3(wback[0:P, :], [P, 2, NT], 2), ALU.mult, ALU.mult))
                    ch_s.wait(k)
                    dve.sem_inc(f["sc"], 1)
                for t in range(NT):
                    for on, batch, src, dst, ready, half, sem_ in ((Bk, b, xs, xq, "xs", "x1", "xq_"), (C, c, ys, yq, "ys", "y1", "yq")):
                        if on:
                            dve.wait_ge(f[ready], 3 * batch + t + 1)
                            v.tensor_scalar(src[:, t], src[:, t], MAGIC, MAGIC - 128.0, ALU.add, ALU.max).then_inc(f[half], 1)
                            dve.wait_ge(f[half], 3 * batch + t + 1)
                            used = "xqT_ps" if on is Bk else "yqT_ps"
                            need(dve, f[used], 3 * batch + t - 2)
                            v.tensor_scalar(dst[:, t], src[:, t], MAGIC + 127.0, MAGIC, ALU.min, ALU.subtract).then_inc(f[sem_], 1)
                if A:
                    dve.wait_ge(f["rs"], a + 1)
                    need(dve, f["sq"], 3 * a)
                    need(dve, f["xg"], 3 * a)
                    for t in range(NT):
                        v.tensor_scalar(xn[:, t, :], tile(3 * a + t), mv[:, t, 0:1], rs[:, t:t + 1],
                                        ALU.subtract, ALU.mult).then_inc(f["xn"], 1)
                if Z:
                    ch_z.turn(z)
                    stand_alone(dve)
                    for t in range(NT):
                        k = ch_z.step(v.bn_stats(stats[:, t, :], tile(3 * z + t)))
                    ch_z.wait(k)
                    stand_alone(dve)
                    if A:
                        dve.wait_ge(f["xn"], 3 * a + 3)
                        stand_alone(dve)
                    for t in range(NT):
                        k = ch_z.step(v.bn_aggr(mv[:, t, :], stats[:, t, :]))
                    ch_z.wait(k)
                    dve.sem_inc(f["var"], 1)
                if C:
                    need(dve, f["out"], 16 * c)
                for t in range(NT):
                    if A:
                        dve.wait_ge(f["xg"], 3 * a + t + 1)
                        v.tensor_reduce(amax[:, 0, t:t + 1], xg[pa][:, t], AX, ALU.max, apply_absolute_value=True).then_inc(f["ax"], 1)
                    if Bk:
                        dve.wait_ge(f["sil"], 3 * b + t + 1)
                        need(dve, f["z"], 3 * b + t - 2)
                        need(dve, f["sq2"], 3 * b + t - 2)
                        v.scalar_tensor_tensor(yf[:, t], bank[2 * (t % 2)][0:P, :], back[:, 0, t:t + 1], sil[:, t], ALU.mult, ALU.mult).then_inc(f["y"], 1)
                    if C:
                        dve.wait_ge(f["st"], 3 * c + t + 1)
                        v.scalar_tensor_tensor(fo[:, t], bank[4][0:P, 0:D], back[:, 1, t:t + 1], tile(3 * c + t), ALU.mult, ALU.add).then_inc(f["o"], 1)
                if Bk:
                    for t in range(NT):
                        dve.wait_ge(f["z"], 3 * b + t + 1)
                        v.tensor_reduce(amax[:, 1, t:t + 1], yg2[par][:, t], AX, ALU.max, apply_absolute_value=True).then_inc(f["ax"], 1)
                    dve.wait_ge(f["ax"], 3 * b + 3)
            pipeline(dve, ffn, 2)


def kernel(**inputs):
    import numpy as _np
    import concourse.bacc as _bacc
    from concourse import mybir as _mybir
    from concourse.bass_utils import run_bass_kernel_spmd as _run

    given = {k: _np.asarray(v) for k, v in inputs.items()}
    arrays = {f"c_{k}": v for k, v in shape_constants().items()}
    arrays.update(laid_out(given["x"], given["txt"], given))
    nc = _bacc.Bacc("TRN2", target_bir_lowering=False, num_devices=1)
    dram = {k: nc.dram_tensor(k, v.shape, _mybir.dt.from_np(v.dtype), kind="ExternalInput").ap()
            for k, v in arrays.items()}
    out = nc.dram_tensor("out", (B, L, D), F32, kind="ExternalOutput").ap()
    early_fusion(nc, dram, out)
    return _run(nc, [arrays], core_ids=[0]).results[0]["out"]
```
